# Optimizing a Trainium2 kernel written in Bass

```python
import numpy as np
import jax
import jax.numpy as jnp

def _softmax(x, axis=-1):
    return jax.nn.softmax(x, axis=axis)

def _gelu(x):
    return jax.nn.gelu(x, approximate=True)

def _silu(x):
    return jax.nn.silu(x)

def _sigmoid(x):
    return jax.nn.sigmoid(x)

def _layernorm(x, axis=-1, eps=1e-05):
    m = jnp.mean(x, axis=axis, keepdims=True)
    v = jnp.var(x, axis=axis, keepdims=True)
    return (x - m) / jnp.sqrt(v + eps)

def _scatter_add(tgt, idx, src, axis=0):
    return tgt.at[idx].add(src)

def _segment_sum(src, seg, n):
    return jax.ops.segment_sum(src, seg, n)
kernel_name = 'mk_gnn_preln_d4_gnn_r16_1c64a7'

def setup_inputs(seed: int=0):
    np.random.seed(seed)
    _w = jnp.asarray

    def _rec_inputs():
        import jax
        import jax.numpy as jnp
        _gk = jax.random.key(seed)
        x = -0.0009044 + 1 * jax.random.normal(jax.random.fold_in(_gk, 1), (6250, 160), jnp.float32)
        src = jax.random.randint(jax.random.fold_in(_gk, 2), (100000,), 0, 6250, jnp.int32)
        dst = jax.random.randint(jax.random.fold_in(_gk, 3), (100000,), 0, 6250, jnp.int32)
        _o = jnp.argsort(dst, stable=True)
        src = src[_o]
        dst = dst[_o]
        edge_attr_10 = jax.random.uniform(jax.random.fold_in(_gk, 12), (100000, 10), jnp.float32, 0.0, 1)
        edge_attr_16 = jax.random.uniform(jax.random.fold_in(_gk, 13), (100000, 16), jnp.float32, 0.0, 1)
        edge_attr_4 = -0.000149047 + 1.00006 * jax.random.normal(jax.random.fold_in(_gk, 14), (100000, 4), jnp.float32)
        edge_attr_8 = 0.000735704 + 1.0001 * jax.random.normal(jax.random.fold_in(_gk, 15), (100000, 8), jnp.float32)
        node_vec1 = jax.random.uniform(jax.random.fold_in(_gk, 17), (6250, 1), jnp.float32, 0.0, 1)
        node_vec1_n2 = jax.random.uniform(jax.random.fold_in(_gk, 18), (6250, 1), jnp.float32, 0.0, 1)
        node_vec1_n3 = jax.random.uniform(jax.random.fold_in(_gk, 19), (6250, 1), jnp.float32, 0.0, 1)
        return (x, src, dst, edge_attr_10, edge_attr_16, edge_attr_4, edge_attr_8, node_vec1, node_vec1_n2, node_vec1_n3)
    x, src, dst, edge_attr_10, edge_attr_16, edge_attr_4, edge_attr_8, node_vec1, node_vec1_n2, node_vec1_n3 = _rec_inputs()

    def _L0_gnn_setup():
        import jax, jax.numpy as jnp
        import numpy as np
        N_NODES = 625
        N_EDGES = 20000
        NUM_NEIGHBORS = 32.0
        INV_SQRT3 = 1.0 / np.sqrt(3.0)

        def _fctp_scalar_attr(xs, xv, Ws, Wv, a):
            out_s = xs @ Ws * (a / np.sqrt(xs.shape[1]))[:, None]
            out_v = jnp.einsum('nuc,uw->nwc', xv, Wv) * (a / np.sqrt(xv.shape[1]))[:, None, None]
            return (out_s, out_v)
        key = jax.random.key(seed)
        ks = jax.random.split(key, 16)
        f32 = jnp.float32
        return {'node_input': jax.random.normal(ks[0], (N_NODES, 160), f32), 'node_attr': jnp.ones((N_NODES, 1), f32), 'edge_attr': jax.random.normal(ks[1], (N_EDGES, 4), f32), 'edge_scalar_attr': jax.random.normal(ks[2], (N_EDGES, 8), f32), 'Wsc0': jax.random.normal(ks[3], (64, 64), f32), 'Wsc1': jax.random.normal(ks[4], (32, 32), f32), 'Wl1_0': jax.random.normal(ks[5], (64, 64), f32), 'Wl1_1': jax.random.normal(ks[6], (32, 32), f32), 'Wfc1': jax.random.normal(ks[7], (8, 64), f32), 'Wfc2': jax.random.normal(ks[8], (64, 64), f32), 'Wfc3': jax.random.normal(ks[9], (64, 192), f32), 'Wl2_s': jax.random.normal(ks[10], (96, 64), f32), 'Wl2_v': jax.random.normal(ks[11], (96, 32), f32), 'Wa': jax.random.normal(ks[12], (96, 1), f32), 'edge_src': jax.random.randint(ks[13], (N_EDGES,), 0, N_NODES), 'edge_dst': jax.random.randint(ks[14], (N_EDGES,), 0, N_NODES)}
    _L0_gnn_all = _L0_gnn_setup()
    _L0_gnn_in = {k: v for k, v in _L0_gnn_all.items() if k in ('Wsc0', 'Wsc1', 'Wl1_0', 'Wl1_1', 'Wfc1', 'Wfc2', 'Wfc3', 'Wl2_s', 'Wl2_v', 'Wa')}
    del _L0_gnn_all

    def _L1_gnn_setup():
        import jax, jax.numpy as jnp
        import numpy as np
        N = 2500
        E = 25000
        MUL0, MUL1 = (64, 32)
        RAD, HID = (8, 64)
        WNUM = 192
        NUM_NEIGHBORS = 10.0
        INV3 = 1.0 / np.sqrt(3.0)

        def _lin(s, v, Ws, Wv, attr):
            out_s = s @ Ws * attr * (1.0 / np.sqrt(Ws.shape[0]))
            out_v = jnp.einsum('nud,uv->nvd', v, Wv) * attr[..., None] * (1.0 / np.sqrt(Wv.shape[0]))
            return (out_s, out_v)
        key = jax.random.key(seed)
        ks = jax.random.split(key, 16)
        return {'node_input': jax.random.normal(ks[0], (N, MUL0 + 3 * MUL1), jnp.float32), 'node_attr': jnp.ones((N, 1), jnp.float32), 'edge_attr': jax.random.normal(ks[1], (E, 4), jnp.float32), 'edge_scalars': jax.random.uniform(ks[2], (E, RAD), jnp.float32), 'W_sc_s': jax.random.normal(ks[3], (MUL0, MUL0), jnp.float32), 'W_sc_v': jax.random.normal(ks[4], (MUL1, MUL1), jnp.float32), 'W1_s': jax.random.normal(ks[5], (MUL0, MUL0), jnp.float32), 'W1_v': jax.random.normal(ks[6], (MUL1, MUL1), jnp.float32), 'W2_s': jax.random.normal(ks[7], (MUL0 + MUL1, MUL0), jnp.float32), 'W2_v': jax.random.normal(ks[8], (MUL0 + MUL1, MUL1), jnp.float32), 'W3': jax.random.normal(ks[9], (MUL0 + MUL1, 1), jnp.float32), 'fcW1': jax.random.normal(ks[10], (RAD, HID), jnp.float32), 'fcW2': jax.random.normal(ks[11], (HID, WNUM), jnp.float32), 'edge_src': jax.random.randint(ks[12], (E,), 0, N, jnp.int32), 'edge_dst': jax.random.randint(ks[13], (E,), 0, N, jnp.int32)}
    _L1_gnn_all = _L1_gnn_setup()
    _L1_gnn_in = {k: v for k, v in _L1_gnn_all.items() if k in ('W_sc_s', 'W_sc_v', 'W1_s', 'W1_v', 'W2_s', 'W2_v', 'W3', 'fcW1', 'fcW2')}
    del _L1_gnn_all

    def _L2_gnn_setup():
        import jax, jax.numpy as jnp
        import numpy as np
        N, E = (1250, 20000)
        CS, CV = (64, 32)
        AS_, AV, H = (16, 8, 4)
        NB = 16
        SQRT3 = 1.7320508075688772
        SQRT2 = 1.4142135623730951
        EPS = 1e-05

        def _cg_tp(s, v, y0, y1, w_ss, w_sv, w_vs, w_vv0, w_vv1):
            out_s = jnp.concatenate([w_ss * s * y0[:, None], w_vv0 * (jnp.einsum('eci,ei->ec', v, y1) / SQRT3)], axis=-1)
            out_v = jnp.concatenate([(w_sv * s)[:, :, None] * y1[:, None, :], (w_vs * jnp.ones_like(v[..., 0]))[..., None] * v * y0[:, None, None], (w_vv1 * jnp.ones_like(v[..., 0]))[..., None] * (jnp.cross(v, y1[:, None, :]) / SQRT2)], axis=1)
            return (out_s, out_v)

        def _equiv_layernorm(s, v, gamma_s, beta_s, gamma_v):
            mu = jnp.mean(s, axis=-1, keepdims=True)
            var = jnp.var(s, axis=-1, keepdims=True)
            s_n = (s - mu) * jax.lax.rsqrt(var + EPS) * gamma_s + beta_s
            rms = jnp.sqrt(jnp.mean(jnp.sum(v * v, axis=-1), axis=-1, keepdims=True) + EPS)
            v_n = v / rms[..., None] * gamma_v[None, :, None]
            return (s_n, v_n)
        key = jax.random.key(seed)
        ks = jax.random.split(key, 26)

        def rn(k, shape, fan):
            return jax.random.normal(k, shape, jnp.float32) / np.sqrt(fan)
        D1S, D1V = (CS + CV, CS + 2 * CV)
        WN = 2 * CS + 3 * CV
        inp = {'node': jax.random.normal(ks[0], (N, CS + 3 * CV), jnp.float32), 'edge_index': jax.random.randint(ks[1], (2, E), 0, N, jnp.int64 if jax.config.jax_enable_x64 else jnp.int32), 'rbf': jax.random.uniform(ks[2], (E, NB), jnp.float32), 'rsh': jax.random.normal(ks[3], (E, 4), jnp.float32), 'gamma_s': jnp.ones((CS,), jnp.float32), 'beta_s': jnp.zeros((CS,), jnp.float32), 'gamma_v': jnp.ones((CV,), jnp.float32), 'Ws_src': rn(ks[4], (CS, CS), CS), 'Wv_src': rn(ks[5], (CV, CV), CV), 'Ws_dst': rn(ks[6], (CS, CS), CS), 'Wv_dst': rn(ks[7], (CV, CV), CV), 'W_rbf': rn(ks[8], (NB, WN), NB), 'W_alpha': rn(ks[9], (D1S, H * AS_), D1S), 'alpha_dot': rn(ks[10], (1, H, AS_), AS_), 'Ws_val': rn(ks[11], (D1S, CS), D1S), 'Wv_val': rn(ks[12], (D1V, CV), D1V), 'Wg': rn(ks[13], (CS, CV), CS), 'w2_ss': rn(ks[14], (CS,), 1), 'w2_sv': rn(ks[15], (CS,), 1), 'w2_vs': rn(ks[16], (CV,), 1), 'w2_vv0': rn(ks[17], (CV,), 1), 'w2_vv1': rn(ks[18], (CV,), 1), 'Ws_vlin': rn(ks[19], (D1S, H * AS_), D1S), 'Wv_vlin': rn(ks[20], (D1V, H * AV), D1V), 'Wps': rn(ks[21], (H * AS_, CS), H * AS_), 'Wpv': rn(ks[22], (H * AV, CV), H * AV)}
        return inp
    _L2_gnn_all = _L2_gnn_setup()
    _L2_gnn_in = {k: v for k, v in _L2_gnn_all.items() if k in ('gamma_s', 'beta_s', 'gamma_v', 'Ws_src', 'Wv_src', 'Ws_dst', 'Wv_dst', 'W_rbf', 'W_alpha', 'alpha_dot', 'Ws_val', 'Wv_val', 'Wg', 'w2_ss', 'w2_sv', 'w2_vs', 'w2_vv0', 'w2_vv1', 'Ws_vlin', 'Wv_vlin', 'Wps', 'Wpv')}
    del _L2_gnn_all

    def _L3_gnn_setup():
        import jax, jax.numpy as jnp
        import numpy as np
        N = 25000
        E = 25000
        S = 64
        V = 32
        NB = 10
        H = 100
        WN = 192
        MID = 96
        NUM_NEIGHBORS = 16.0
        C_S = float(np.sin(np.pi / 8.0))
        C_X = float(np.cos(np.pi / 8.0))
        SQRT3 = float(np.sqrt(3.0))

        def fctp_scalar_attr(xs, xv, attr, Ws, Wv):
            s = xs * attr @ Ws
            v = jnp.einsum('nuc,uo->noc', xv * attr[:, :, None], Wv)
            return (s, v)
        key = jax.random.key(seed)
        k = jax.random.split(key, 24)

        def w(i, shape):
            return jax.random.normal(k[i], shape, jnp.float32) / np.sqrt(float(shape[0]))
        return {'node_input': jax.random.normal(k[0], (N, S + 3 * V), jnp.float32), 'node_attr': jax.random.normal(k[1], (N, 1), jnp.float32), 'node_crystal_attr': jax.random.normal(k[2], (N, 1), jnp.float32), 'sym_mask': jax.random.normal(k[3], (N, 1), jnp.float32), 'edge_attr': jax.random.normal(k[4], (E, 4), jnp.float32), 'edge_length_embedded': jax.random.uniform(k[5], (E, NB), dtype=jnp.float32), 'edge_src': jax.random.randint(k[6], (E,), 0, N), 'edge_dst': jax.random.randint(k[7], (E,), 0, N), 'Ws_sc_a': w(8, (S, S)), 'Wv_sc_a': w(9, (V, V)), 'Ws_sc_c': w(10, (S, S)), 'Wv_sc_c': w(11, (V, V)), 'Ws_l1_a': w(12, (S, S)), 'Wv_l1_a': w(13, (V, V)), 'Ws_l1_c': w(14, (S, S)), 'Wv_l1_c': w(15, (V, V)), 'W_fc1': w(16, (NB, H)), 'W_fc2': w(17, (H, WN)), 'Ws_l2_a': w(18, (MID, MID)), 'Wv_l2_a': w(19, (MID, MID)), 'Ws_l2_c': w(20, (MID, MID)), 'Wv_l2_c': w(21, (MID, MID)), 'Ws_l3': w(22, (MID, S)), 'Wv_l3': w(23, (MID, V))}
    _L3_gnn_all = _L3_gnn_setup()
    _L3_gnn_in = {k: v for k, v in _L3_gnn_all.items() if k in ('Ws_sc_a', 'Wv_sc_a', 'Ws_sc_c', 'Wv_sc_c', 'Ws_l1_a', 'Wv_l1_a', 'Ws_l1_c', 'Wv_l1_c', 'W_fc1', 'W_fc2', 'Ws_l2_a', 'Wv_l2_a', 'Ws_l2_c', 'Wv_l2_c', 'Ws_l3', 'Wv_l3')}
    del _L3_gnn_all
    return {'x': x, 'src': src, 'dst': dst, 'edge_attr_10': edge_attr_10, 'edge_attr_16': edge_attr_16, 'edge_attr_4': edge_attr_4, 'edge_attr_8': edge_attr_8, 'node_vec1': node_vec1, 'node_vec1_n2': node_vec1_n2, 'node_vec1_n3': node_vec1_n3, 'L0_gnn_Wsc0': _L0_gnn_in['Wsc0'], 'L0_gnn_Wsc1': _L0_gnn_in['Wsc1'], 'L0_gnn_Wl1_0': _L0_gnn_in['Wl1_0'], 'L0_gnn_Wl1_1': _L0_gnn_in['Wl1_1'], 'L0_gnn_Wfc1': _L0_gnn_in['Wfc1'], 'L0_gnn_Wfc2': _L0_gnn_in['Wfc2'], 'L0_gnn_Wfc3': _L0_gnn_in['Wfc3'], 'L0_gnn_Wl2_s': _L0_gnn_in['Wl2_s'], 'L0_gnn_Wl2_v': _L0_gnn_in['Wl2_v'], 'L0_gnn_Wa': _L0_gnn_in['Wa'], 'L1_gnn_W_sc_s': _L1_gnn_in['W_sc_s'], 'L1_gnn_W_sc_v': _L1_gnn_in['W_sc_v'], 'L1_gnn_W1_s': _L1_gnn_in['W1_s'], 'L1_gnn_W1_v': _L1_gnn_in['W1_v'], 'L1_gnn_W2_s': _L1_gnn_in['W2_s'], 'L1_gnn_W2_v': _L1_gnn_in['W2_v'], 'L1_gnn_W3': _L1_gnn_in['W3'], 'L1_gnn_fcW1': _L1_gnn_in['fcW1'], 'L1_gnn_fcW2': _L1_gnn_in['fcW2'], 'L2_gnn_gamma_s': _L2_gnn_in['gamma_s'], 'L2_gnn_beta_s': _L2_gnn_in['beta_s'], 'L2_gnn_gamma_v': _L2_gnn_in['gamma_v'], 'L2_gnn_Ws_src': _L2_gnn_in['Ws_src'], 'L2_gnn_Wv_src': _L2_gnn_in['Wv_src'], 'L2_gnn_Ws_dst': _L2_gnn_in['Ws_dst'], 'L2_gnn_Wv_dst': _L2_gnn_in['Wv_dst'], 'L2_gnn_W_rbf': _L2_gnn_in['W_rbf'], 'L2_gnn_W_alpha': _L2_gnn_in['W_alpha'], 'L2_gnn_alpha_dot': _L2_gnn_in['alpha_dot'], 'L2_gnn_Ws_val': _L2_gnn_in['Ws_val'], 'L2_gnn_Wv_val': _L2_gnn_in['Wv_val'], 'L2_gnn_Wg': _L2_gnn_in['Wg'], 'L2_gnn_w2_ss': _L2_gnn_in['w2_ss'], 'L2_gnn_w2_sv': _L2_gnn_in['w2_sv'], 'L2_gnn_w2_vs': _L2_gnn_in['w2_vs'], 'L2_gnn_w2_vv0': _L2_gnn_in['w2_vv0'], 'L2_gnn_w2_vv1': _L2_gnn_in['w2_vv1'], 'L2_gnn_Ws_vlin': _L2_gnn_in['Ws_vlin'], 'L2_gnn_Wv_vlin': _L2_gnn_in['Wv_vlin'], 'L2_gnn_Wps': _L2_gnn_in['Wps'], 'L2_gnn_Wpv': _L2_gnn_in['Wpv'], 'L3_gnn_Ws_sc_a': _L3_gnn_in['Ws_sc_a'], 'L3_gnn_Wv_sc_a': _L3_gnn_in['Wv_sc_a'], 'L3_gnn_Ws_sc_c': _L3_gnn_in['Ws_sc_c'], 'L3_gnn_Wv_sc_c': _L3_gnn_in['Wv_sc_c'], 'L3_gnn_Ws_l1_a': _L3_gnn_in['Ws_l1_a'], 'L3_gnn_Wv_l1_a': _L3_gnn_in['Wv_l1_a'], 'L3_gnn_Ws_l1_c': _L3_gnn_in['Ws_l1_c'], 'L3_gnn_Wv_l1_c': _L3_gnn_in['Wv_l1_c'], 'L3_gnn_W_fc1': _L3_gnn_in['W_fc1'], 'L3_gnn_W_fc2': _L3_gnn_in['W_fc2'], 'L3_gnn_Ws_l2_a': _L3_gnn_in['Ws_l2_a'], 'L3_gnn_Wv_l2_a': _L3_gnn_in['Wv_l2_a'], 'L3_gnn_Ws_l2_c': _L3_gnn_in['Ws_l2_c'], 'L3_gnn_Wv_l2_c': _L3_gnn_in['Wv_l2_c'], 'L3_gnn_Ws_l3': _L3_gnn_in['Ws_l3'], 'L3_gnn_Wv_l3': _L3_gnn_in['Wv_l3']}

def reference(x, src, dst, edge_attr_10, edge_attr_16, edge_attr_4, edge_attr_8, node_vec1, node_vec1_n2, node_vec1_n3, L0_gnn_Wsc0, L0_gnn_Wsc1, L0_gnn_Wl1_0, L0_gnn_Wl1_1, L0_gnn_Wfc1, L0_gnn_Wfc2, L0_gnn_Wfc3, L0_gnn_Wl2_s, L0_gnn_Wl2_v, L0_gnn_Wa, L1_gnn_W_sc_s, L1_gnn_W_sc_v, L1_gnn_W1_s, L1_gnn_W1_v, L1_gnn_W2_s, L1_gnn_W2_v, L1_gnn_W3, L1_gnn_fcW1, L1_gnn_fcW2, L2_gnn_gamma_s, L2_gnn_beta_s, L2_gnn_gamma_v, L2_gnn_Ws_src, L2_gnn_Wv_src, L2_gnn_Ws_dst, L2_gnn_Wv_dst, L2_gnn_W_rbf, L2_gnn_W_alpha, L2_gnn_alpha_dot, L2_gnn_Ws_val, L2_gnn_Wv_val, L2_gnn_Wg, L2_gnn_w2_ss, L2_gnn_w2_sv, L2_gnn_w2_vs, L2_gnn_w2_vv0, L2_gnn_w2_vv1, L2_gnn_Ws_vlin, L2_gnn_Wv_vlin, L2_gnn_Wps, L2_gnn_Wpv, L3_gnn_Ws_sc_a, L3_gnn_Wv_sc_a, L3_gnn_Ws_sc_c, L3_gnn_Wv_sc_c, L3_gnn_Ws_l1_a, L3_gnn_Wv_l1_a, L3_gnn_Ws_l1_c, L3_gnn_Wv_l1_c, L3_gnn_W_fc1, L3_gnn_W_fc2, L3_gnn_Ws_l2_a, L3_gnn_Wv_l2_a, L3_gnn_Ws_l2_c, L3_gnn_Wv_l2_c, L3_gnn_Ws_l3, L3_gnn_Wv_l3):
    import jax
    import jax.numpy as jnp

    def _L0_gnn_ref(node_input, node_attr, edge_attr, edge_scalar_attr, Wsc0, Wsc1, Wl1_0, Wl1_1, Wfc1, Wfc2, Wfc3, Wl2_s, Wl2_v, Wa, edge_src, edge_dst):
        import jax, jax.numpy as jnp
        import numpy as np
        N_NODES = 625
        N_EDGES = 20000
        NUM_NEIGHBORS = 32.0
        INV_SQRT3 = 1.0 / np.sqrt(3.0)

        def _fctp_scalar_attr(xs, xv, Ws, Wv, a):
            out_s = xs @ Ws * (a / np.sqrt(xs.shape[1]))[:, None]
            out_v = jnp.einsum('nuc,uw->nwc', xv, Wv) * (a / np.sqrt(xv.shape[1]))[:, None, None]
            return (out_s, out_v)
        N = node_input.shape[0]
        a = node_attr[:, 0]
        xs = node_input[:, :64]
        xv = node_input[:, 64:].reshape(N, 32, 3)
        sc_s, sc_v = _fctp_scalar_attr(xs, xv, Wsc0, Wsc1, a)
        f_s, f_v = _fctp_scalar_attr(xs, xv, Wl1_0, Wl1_1, a)
        h = jax.nn.gelu(edge_scalar_attr @ Wfc1 / np.sqrt(8.0))
        h = jax.nn.gelu(h @ Wfc2 / np.sqrt(64.0))
        w = h @ Wfc3 / np.sqrt(64.0)
        w0, w1, w2, w3 = (w[:, :64], w[:, 64:128], w[:, 128:160], w[:, 160:192])
        gs = f_s[edge_src]
        gv = f_v[edge_src]
        y0 = edge_attr[:, 0]
        y1 = edge_attr[:, 1:4]
        mid0 = w0 * gs * y0[:, None]
        mid1 = w3 * jnp.einsum('euc,ec->eu', gv, y1) * INV_SQRT3
        mid2 = (w1 * gs)[:, :, None] * y1[:, None, :]
        mid3 = w2[:, :, None] * gv * y0[:, None, None]
        inv = 1.0 / np.sqrt(NUM_NEIGHBORS)
        seg = lambda x: jax.ops.segment_sum(x, edge_dst, num_segments=N) * inv
        ns0, ns1, nv2, nv3 = (seg(mid0), seg(mid1), seg(mid2), seg(mid3))
        mid_s = jnp.concatenate([ns0, ns1], axis=1)
        mid_v = jnp.concatenate([nv2, nv3], axis=1)
        out_s = mid_s @ Wl2_s * (a / np.sqrt(96.0))[:, None]
        out_v = jnp.einsum('nuc,uw->nwc', mid_v, Wl2_v) * (a / np.sqrt(96.0))[:, None, None]
        alpha = mid_s @ Wa * (a / np.sqrt(96.0))[:, None]
        res_s = sc_s + alpha * out_s
        res_v = sc_v + alpha[:, :, None] * out_v
        return jnp.concatenate([res_s, res_v.reshape(N, 96)], axis=1)

    def _L1_gnn_ref(node_input, node_attr, edge_attr, edge_scalars, W_sc_s, W_sc_v, W1_s, W1_v, W2_s, W2_v, W3, fcW1, fcW2, edge_src, edge_dst):
        import jax, jax.numpy as jnp
        import numpy as np
        N = 2500
        E = 25000
        MUL0, MUL1 = (64, 32)
        RAD, HID = (8, 64)
        WNUM = 192
        NUM_NEIGHBORS = 10.0
        INV3 = 1.0 / np.sqrt(3.0)

        def _lin(s, v, Ws, Wv, attr):
            out_s = s @ Ws * attr * (1.0 / np.sqrt(Ws.shape[0]))
            out_v = jnp.einsum('nud,uv->nvd', v, Wv) * attr[..., None] * (1.0 / np.sqrt(Wv.shape[0]))
            return (out_s, out_v)
        n = node_input.shape[0]
        s_in = node_input[:, :MUL0]
        v_in = node_input[:, MUL0:].reshape(n, MUL1, 3)
        sc_s, sc_v = _lin(s_in, v_in, W_sc_s, W_sc_v, node_attr)
        f_s, f_v = _lin(s_in, v_in, W1_s, W1_v, node_attr)
        h = jax.nn.silu(edge_scalars @ fcW1 * (1.0 / np.sqrt(RAD)))
        w = h @ fcW2 * (1.0 / np.sqrt(HID))
        wA, wB, wC, wD = (w[:, :64], w[:, 64:128], w[:, 128:160], w[:, 160:192])
        xs = f_s[edge_src]
        xv = f_v[edge_src]
        y0 = edge_attr[:, :1]
        y1 = edge_attr[:, 1:4]
        outA = wA * xs * y0
        outD = wD * jnp.einsum('eud,ed->eu', xv, y1) * INV3
        outB = wB[:, :, None] * xs[:, :, None] * y1[:, None, :]
        outC = wC[:, :, None] * xv * y0[:, :, None]
        edge_feat = jnp.concatenate([outA, outD, outB.reshape(-1, MUL0 * 3), outC.reshape(-1, MUL1 * 3)], axis=1)
        agg = jax.ops.segment_sum(edge_feat, edge_dst, num_segments=n)
        agg = agg * (1.0 / np.sqrt(NUM_NEIGHBORS))
        ms = agg[:, :MUL0 + MUL1]
        mv = agg[:, MUL0 + MUL1:].reshape(n, MUL0 + MUL1, 3)
        c_s, c_v = _lin(ms, mv, W2_s, W2_v, node_attr)
        conv = jnp.concatenate([c_s, c_v.reshape(n, -1)], axis=1)
        sc = jnp.concatenate([sc_s, sc_v.reshape(n, -1)], axis=1)
        angle = 0.1 * (ms @ W3) * node_attr * (1.0 / np.sqrt(MUL0 + MUL1))
        cos, sin = (jnp.cos(angle), jnp.sin(angle))
        return cos * sc + sin * conv

    def _L2_gnn_ref(node, rbf, rsh, gamma_s, beta_s, gamma_v, Ws_src, Wv_src, Ws_dst, Wv_dst, W_rbf, W_alpha, alpha_dot, Ws_val, Wv_val, Wg, w2_ss, w2_sv, w2_vs, w2_vv0, w2_vv1, Ws_vlin, Wv_vlin, Wps, Wpv, edge_index):
        import jax, jax.numpy as jnp
        import numpy as np
        N, E = (1250, 20000)
        CS, CV = (64, 32)
        AS_, AV, H = (16, 8, 4)
        NB = 16
        SQRT3 = 1.7320508075688772
        SQRT2 = 1.4142135623730951
        EPS = 1e-05

        def _cg_tp(s, v, y0, y1, w_ss, w_sv, w_vs, w_vv0, w_vv1):
            out_s = jnp.concatenate([w_ss * s * y0[:, None], w_vv0 * (jnp.einsum('eci,ei->ec', v, y1) / SQRT3)], axis=-1)
            out_v = jnp.concatenate([(w_sv * s)[:, :, None] * y1[:, None, :], (w_vs * jnp.ones_like(v[..., 0]))[..., None] * v * y0[:, None, None], (w_vv1 * jnp.ones_like(v[..., 0]))[..., None] * (jnp.cross(v, y1[:, None, :]) / SQRT2)], axis=1)
            return (out_s, out_v)

        def _equiv_layernorm(s, v, gamma_s, beta_s, gamma_v):
            mu = jnp.mean(s, axis=-1, keepdims=True)
            var = jnp.var(s, axis=-1, keepdims=True)
            s_n = (s - mu) * jax.lax.rsqrt(var + EPS) * gamma_s + beta_s
            rms = jnp.sqrt(jnp.mean(jnp.sum(v * v, axis=-1), axis=-1, keepdims=True) + EPS)
            v_n = v / rms[..., None] * gamma_v[None, :, None]
            return (s_n, v_n)
        n = node.shape[0]
        e = rsh.shape[0]
        s = node[:, :CS]
        v = node[:, CS:].reshape(n, CV, 3)
        s_n, v_n = _equiv_layernorm(s, v, gamma_s, beta_s, gamma_v)
        src, dst = (edge_index[0], edge_index[1])
        msg_s = (s_n @ Ws_src)[src] + (s_n @ Ws_dst)[dst]
        msg_v = jnp.einsum('ncx,cd->ndx', v_n, Wv_src)[src] + jnp.einsum('ncx,cd->ndx', v_n, Wv_dst)[dst]
        y0, y1 = (rsh[:, 0], rsh[:, 1:4])
        w1 = rbf @ W_rbf
        m1_s, m1_v = _cg_tp(msg_s, msg_v, y0, y1, w1[:, :CS], w1[:, CS:2 * CS], w1[:, 2 * CS:2 * CS + CV], w1[:, 2 * CS + CV:2 * CS + 2 * CV], w1[:, 2 * CS + 2 * CV:])
        a = (m1_s @ W_alpha).reshape(e, H, AS_)
        a = jnp.where(a > 0, a, 0.2 * a)
        a = jnp.sum(a * alpha_dot, axis=-1, keepdims=True)
        amax = jax.ops.segment_max(a, dst, num_segments=n)
        amax = jnp.where(jnp.isfinite(amax), amax, 0.0)
        ex = jnp.exp(a - amax[dst])
        den = jax.ops.segment_sum(ex, dst, num_segments=n)
        alpha = ex / (den[dst] + 1e-16)
        val_s = m1_s @ Ws_val
        val_v = jnp.einsum('ecx,cd->edx', m1_v, Wv_val)
        val_v = val_v * jax.nn.sigmoid(val_s @ Wg)[..., None]
        val_s = jax.nn.sigmoid(val_s)
        m2_s, m2_v = _cg_tp(val_s, val_v, y0, y1, w2_ss, w2_sv, w2_vs, w2_vv0, w2_vv1)
        hs = (m2_s @ Ws_vlin).reshape(e, H, AS_)
        hv = jnp.einsum('ecx,cd->edx', m2_v, Wv_vlin).reshape(e, H, AV, 3)
        h = jnp.concatenate([hs, hv.reshape(e, H, AV * 3)], axis=-1)
        agg = jax.ops.segment_sum(alpha * h, dst, num_segments=n)
        agg_s = agg[:, :, :AS_].reshape(n, H * AS_)
        agg_v = agg[:, :, AS_:].reshape(n, H * AV, 3)
        out = node + jnp.concatenate([agg_s @ Wps, jnp.einsum('ncx,cd->ndx', agg_v, Wpv).reshape(n, CV * 3)], axis=-1)
        return out

    def _L3_gnn_ref(node_input, node_attr, node_crystal_attr, sym_mask, edge_attr, edge_length_embedded, edge_src, edge_dst, Ws_sc_a, Wv_sc_a, Ws_sc_c, Wv_sc_c, Ws_l1_a, Wv_l1_a, Ws_l1_c, Wv_l1_c, W_fc1, W_fc2, Ws_l2_a, Wv_l2_a, Ws_l2_c, Wv_l2_c, Ws_l3, Wv_l3):
        import jax, jax.numpy as jnp
        import numpy as np
        N = 25000
        E = 25000
        S = 64
        V = 32
        NB = 10
        H = 100
        WN = 192
        MID = 96
        NUM_NEIGHBORS = 16.0
        C_S = float(np.sin(np.pi / 8.0))
        C_X = float(np.cos(np.pi / 8.0))
        SQRT3 = float(np.sqrt(3.0))

        def fctp_scalar_attr(xs, xv, attr, Ws, Wv):
            s = xs * attr @ Ws
            v = jnp.einsum('nuc,uo->noc', xv * attr[:, :, None], Wv)
            return (s, v)
        n = node_input.shape[0]
        xs = node_input[:, :S]
        xv = node_input[:, S:].reshape(n, V, 3)
        ssa, sva = fctp_scalar_attr(xs, xv, node_attr, Ws_sc_a, Wv_sc_a)
        ssc, svc = fctp_scalar_attr(xs, xv, node_crystal_attr, Ws_sc_c, Wv_sc_c)
        s_s, s_v = (ssa + ssc, sva + svc)
        l1a_s, l1a_v = fctp_scalar_attr(xs, xv, node_attr, Ws_l1_a, Wv_l1_a)
        l1c_s, l1c_v = fctp_scalar_attr(xs, xv, node_crystal_attr, Ws_l1_c, Wv_l1_c)
        x1s, x1v = (l1a_s + l1c_s, l1a_v + l1c_v)
        weight = jax.nn.silu(edge_length_embedded @ W_fc1) @ W_fc2
        w0 = weight[:, :S]
        w1 = weight[:, S:2 * S]
        w2 = weight[:, 2 * S:2 * S + V]
        w3 = weight[:, 2 * S + V:]
        gs = x1s[edge_src]
        gv = x1v[edge_src]
        e_s = edge_attr[:, :1]
        e_v = edge_attr[:, 1:]
        mid0a = w0 * gs * e_s
        mid0b = w3 * (jnp.einsum('euc,ec->eu', gv, e_v) / SQRT3)
        mid1a = w1[:, :, None] * gs[:, :, None] * e_v[:, None, :]
        mid1b = w2[:, :, None] * gv * e_s[:, :, None]
        edge_feat = jnp.concatenate([mid0a, mid0b, mid1a.reshape(-1, 3 * S), mid1b.reshape(-1, 3 * V)], axis=-1)
        agg = jax.ops.segment_sum(edge_feat, edge_dst, num_segments=n) / np.sqrt(NUM_NEIGHBORS)
        m_s = agg[:, :MID]
        m_v = agg[:, MID:].reshape(n, MID, 3)
        l2a_s, l2a_v = fctp_scalar_attr(m_s, m_v, node_attr, Ws_l2_a, Wv_l2_a)
        l2c_s, l2c_v = fctp_scalar_attr(m_s, m_v, node_crystal_attr, Ws_l2_c, Wv_l2_c)
        m_s, m_v = (l2a_s + l2c_s, l2a_v + l2c_v)
        o_s, o_v = fctp_scalar_attr(m_s, m_v, sym_mask, Ws_l3, Wv_l3)
        out_s = C_S * s_s + C_X * o_s
        out_v = C_S * s_v + C_X * o_v
        return jnp.concatenate([out_s, out_v.reshape(n, 3 * V)], axis=-1)
    edge_index = jnp.stack([src, dst])
    h = jnp.maximum(_layernorm(x, axis=-1), 0.0)
    x = x + _L0_gnn_ref(h, node_vec1, edge_attr_4, edge_attr_8, L0_gnn_Wsc0, L0_gnn_Wsc1, L0_gnn_Wl1_0, L0_gnn_Wl1_1, L0_gnn_Wfc1, L0_gnn_Wfc2, L0_gnn_Wfc3, L0_gnn_Wl2_s, L0_gnn_Wl2_v, L0_gnn_Wa, src, dst)
    h = jnp.maximum(_layernorm(x, axis=-1), 0.0)
    x = x + _L1_gnn_ref(h, node_vec1, edge_attr_4, edge_attr_8, L1_gnn_W_sc_s, L1_gnn_W_sc_v, L1_gnn_W1_s, L1_gnn_W1_v, L1_gnn_W2_s, L1_gnn_W2_v, L1_gnn_W3, L1_gnn_fcW1, L1_gnn_fcW2, src, dst)
    h = jnp.maximum(_layernorm(x, axis=-1), 0.0)
    x = x + _L2_gnn_ref(h, edge_attr_16, edge_attr_4, L2_gnn_gamma_s, L2_gnn_beta_s, L2_gnn_gamma_v, L2_gnn_Ws_src, L2_gnn_Wv_src, L2_gnn_Ws_dst, L2_gnn_Wv_dst, L2_gnn_W_rbf, L2_gnn_W_alpha, L2_gnn_alpha_dot, L2_gnn_Ws_val, L2_gnn_Wv_val, L2_gnn_Wg, L2_gnn_w2_ss, L2_gnn_w2_sv, L2_gnn_w2_vs, L2_gnn_w2_vv0, L2_gnn_w2_vv1, L2_gnn_Ws_vlin, L2_gnn_Wv_vlin, L2_gnn_Wps, L2_gnn_Wpv, edge_index)
    h = jnp.maximum(_layernorm(x, axis=-1), 0.0)
    x = x + _L3_gnn_ref(h, node_vec1, node_vec1_n2, node_vec1_n3, edge_attr_4, edge_attr_10, src, dst, L3_gnn_Ws_sc_a, L3_gnn_Wv_sc_a, L3_gnn_Ws_sc_c, L3_gnn_Wv_sc_c, L3_gnn_Ws_l1_a, L3_gnn_Wv_l1_a, L3_gnn_Ws_l1_c, L3_gnn_Wv_l1_c, L3_gnn_W_fc1, L3_gnn_W_fc2, L3_gnn_Ws_l2_a, L3_gnn_Wv_l2_a, L3_gnn_Ws_l2_c, L3_gnn_Wv_l2_c, L3_gnn_Ws_l3, L3_gnn_Wv_l3)
    return x

_drawn_inputs = setup_inputs


def setup_inputs(seed=0):
    import zlib

    import numpy as np

    out = dict(_drawn_inputs(seed))
    spreads = {'L2_gnn_gamma_s': (1.0, 0.2), 'L2_gnn_beta_s': (0.0, 0.1), 'L2_gnn_gamma_v': (1.0, 0.2)}
    factors = {}
    for name, (base, spread) in spreads.items():
        noise = np.random.default_rng([zlib.crc32(name.encode()), seed]).standard_normal(out[name].shape)
        drawn = base * np.exp(spread * noise) if base else spread * noise
        out[name] = jnp.asarray(drawn.astype(out[name].dtype))
    for name, factor in factors.items():
        out[name] = (out[name] * factor).astype(out[name].dtype)
    return out
```

```python
NODES, EDGES, FEAT = 6250, 100000, 160
P = 128
SC, VC, XYZ = 64, 32, 3
VF = VC * XYZ
NT = -(-NODES // P)
NPAD = NT * P
TG = 4
GE = TG * P
NG = 196
EPAD = NG * GE
WIN = 64
COLS = NPAD + WIN
MID = SC + VC
YC = 6
HEADS, HS, HV = 4, 16, 8
HF = HS + XYZ * HV
CHUNKS = P // HEADS
CHUNK = EPAD // CHUNKS
EPS = 1e-5
LOWEST = -1.5e38


def build(nc, A, out):
    from contextlib import ExitStack

    import concourse.bass as bass
    from concourse import mybir

    F32, I32 = mybir.dt.float32, mybir.dt.int32
    ALU, ACT, AX = mybir.AluOpType, mybir.ActivationFunctionType, mybir.AxisListType
    ds = bass.ds

    def at_least(eng, sem, value):
        if isinstance(value, int) and value <= 0:
            return
        eng.wait_ge(sem, value)

    def gate(eng, settled, *waits):
        waits = [(sem, v if isinstance(v, int) else eng.to_reg(v)) for sem, v in waits if not isinstance(v, int) or v > 0]
        eng.wait_ge(*settled)
        for sem, v in waits:
            eng.wait_ge(sem, v)

    def steps(eng, n, lag, emit, warm=4, unroll=2):
        for i in range(warm):
            emit(i, i % unroll, i // unroll)
        turns = (n - warm) // unroll
        with eng.Fori(0, turns) as j:
            for k in range(unroll):
                emit(j * unroll + (warm + k), (warm + k) % unroll, j + (warm + k) // unroll)
        for i in range(warm + turns * unroll, n + lag):
            emit(i, i % unroll, i // unroll)

    def live(i, n):
        return not isinstance(i, int) or 0 <= i < n

    def back(s, r, lag, unroll=2):
        return (s - lag) % unroll, r + (s - lag) // unroll

    table = [nc.dram_tensor(f"node_table_{n}", (NPAD, FEAT), F32).ap() for n in range(5)]
    self_rows = nc.dram_tensor("l1_self_rows", (NPAD, FEAT), F32).ap()
    messages = nc.dram_tensor("l2_messages", (EPAD, FEAT), F32).ap()
    scores_T = nc.dram_tensor("l2_scores", (HEADS, EPAD), F32).ap()
    exps_T = nc.dram_tensor("l2_exps", (HEADS, EPAD), F32).ap()
    chunk_ends = nc.dram_tensor("l2_chunk_ends", (2, P), F32).ap()
    chunk_carries = nc.dram_tensor("l2_chunk_carries", (2, P), F32).ap()
    turn_row = nc.dram_tensor("l1_turn_row", (1, NPAD), F32).ap()

    whole = ExitStack()

    def sbuf(ctx, name, shape, dt=F32):
        return ctx.enter_context(nc.sbuf_tensor(name, shape, dt))

    def psum(ctx, name, shape):
        return ctx.enter_context(nc.psum_tensor(name, shape, F32))

    layer_sems = []

    def sem(ctx, name):
        layer_sems.append(nc.alloc_semaphore(name))
        return layer_sems[-1]

    def end_layer():
        nc.clear_and_free_semaphores(layer_sems)
        layer_sems.clear()
        nc.all_engine_barrier()

    with whole:
        x = sbuf(whole, "x", [P, NT * FEAT])
        y4 = sbuf(whole, "y4", [P, NG * TG * 4])
        sums_T = sbuf(whole, "sums_T", [P, 4 * COLS])
        dst_rel = sbuf(whole, "dst_rel", [P, NG * TG])
        window_row = sbuf(whole, "window_row", [1, NG], I32)
        iota_win = sbuf(whole, "iota_win", [P, WIN])
        ident = sbuf(whole, "ident", [P, P])
        attr = sbuf(whole, "attr", [P, 3, NT])
        row_scale = sbuf(whole, "row_scale", [P, 4])

        x3 = x[:, :].rearrange("p (t f) -> p t f", t=NT)
        sums4 = sums_T[:, :].rearrange("p (b n) -> p b n", b=4)

        def setup():
            with ExitStack() as ctx:
                dst_i = sbuf(ctx, "dst_i", [P, NG * TG], I32)
                dst_f = sbuf(ctx, "dst_f", [P, NG * TG])
                first_f = sbuf(ctx, "first_f", [1, NG])
                ones_row = sbuf(ctx, "ones_row", [1, P])
                iota_i = sbuf(ctx, "iota_i", [P, WIN], I32)
                diag_i = sbuf(ctx, "diag_i", [P, P], I32)
                first_ps = psum(ctx, "first_ps", [P, NG])
                loaded = sem(ctx, "setup_loaded")
                iotas = sem(ctx, "setup_iotas")
                firsts = sem(ctx, "setup_firsts")
                spread = sem(ctx, "setup_spread")
                made = sem(ctx, "setup_made")
                with nc.Block() as block:

                    @block.sync
                    def _(sp):
                        sp.dma_start(x3, A["x"].rearrange("(t p) f -> p t f", p=P)).then_inc(loaded, 16)
                        sp.dma_start(dst_i[:, :], A["dst_tiles"]).then_inc(loaded, 16)
                        sp.dma_start(window_row[:, :], A["dst_first"]).then_inc(loaded, 16)
                        sp.dma_start(y4[:, :], A["y4"]).then_inc(loaded, 16)
                        for n in range(3):
                            sp.dma_start(attr[:, n, :], A[f"attr_{n}"]).then_inc(loaded, 16)

                    @block.gpsimd
                    def _(pool):
                        nc.gpsimd.iota(iota_i[:, :], pattern=[[1, WIN]], base=0, channel_multiplier=0).then_inc(iotas, 1)
                        nc.gpsimd.iota(diag_i[:, :], pattern=[[1, P]], base=0, channel_multiplier=-1).then_inc(iotas, 1)

                    @block.vector
                    def _(dve):
                        nc.vector.memset(ones_row[:, :], 1.0).then_inc(made, 1)
                        nc.vector.memset(row_scale[:, :], 1.0).then_inc(made, 1)
                        dve.wait_ge(made, 2)
                        nc.vector.memset(row_scale[SC:MID, 0:1], 3.0 ** -0.5).then_inc(made, 1)
                        nc.vector.memset(row_scale[MID:P, 1:2], 2.0 ** -0.5).then_inc(made, 1)
                        nc.vector.memset(row_scale[VC:SC, 2:3], 2.0 ** -0.5).then_inc(made, 1)
                        nc.vector.memset(row_scale[MID:P, 2:3], 2.0 ** -0.5).then_inc(made, 1)
                        dve.wait_ge(iotas, 2)
                        nc.vector.tensor_copy(iota_win[:, :], iota_i[:, :]).then_inc(made, 1)
                        nc.vector.tensor_scalar(ident[:, :], diag_i[:, :], 0.0, None, ALU.is_equal).then_inc(made, 1)
                        dve.wait_ge(loaded, 16 * 7)
                        nc.vector.tensor_copy(first_f[:, :], window_row[:, :]).then_inc(firsts, 1)
                        nc.vector.tensor_copy(dst_f[:, :], dst_i[:, :]).then_inc(made, 1)
                        dve.wait_ge(made, 9)
                        dve.wait_ge(spread, 1)
                        nc.vector.tensor_tensor(
                            dst_rel[:, :].rearrange("p (g t) -> p g t", t=TG),
                            dst_f[:, :].rearrange("p (g t) -> p g t", t=TG),
                            first_ps[:, :].unsqueeze(2).to_broadcast([P, NG, TG]),
                            ALU.subtract).then_inc(made, 1)

                    @block.tensor
                    def _(pe):
                        pe.wait_ge(made, 1)
                        pe.wait_ge(firsts, 1)
                        nc.tensor.matmul(first_ps[:, :], ones_row[:, :], first_f[:, :]).then_inc(spread, 1)

        def norm_all(tag, equivariant):
            h = sums_T[:, 0:NT * FEAT]
            sq = sums_T[:, NT * FEAT:2 * NT * FEAT]
            h3 = h.rearrange("p (t f) -> p t f", t=NT)
            sq3 = sq.rearrange("p (t f) -> p t f", t=NT)
            with ExitStack() as ctx:
                stat = sbuf(ctx, f"{tag}_stat", [P, 8, NT])
                dve_at = sem(ctx, f"{tag}_norm_dve")
                act_at = sem(ctx, f"{tag}_norm_act")

                def wide(n, width):
                    return stat[:, n, :].unsqueeze(2).to_broadcast([P, NT, width])

                with nc.Block() as block:

                    @block.vector
                    def _(dve):
                        count = [0]

                        def then(ins):
                            count[0] += 1
                            ins.then_inc(dve_at, 1)
                            dve.wait_ge(dve_at, count[0])

                        then(nc.vector.tensor_reduce(stat[:, 0, :], x3, AX.X, ALU.add))
                        then(nc.vector.tensor_scalar(stat[:, 1, :], stat[:, 0, :], 1.0 / FEAT, None, ALU.mult))
                        then(nc.vector.tensor_tensor(h3, x3, wide(1, FEAT), ALU.subtract))
                        dve.wait_ge(act_at, 1)
                        then(nc.vector.tensor_reduce(stat[:, 2, :], sq3, AX.X, ALU.add))
                        then(nc.vector.tensor_scalar(stat[:, 3, :], stat[:, 2, :], 1.0 / FEAT, EPS, ALU.mult, ALU.add))
                        dve.wait_ge(act_at, 2)
                        then(nc.vector.reciprocal(stat[:, 5, :], stat[:, 4, :]))
                        then(nc.vector.tensor_tensor(h3, h3, wide(5, FEAT), ALU.mult))
                        then(nc.vector.tensor_scalar(h, h, 0.0, None, ALU.max))
                        if equivariant:
                            then(nc.vector.tensor_tensor(x[:, :], x[:, :], h, ALU.add))
                            hs, hv = h3[:, :, 0:SC], h3[:, :, SC:FEAT]
                            then(nc.vector.tensor_reduce(stat[:, 0, :], hs, AX.X, ALU.add))
                            then(nc.vector.tensor_scalar(stat[:, 1, :], stat[:, 0, :], 1.0 / SC, None, ALU.mult))
                            then(nc.vector.tensor_tensor(hs, hs, wide(1, SC), ALU.subtract))
                            dve.wait_ge(act_at, 3)
                            then(nc.vector.tensor_reduce(stat[:, 2, :], sq3[:, :, 0:SC], AX.X, ALU.add))
                            then(nc.vector.tensor_reduce(stat[:, 3, :], sq3[:, :, SC:FEAT], AX.X, ALU.add))
                            then(nc.vector.tensor_scalar(stat[:, 2, :], stat[:, 2, :], 1.0 / SC, EPS, ALU.mult, ALU.add))
                            then(nc.vector.tensor_scalar(stat[:, 3, :], stat[:, 3, :], 1.0 / VC, EPS, ALU.mult, ALU.add))
                            dve.wait_ge(act_at, 4)
                            then(nc.vector.reciprocal(stat[:, 6:8, :], stat[:, 4:6, :]))
                            then(nc.vector.tensor_tensor(hs, hs, wide(6, SC), ALU.mult))
                            then(nc.vector.tensor_tensor(hv, hv, wide(7, VF), ALU.mult))

                    @block.scalar
                    def _(act):
                        act.wait_ge(dve_at, 3)
                        nc.scalar.activation(sq, h, ACT.Square).then_inc(act_at, 1)
                        act.wait_ge(dve_at, 5)
                        nc.scalar.activation(stat[:, 4, :], stat[:, 3, :], ACT.Sqrt).then_inc(act_at, 1)
                        if equivariant:
                            act.wait_ge(dve_at, 12)
                            nc.scalar.activation(sq, h, ACT.Square).then_inc(act_at, 1)
                            act.wait_ge(dve_at, 16)
                            nc.scalar.activation(stat[:, 4:6, :], stat[:, 2:4, :], ACT.Sqrt).then_inc(act_at, 1)

        def node_pass(tag, scalar_maps, vector_maps, tables, finish, n_fin, coefs=(), gamma=None):
            ns, nv, n_tab = SC * len(scalar_maps), VF * len(vector_maps), len(tables)
            norm = sums_T[:, 0:NT * FEAT]
            with ExitStack() as ctx:
                w_s = sbuf(ctx, f"{tag}_w_s", [SC, ns])
                w_v = sbuf(ctx, f"{tag}_w_v", [VF, nv])
                coef = sbuf(ctx, f"{tag}_coef", [P, 8, NT])
                gam = sbuf(ctx, f"{tag}_gam", [VF, 4])
                tile = [sbuf(ctx, f"{tag}_tile{s}", [P, FEAT]) for s in range(2)]
                tile_T = [sbuf(ctx, f"{tag}_tile_T{s}", [VF, 2 * P]) for s in range(2)]
                rows = [[sbuf(ctx, f"{tag}_rows{k}_{s}", [P, FEAT]) for k in range(n_tab)] for s in range(2)]
                temp = sbuf(ctx, f"{tag}_temp", [P, 2 * FEAT])
                ps_t = [psum(ctx, f"{tag}_ps_t{s}", [P, 512]) for s in range(2)]
                ps_s = [psum(ctx, f"{tag}_ps_s{s}", [P, 512]) for s in range(2)]
                ps_v = [psum(ctx, f"{tag}_ps_v{s}", [P, 512]) for s in range(2)]
                zeroed = sem(ctx, f"{tag}_zeroed")
                w_loaded = sem(ctx, f"{tag}_w_loaded")
                w_ready = sem(ctx, f"{tag}_w_ready")
                coef_ready = sem(ctx, f"{tag}_coef_ready")
                copied = sem(ctx, f"{tag}_copied")
                turned = sem(ctx, f"{tag}_turned")
                tile_ready = sem(ctx, f"{tag}_tile_ready")
                mapped = sem(ctx, f"{tag}_mapped")
                fin = sem(ctx, f"{tag}_fin")
                stored = [sem(ctx, f"{tag}_stored{s}") for s in range(2)]
                n_w = len(scalar_maps) + XYZ * len(vector_maps) + (2 + XYZ if gamma else 0)

                with nc.Block() as block:

                    @block.sync
                    def _(sp):
                        for n, w in enumerate(scalar_maps):
                            sp.dma_start(w_s[:, n * SC:(n + 1) * SC], A[w]).then_inc(w_loaded, 16)
                        sp.wait_ge(zeroed, 1)
                        for n, w in enumerate(vector_maps):
                            for c in range(XYZ):
                                at = n * VF + c * VC
                                sp.dma_start(w_v[c:VF:XYZ, at:at + VC], A[w]).then_inc(w_loaded, 16)
                        if gamma:
                            sp.dma_start(gam[0:SC, 0:1], A[gamma[0]]).then_inc(w_loaded, 16)
                            sp.dma_start(gam[0:SC, 1:2], A[gamma[1]]).then_inc(w_loaded, 16)
                            for c in range(XYZ):
                                sp.dma_start(gam[c:VF:XYZ, 2:3], A[gamma[2]]).then_inc(w_loaded, 16)

                        def store(i, s, r):
                            sp.wait_ge(fin, (i + 1) * n_fin)
                            for k in range(n_tab):
                                sp.dma_start(tables[k][ds(i * P, P), :], rows[s][k][:, :]).then_inc(stored[s], 16)

                        steps(sp, NT, 0, store)
                        for s in range(2):
                            sp.wait_ge(stored[s], 16 * n_tab * ((NT + 1 - s) // 2))

                    @block.scalar
                    def _(act):
                        if gamma:
                            act.wait_ge(w_loaded, 16 * n_w)

                        def step(i, s, r):
                            if live(i, NT):
                                at_least(act, turned, i - 1)
                                nc.scalar.activation(tile[s][:, :], norm[:, ds(i * FEAT, FEAT)], ACT.Copy).then_inc(copied, 1)
                            if live(i - 1, NT):
                                s1, _ = back(s, r, 1)
                                at_least(act, turned, i)
                                at_least(act, mapped, i - 2)
                                if gamma:
                                    nc.scalar.activation(tile_T[s1][0:SC, 0:P], ps_t[s1][0:SC, 0:P], ACT.Identity,
                                                         bias=gam[0:SC, 1:2], scale=gam[0:SC, 0:1]).then_inc(tile_ready, 1)
                                else:
                                    nc.scalar.activation(tile_T[s1][0:SC, 0:P], ps_t[s1][0:SC, 0:P], ACT.Copy).then_inc(tile_ready, 1)
                                nc.scalar.activation(tile_T[s1][0:VF, P:2 * P], ps_t[s1][0:VF, P:2 * P], ACT.Copy).then_inc(tile_ready, 1)

                        steps(act, NT, 1, step)

                    @block.tensor
                    def _(pe):
                        pe.wait_ge(w_loaded, 16 * n_w)
                        if gamma:
                            pe.wait_ge(w_ready, 1)

                        def step(i, s, r):
                            if live(i, NT):
                                at_least(pe, copied, i + 1)
                                at_least(pe, tile_ready, 2 * (i - 1))
                                nc.tensor.transpose(ps_t[s][0:VF, P:2 * P], tile[s][:, SC:FEAT], ident[:, :])
                                nc.tensor.transpose(ps_t[s][0:SC, 0:P], tile[s][:, 0:SC], ident[:, :]).then_inc(turned, 1)
                            if live(i - 1, NT):
                                s1, _ = back(s, r, 1)
                                at_least(pe, tile_ready, 2 * i)
                                at_least(pe, fin, (i - 2) * n_fin)
                                nc.tensor.matmul(ps_s[s1][:, 0:ns], tile_T[s1][0:SC, 0:P], w_s[:, :])
                                nc.tensor.matmul(ps_v[s1][:, 0:nv], tile_T[s1][0:VF, P:2 * P], w_v[:, :]).then_inc(mapped, 1)

                        steps(pe, NT, 1, step)

                    @block.vector
                    def _(dve):
                        nc.vector.memset(w_v[:, :], 0.0).then_inc(zeroed, 1)
                        for n, (k, factor) in enumerate(coefs):
                            nc.vector.tensor_scalar(coef[:, n, :], attr[:, k, :], factor, None, ALU.mult).then_inc(coef_ready, 1)
                        if gamma:
                            dve.wait_ge(w_loaded, 16 * n_w)
                            nc.vector.tensor_scalar(w_v[:, :], w_v[:, :], gam[0:VF, 2:3], None, ALU.mult).then_inc(w_ready, 1)
                        dve.wait_ge(coef_ready, len(coefs))

                        def step(i, s, r):
                            at_least(dve, mapped, i + 1)
                            at_least(dve, stored[s], 16 * n_tab * r)
                            at_least(dve, fin, i * n_fin)
                            finish(dve, i, ps_s[s], ps_v[s], rows[s], coef, temp, fin, i * n_fin)

                        steps(dve, NT, 0, step)

        def xs_at(t):
            return x[:, ds(t * FEAT, SC)]

        def xv_at(t):
            return x[:, ds(t * FEAT + SC, VF)].rearrange("p (u c) -> p c u", c=XYZ)

        def by_component(ap):
            return ap.rearrange("p (c u) -> p c u", c=XYZ)

        def finish_l0(dve, t, ps_s, ps_v, rows, coef, temp, fin, k):
            a_s, a_v = coef[:, 0, ds(t, 1)], coef[:, 1, ds(t, 1)]
            nc.vector.tensor_scalar(rows[0][:, 0:SC], ps_s[:, 0:SC], a_s, None, ALU.mult).then_inc(fin, 1)
            nc.vector.tensor_scalar(rows[0][:, SC:FEAT], ps_v[:, 0:VF], a_v, None, ALU.mult).then_inc(fin, 1)
            nc.vector.scalar_tensor_tensor(xs_at(t), ps_s[:, SC:2 * SC], a_s, xs_at(t), ALU.mult, ALU.add).then_inc(fin, 1)
            nc.vector.scalar_tensor_tensor(xv_at(t), by_component(ps_v[:, VF:2 * VF]), a_v, xv_at(t),
                                           ALU.mult, ALU.add).then_inc(fin, 1)

        def finish_l1(dve, t, ps_s, ps_v, rows, coef, temp, fin, k):
            a_s, a_v = coef[:, 0, ds(t, 1)], coef[:, 1, ds(t, 1)]
            for n in range(2):
                nc.vector.tensor_scalar(rows[n][:, 0:SC], ps_s[:, n * SC:(n + 1) * SC], a_s, None, ALU.mult).then_inc(fin, 1)
                nc.vector.tensor_scalar(rows[n][:, SC:FEAT], ps_v[:, n * VF:(n + 1) * VF], a_v, None, ALU.mult).then_inc(fin, 1)

        def finish_l2(dve, t, ps_s, ps_v, rows, coef, temp, fin, k):
            for n in range(2):
                nc.vector.tensor_copy(rows[n][:, 0:SC], ps_s[:, n * SC:(n + 1) * SC]).then_inc(fin, 1)
                nc.vector.tensor_copy(rows[n][:, SC:FEAT], ps_v[:, n * VF:(n + 1) * VF]).then_inc(fin, 1)

        def finish_l3(dve, t, ps_s, ps_v, rows, coef, temp, fin, k):
            a0, a1, c0, c1 = (coef[:, n, ds(t, 1)] for n in range(4))
            nc.vector.tensor_scalar(temp[:, 0:SC], ps_s[:, 0:SC], a0, None, ALU.mult).then_inc(fin, 1)
            nc.vector.tensor_scalar(temp[:, SC:FEAT], ps_v[:, 0:VF], a0, None, ALU.mult).then_inc(fin, 1)
            nc.vector.scalar_tensor_tensor(xs_at(t), ps_s[:, 2 * SC:3 * SC], c0, xs_at(t), ALU.mult, ALU.add).then_inc(fin, 1)
            nc.vector.scalar_tensor_tensor(xv_at(t), by_component(ps_v[:, 2 * VF:3 * VF]), c0, xv_at(t),
                                           ALU.mult, ALU.add).then_inc(fin, 1)
            dve.wait_ge(fin, k + 4)
            nc.vector.scalar_tensor_tensor(rows[0][:, 0:SC], ps_s[:, SC:2 * SC], a1, temp[:, 0:SC], ALU.mult, ALU.add).then_inc(fin, 1)
            nc.vector.scalar_tensor_tensor(rows[0][:, SC:FEAT], ps_v[:, VF:2 * VF], a1, temp[:, SC:FEAT],
                                           ALU.mult, ALU.add).then_inc(fin, 1)
            nc.vector.scalar_tensor_tensor(xs_at(t), ps_s[:, 3 * SC:4 * SC], c1, xs_at(t), ALU.mult, ALU.add).then_inc(fin, 1)
            nc.vector.scalar_tensor_tensor(xv_at(t), by_component(ps_v[:, 3 * VF:4 * VF]), c1, xv_at(t),
                                           ALU.mult, ALU.add).then_inc(fin, 1)

        def warm_up(bank):
            for _ in range(6):
                nc.tensor.matmul(bank[:, 0:512], ident[:, :], x[:, 0:512])

        def edge_pass(tag, rows_of, edge_T, w_in, w_mid, w_out, act_fn, scales):
            k_in, hid = A[w_in].shape
            layers = 2 if w_mid else 1
            wn = 2 * SC + 2 * VC
            SS, SV, VS, VV = 0, SC, 2 * SC, 2 * SC + VC
            K = 9
            U = 4
            FETCH = 4
            lag = layers + 1
            with ExitStack() as ctx:
                def slots(n, name, shape, dt=F32):
                    return [sbuf(ctx, f"{tag}_edge_{name}{s}", shape, dt) for s in range(n)]

                wi = sbuf(ctx, f"{tag}_edge_wi", [k_in, hid])
                wm = sbuf(ctx, f"{tag}_edge_wm", [hid, hid])
                wo = sbuf(ctx, f"{tag}_edge_wo", [hid, wn])
                idx = slots(FETCH, "idx", [P, TG], I32)
                g = slots(FETCH, "g", [P, TG, FEAT])
                ea = slots(2, "ea", [k_in, GE])
                h = [slots(2, f"h{n}_", [hid, GE]) for n in range(layers)]
                gy = slots(2, "gy", [P, TG, FEAT])
                prod = slots(2, "prod", [P, TG, 4, MID])
                hot = slots(2, "hot", [P, TG, WIN])
                pw = sbuf(ctx, f"{tag}_edge_pw", [P, TG, SC])
                vy = sbuf(ctx, f"{tag}_edge_vy", [P, TG, XYZ, VC])
                dot = sbuf(ctx, f"{tag}_edge_dot", [P, 2, TG, VC])
                h_ps = [psum(ctx, f"{tag}_edge_h_ps{n}", [P, GE]) for n in range(2)]
                w_ps = [psum(ctx, f"{tag}_edge_w_ps{s}", [P, TG, 256]) for s in range(2)]
                win_ps = [psum(ctx, f"{tag}_edge_win_ps{s}", [P, 512]) for s in range(2)]
                zeroed = sem(ctx, f"{tag}_edge_zeroed")
                w_loaded = sem(ctx, f"{tag}_edge_w_loaded")
                idx_loaded = [sem(ctx, f"{tag}_edge_idx_loaded{s}") for s in range(FETCH)]
                fetched = [sem(ctx, f"{tag}_edge_fetched{s}") for s in range(FETCH)]
                ea_loaded = [sem(ctx, f"{tag}_edge_ea_loaded{s}") for s in range(2)]
                hidden = [sem(ctx, f"{tag}_edge_hidden{n}") for n in range(layers)]
                active = [sem(ctx, f"{tag}_edge_active{n}") for n in range(layers)]
                scaled = sem(ctx, f"{tag}_edge_scaled")
                weighed = sem(ctx, f"{tag}_edge_weighed")
                made = sem(ctx, f"{tag}_edge_made")
                summed = sem(ctx, f"{tag}_edge_summed")
                added = sem(ctx, f"{tag}_edge_added")
                last = layers - 1

                def half(s, r):
                    return s % 2, r * 2 + s // 2

                with nc.Block() as block:

                    @block.sync
                    def _(sp):
                        sp.dma_start(wi[:, :], A[w_in]).then_inc(w_loaded, 16)
                        if w_mid:
                            sp.dma_start(wm[:, :], A[w_mid]).then_inc(w_loaded, 16)
                        sp.dma_start(wo[:, :], A[w_out]).then_inc(w_loaded, 16)

                        def step(i, s, r):
                            at_least(sp, fetched[s], 16 * TG * r)
                            sp.dma_start(idx[s][:, :], A["src_groups"][ds(i * P, P), :]).then_inc(idx_loaded[s], 16)
                            at_least(sp, hidden[0], i - 1)
                            sp.dma_start(ea[s % 2][:, :], A[edge_T][:, ds(i * GE, GE)]).then_inc(ea_loaded[s % 2], 16)

                        steps(sp, NG, 0, step, unroll=U)

                    @block.gpsimd
                    def _(pool):
                        for b in range(4):
                            nc.gpsimd.memset(sums_T[:, b * COLS:(b + 1) * COLS], 0.0).then_inc(zeroed, 1)

                        def step(i, s, r):
                            gate(pool, (w_loaded, 16 * (layers + 1)),
                                 (idx_loaded[s], 16 * (r + 1)),
                                 (made, (i - 3) * K))
                            for t in range(TG):
                                pool.indirect_dma_start(g[s][:, t, :], None, rows_of,
                                                        bass.IndirectOffsetOnAxis(idx[s][:, t:t + 1], 0)).then_inc(fetched[s], 16)

                        steps(pool, NG, 0, step, unroll=U)

                    @block.tensor
                    def _(pe):
                        pe.wait_ge(w_loaded, 16 * (layers + 1))

                        def step(i, s, r):
                            if isinstance(i, int) and i == lag + 2:
                                pe.wait_ge(active[last], i - last)
                                warm_up(h_ps[1])
                            if live(i, NG):
                                s0, r0 = half(s, r)
                                at_least(pe, ea_loaded[s0], 16 * (r0 + 1))
                                at_least(pe, active[0], i)
                                nc.tensor.matmul(h_ps[0][0:hid, :], wi[:, :], ea[s0][:, :]).then_inc(hidden[0], 1)
                            if w_mid and live(i - 1, NG):
                                s1 = (s - 1) % 2
                                gate(pe, (w_loaded, 16 * (layers + 1)),
                                     (active[0], i),
                                     (active[1], i - 1))
                                nc.tensor.matmul(h_ps[1][0:hid, :], wm[:, :], h[0][s1][:, :]).then_inc(hidden[1], 1)
                            if live(i - layers, NG):
                                s2 = (s - layers) % 2
                                at_least(pe, active[last], i - layers + 1)
                                at_least(pe, made, (i - layers - 1) * K)
                                for t in range(TG):
                                    ins = nc.tensor.matmul(w_ps[s2][:, t, 0:wn], h[last][s2][:, t * P:(t + 1) * P], wo[:, :])
                                ins.then_inc(weighed, 1)
                            if live(i - lag, NG):
                                s3 = (s - lag) % 2
                                at_least(pe, made, (i - lag + 1) * K)
                                at_least(pe, added, i - lag - 1)
                                for b in range(4):
                                    for t in range(TG):
                                        ins = nc.tensor.matmul(win_ps[s3][0:MID, b * WIN:(b + 1) * WIN], prod[s3][:, t, b, :],
                                                               hot[s3][:, t, :], start=t == 0, stop=t == TG - 1)
                                ins.then_inc(summed, 1)

                        steps(pe, NG, lag, step, warm=8, unroll=U)

                    @block.scalar
                    def _(act):
                        def step(i, s, r):
                            for n in range(layers):
                                if live(i - n, NG):
                                    s1 = (s - n) % 2
                                    after = hidden[n + 1] if n < last else weighed
                                    at_least(act, hidden[n], i - n + 1)
                                    at_least(act, after, i - n - 1)
                                    nc.scalar.activation(h[n][s1][:, :], h_ps[n][0:hid, :], act_fn,
                                                         scale=scales[n]).then_inc(active[n], 1)
                            if live(i - last, NG):
                                k = i - last
                                sk, rk = back(s, r, last, U)
                                at_least(act, made, (k - 1) * K)
                                at_least(act, fetched[sk], 16 * TG * (rk + 1))
                                for t in range(TG):
                                    ins = nc.scalar.activation(gy[sk % 2][:, t, :], g[sk][:, t, :], ACT.Copy,
                                                               scale=y4[:, ds((k * TG + t) * 4, 1)])
                                ins.then_inc(scaled, 1)

                        steps(act, NG, last, step, warm=8, unroll=U)

                    @block.vector
                    def _(dve):
                        dve.wait_ge(zeroed, 4)

                        def products(i, s, r):
                            def done(n):
                                return i * K + n

                            s0, _ = half(s, r)
                            w, rows, q = w_ps[s0], g[s], prod[s0]
                            xyz = y4[:, ds(i * TG * 4, TG * 4)].rearrange("p (t c) -> p t c", c=4)[:, :, 1:4].unsqueeze(3)
                            vec = rows[:, :, SC:FEAT].rearrange("p t (c u) -> p t c u", c=XYZ)
                            vec0 = gy[s0][:, :, SC:FEAT].rearrange("p t (c u) -> p t c u", c=XYZ)
                            at_least(dve, summed, i - 1)
                            at_least(dve, made, done(0))
                            nc.vector.tensor_tensor(hot[s0][:, :, :], iota_win[:, :].unsqueeze(1).to_broadcast([P, TG, WIN]),
                                                    dst_rel[:, ds(i * TG, TG)].unsqueeze(2).to_broadcast([P, TG, WIN]),
                                                    ALU.is_equal).then_inc(made, 1)
                            at_least(dve, fetched[s], 16 * TG * (r + 1))
                            nc.vector.tensor_tensor(vy[:, :, :, :], vec, xyz.to_broadcast([P, TG, XYZ, VC]), ALU.mult).then_inc(made, 1)
                            at_least(dve, weighed, i + 1)
                            nc.vector.tensor_tensor(pw[:, :, :], w[:, :, SV:VS], rows[:, :, 0:SC], ALU.mult).then_inc(made, 1)
                            dve.wait_ge(made, done(2))
                            nc.vector.tensor_tensor(dot[:, 0, :, :], vy[:, :, 0, :], vy[:, :, 1, :], ALU.add).then_inc(made, 1)
                            at_least(dve, scaled, i + 1)
                            nc.vector.tensor_tensor(q[:, :, 0, 0:SC], w[:, :, SS:SV], gy[s0][:, :, 0:SC], ALU.mult).then_inc(made, 1)
                            dve.wait_ge(made, done(4))
                            nc.vector.tensor_tensor(dot[:, 1, :, :], dot[:, 0, :, :], vy[:, :, 2, :], ALU.add).then_inc(made, 1)
                            nc.vector.tensor_tensor(q[:, :, 1:4, 0:SC], pw[:, :, :].unsqueeze(2).to_broadcast([P, TG, XYZ, SC]),
                                                    xyz.to_broadcast([P, TG, XYZ, SC]), ALU.mult).then_inc(made, 1)
                            nc.vector.tensor_tensor(q[:, :, 1:4, SC:MID], vec0, w[:, :, VS:VV].unsqueeze(2).to_broadcast([P, TG, XYZ, VC]),
                                                    ALU.mult).then_inc(made, 1)
                            dve.wait_ge(made, done(6))
                            nc.vector.tensor_tensor(q[:, :, 0, SC:MID], w[:, :, VV:wn], dot[:, 1, :, :], ALU.mult).then_inc(made, 1)

                        def step(i, s, r):
                            if live(i, NG):
                                products(i, s, r)
                            if live(i - 2, NG):
                                add_window(dve, i - 2, win_ps[s % 2], MID, 4, summed, added)

                        steps(dve, NG, 2, step, unroll=U)

        def add_window(dve, i, bank, rows, blocks, summed, added):
            first = dve.value_load(window_row[0:1, ds(i, 1)], min_val=0, max_val=NODES)
            at = sums4[0:rows, 0:blocks, ds(first, WIN)]
            at_least(dve, added, i)
            at_least(dve, summed, i + 1)
            nc.vector.tensor_tensor(at, at, bank[0:rows, 0:blocks * WIN].rearrange("p (b n) -> p b n", b=blocks),
                                    ALU.add).then_inc(added, 1)

        def post_pass(tag, load_weights, n_loads, prepare, cols, finish, n_fin, coef_of, self_loads=False):
            c_s, c_v = cols
            with ExitStack() as ctx:
                w = sbuf(ctx, f"{tag}_post_w", [P, 1024])
                coef = sbuf(ctx, f"{tag}_post_coef", [P, 8, NT])
                sums = [sbuf(ctx, f"{tag}_post_sums{s}", [MID, 4, P]) for s in range(2)]
                own = [sbuf(ctx, f"{tag}_post_own{s}", [P, FEAT]) for s in range(2)]
                small = sbuf(ctx, f"{tag}_post_small", [P, 2])
                line = sbuf(ctx, f"{tag}_post_line", [1, NPAD if self_loads else 2])
                ps = [psum(ctx, f"{tag}_post_ps{s}", [P, 512]) for s in range(2)]
                pw = [psum(ctx, f"{tag}_post_pw{s}", [P, 512]) for s in range(2)]
                w_loaded = sem(ctx, f"{tag}_post_w_loaded")
                w_ready = sem(ctx, f"{tag}_post_w_ready")
                prep = sem(ctx, f"{tag}_post_prep")
                prep_act = sem(ctx, f"{tag}_post_prep_act")
                prep_pe = sem(ctx, f"{tag}_post_prep_pe")
                prep_dma = sem(ctx, f"{tag}_post_prep_dma")
                copied = sem(ctx, f"{tag}_post_copied")
                mapped = sem(ctx, f"{tag}_post_mapped")
                fin = sem(ctx, f"{tag}_post_fin")
                own_loaded = [sem(ctx, f"{tag}_post_own_loaded{s}") for s in range(2)]
                B = dict(w=w, coef=coef, small=small, line=line, ps=ps, pw=pw, w_loaded=w_loaded, w_ready=w_ready, prep=prep,
                         prep_act=prep_act, prep_pe=prep_pe, prep_dma=prep_dma, n_loads=n_loads, fin=fin)

                with nc.Block() as block:

                    @block.sync
                    def _(sp):
                        load_weights(sp, B)
                        if "sp" in prepare:
                            prepare["sp"](sp, B)
                        if self_loads:
                            def step(i, s, r):
                                at_least(sp, fin, (i - 1) * n_fin)
                                sp.dma_start(own[s][:, :], self_rows[ds(i * P, P), :]).then_inc(own_loaded[s], 16)

                            steps(sp, NT, 0, step)

                    @block.scalar
                    def _(act):
                        if "act" in prepare:
                            prepare["act"](act, B)

                        def step(i, s, r):
                            at_least(act, mapped, i - 1)
                            nc.scalar.activation(sums[s][:, :, :], sums4[0:MID, :, ds(i * P, P)], ACT.Copy).then_inc(copied, 1)

                        steps(act, NT, 0, step)

                    @block.tensor
                    def _(pe):
                        if "pe" in prepare:
                            prepare["pe"](pe, B)
                        pe.wait_ge(w_ready, 1)

                        def step(i, s, r):
                            at_least(pe, copied, i + 1)
                            at_least(pe, fin, (i - 1) * n_fin)
                            nc.tensor.matmul(ps[s][:, 0:c_s], sums[s][:, 0, :], w[0:MID, 0:c_s])
                            for c in range(XYZ):
                                ins = nc.tensor.matmul(ps[s][:, c_s + c * c_v:c_s + (c + 1) * c_v], sums[s][:, 1 + c, :],
                                                       w[0:MID, c_s:c_s + c_v])
                            ins.then_inc(mapped, 1)

                        steps(pe, NT, 0, step)

                    @block.vector
                    def _(dve):
                        prepare["dve"](dve, B)

                        def step(i, s, r):
                            at_least(dve, mapped, i + 1)
                            at_least(dve, fin, i * n_fin)
                            if self_loads:
                                at_least(dve, own_loaded[s], 16 * (r + 1))
                            finish(dve, i, ps[s], own[s], coef, small, fin, i * n_fin)

                        steps(dve, NT, 0, step)

        def vectors_of(ps, at, width, col, n):
            return ps[:, at:at + XYZ * width].rearrange("p (c w) -> p c w", c=XYZ)[:, :, col:col + n]

        def post_l0():
            k = (SC ** -0.5) * (32.0 ** -0.5) * (MID ** -0.5)
            cs = SC + 1

            def load(sp, B):
                sp.dma_start(B["w"][0:MID, 0:SC], A["L0_gnn_Wl2_s"]).then_inc(B["w_loaded"], 16)
                sp.dma_start(B["w"][0:MID, SC:cs], A["L0_gnn_Wa"]).then_inc(B["w_loaded"], 16)
                sp.dma_start(B["w"][0:MID, cs:cs + VC], A["L0_gnn_Wl2_v"]).then_inc(B["w_loaded"], 16)

            def prep(dve, B):
                nc.vector.tensor_scalar(B["coef"][:, 1, :], attr[:, 0, :], k, None, ALU.mult).then_inc(B["prep"], 1)
                dve.wait_ge(B["prep"], 1)
                nc.vector.tensor_tensor(B["coef"][:, 0, :], B["coef"][:, 1, :], B["coef"][:, 1, :], ALU.mult).then_inc(B["prep"], 1)
                dve.wait_ge(B["w_loaded"], 48)
                nc.vector.tensor_scalar(B["w"][0:MID, 0:cs], B["w"][0:MID, 0:cs], row_scale[0:MID, 0:1], None, ALU.mult).then_inc(B["w_ready"], 1)
                dve.wait_ge(B["prep"], 2)

            def finish(dve, t, ps, own, coef, small, fin, k0):
                nc.vector.tensor_scalar(small[:, 0:1], ps[:, SC:cs], coef[:, 0, ds(t, 1)], None, ALU.mult).then_inc(fin, 1)
                dve.wait_ge(fin, k0 + 1)
                nc.vector.scalar_tensor_tensor(xs_at(t), ps[:, 0:SC], small[:, 0:1], xs_at(t), ALU.mult, ALU.add).then_inc(fin, 1)
                nc.vector.scalar_tensor_tensor(xv_at(t), vectors_of(ps, cs, VC, 0, VC), small[:, 0:1], xv_at(t),
                                               ALU.mult, ALU.add).then_inc(fin, 1)

            post_pass("l0", load, 3, {"dve": prep}, (cs, VC), finish, 3, None)

        def post_l1():
            k = (SC ** -0.5) * (10.0 ** -0.5) * (MID ** -0.5)
            ROUND = 1.5 * 2.0 ** 23
            pieces = [(n, min(512, NPAD - n)) for n in range(0, NPAD, 512)]

            def load(sp, B):
                sp.dma_start(B["w"][0:MID, 0:SC], A["L1_gnn_W2_s"]).then_inc(B["w_loaded"], 16)
                sp.dma_start(B["w"][0:MID, SC:MID], A["L1_gnn_W2_v"]).then_inc(B["w_loaded"], 16)
                sp.dma_start(B["w"][0:MID, 512:513], A["L1_gnn_W3"]).then_inc(B["w_loaded"], 16)

            def prep_pe(pe, B):
                pe.wait_ge(B["w_ready"], 1)
                for n, (at, width) in enumerate(pieces):
                    at_least(pe, B["prep_act"], n - 1)
                    nc.tensor.matmul(B["pw"][n % 2][0:1, 0:width], B["w"][0:MID, 512:513], sums4[0:MID, 0, at:at + width]
                                     ).then_inc(B["prep_pe"], 1)

            def prep_act(act, B):
                for n, (at, width) in enumerate(pieces):
                    act.wait_ge(B["prep_pe"], n + 1)
                    nc.scalar.activation(B["line"][0:1, at:at + width], B["pw"][n % 2][0:1, 0:width], ACT.Copy).then_inc(B["prep_act"], 1)
                act.wait_ge(B["prep"], 6)
                nc.scalar.activation(B["coef"][:, 5:7, :], B["coef"][:, 3:5, :], ACT.Sin, scale=6.2831850).then_inc(B["prep_act"], 1)

            def prep_sp(sp, B):
                sp.wait_ge(B["prep_act"], len(pieces))
                sp.dma_start(turn_row, B["line"][0:1, :]).then_inc(B["prep_dma"], 16)
                sp.wait_ge(B["prep_dma"], 16)
                with nc.allow_non_contiguous_dma(reason="a row of node values onto partitions, once"):
                    sp.dma_start(B["coef"][:, 0, :], turn_row[0, :].rearrange("(t p) -> p t", p=P)).then_inc(B["prep_dma"], 16)

            def prep(dve, B):
                c, prep = B["coef"], B["prep"]
                dve.wait_ge(B["w_loaded"], 48)
                nc.vector.tensor_scalar(B["w"][0:MID, 512:513], B["w"][0:MID, 512:513], row_scale[0:MID, 0:1], None, ALU.mult).then_inc(B["w_ready"], 0 + 1)
                nc.vector.tensor_scalar(B["w"][0:MID, 0:SC], B["w"][0:MID, 0:SC], row_scale[0:MID, 0:1], None, ALU.mult).then_inc(B["w_ready"], 1)
                nc.vector.tensor_scalar(c[:, 7, :], attr[:, 0, :], k, None, ALU.mult).then_inc(prep, 1)
                dve.wait_ge(B["prep_dma"], 32)
                dve.wait_ge(prep, 1)
                nc.vector.scalar_tensor_tensor(c[:, 1, :], c[:, 0, :], 0.1 / 6.283185307179586, c[:, 7, :], ALU.mult, ALU.mult).then_inc(prep, 1)
                dve.wait_ge(prep, 2)
                nc.vector.tensor_scalar(c[:, 2, :], c[:, 1, :], 0.25, None, ALU.add).then_inc(prep, 1)
                dve.wait_ge(prep, 3)
                nc.vector.tensor_scalar(c[:, 5:7, :], c[:, 1:3, :], ROUND, None, ALU.add).then_inc(prep, 1)
                dve.wait_ge(prep, 4)
                nc.vector.tensor_scalar(c[:, 3:5, :], c[:, 5:7, :], ROUND, None, ALU.subtract).then_inc(prep, 1)
                dve.wait_ge(prep, 5)
                nc.vector.tensor_tensor(c[:, 3:5, :], c[:, 1:3, :], c[:, 3:5, :], ALU.subtract).then_inc(prep, 1)
                dve.wait_ge(B["prep_act"], len(pieces) + 1)
                nc.vector.tensor_tensor(c[:, 0, :], c[:, 5, :], c[:, 7, :], ALU.mult).then_inc(prep, 1)
                dve.wait_ge(prep, 7)

            def finish(dve, t, ps, own, coef, small, fin, k0):
                sin, cos = coef[:, 0, ds(t, 1)], coef[:, 6, ds(t, 1)]
                nc.vector.scalar_tensor_tensor(xs_at(t), ps[:, 0:SC], sin, xs_at(t), ALU.mult, ALU.add).then_inc(fin, 1)
                nc.vector.scalar_tensor_tensor(xv_at(t), vectors_of(ps, SC, VC, 0, VC), sin, xv_at(t), ALU.mult, ALU.add).then_inc(fin, 1)
                dve.wait_ge(fin, k0 + 2)
                nc.vector.scalar_tensor_tensor(xs_at(t), own[:, 0:SC], cos, xs_at(t), ALU.mult, ALU.add).then_inc(fin, 1)
                nc.vector.scalar_tensor_tensor(xv_at(t), by_component(own[:, SC:FEAT]), cos, xv_at(t), ALU.mult, ALU.add).then_inc(fin, 1)

            post_pass("l1", load, 3, {"dve": prep, "pe": prep_pe, "act": prep_act, "sp": prep_sp}, (SC, VC), finish, 4, None,
                      self_loads=True)

        def post_l3():
            import math
            k = math.cos(math.pi / 8) / math.sqrt(16.0)
            T = {"L3_gnn_Ws_l2_a": 192, "L3_gnn_Ws_l2_c": 288, "L3_gnn_Wv_l2_a": 384, "L3_gnn_Wv_l2_c": 480}
            L = {"L3_gnn_Ws_l3": (576, SC), "L3_gnn_Wv_l3": (640, VC)}
            outs = [("L3_gnn_Ws_l2_a", "L3_gnn_Ws_l3", 0), ("L3_gnn_Ws_l2_c", "L3_gnn_Ws_l3", SC),
                    ("L3_gnn_Wv_l2_a", "L3_gnn_Wv_l3", 2 * SC), ("L3_gnn_Wv_l2_c", "L3_gnn_Wv_l3", 2 * SC + VC)]

            def load(sp, B):
                for n, at in T.items():
                    sp.dma_start(B["w"][0:MID, at:at + MID], A[n + "_T"]).then_inc(B["w_loaded"], 16)
                for n, (at, width) in L.items():
                    sp.dma_start(B["w"][0:MID, at:at + width], A[n]).then_inc(B["w_loaded"], 16)

            def prep_pe(pe, B):
                pe.wait_ge(B["w_loaded"], 16 * 6)
                for l2, l3, at in outs:
                    src, width = L[l3]
                    ins = nc.tensor.matmul(B["pw"][0][0:MID, at:at + width], B["w"][0:MID, T[l2]:T[l2] + MID], B["w"][0:MID, src:src + width])
                ins.then_inc(B["prep_pe"], 1)

            def prep(dve, B):
                c, prep = B["coef"], B["prep"]
                for n in range(2):
                    nc.vector.scalar_tensor_tensor(c[:, n, :], attr[:, n, :], k, attr[:, 2, :], ALU.mult, ALU.mult).then_inc(prep, 1)
                dve.wait_ge(B["prep_pe"], 1)
                nc.vector.tensor_copy(B["w"][0:MID, 2 * SC:192], B["pw"][0][0:MID, 2 * SC:192]).then_inc(prep, 1)
                dve.wait_ge(prep, 3)
                nc.vector.tensor_scalar(B["w"][0:MID, 0:2 * SC], B["pw"][0][0:MID, 0:2 * SC], row_scale[0:MID, 0:1], None,
                                        ALU.mult).then_inc(B["w_ready"], 1)

            def finish(dve, t, ps, own, coef, small, fin, k0):
                for n in range(2):
                    f = coef[:, n, ds(t, 1)]
                    if n:
                        dve.wait_ge(fin, k0 + 2)
                    nc.vector.scalar_tensor_tensor(xs_at(t), ps[:, n * SC:(n + 1) * SC], f, xs_at(t), ALU.mult, ALU.add).then_inc(fin, 1)
                    nc.vector.scalar_tensor_tensor(xv_at(t), vectors_of(ps, 2 * SC, 2 * VC, n * VC, VC), f, xv_at(t),
                                                   ALU.mult, ALU.add).then_inc(fin, 1)

            post_pass("l3", load, 6, {"dve": prep, "pe": prep_pe}, (2 * SC, 2 * VC), finish, 4, None)

        def attention_pass():
            FW = MID + SC + XYZ * 2 * VC
            PARTS = [(0, MID), (MID, P), (MID + P, P)]
            WW = 2 * SC + 3 * VC
            VS, VV0, VV1 = 2 * SC, 2 * SC + VC, 2 * SC + 2 * VC
            GATE, Q, PV = SC, SC + VC, SC + 2 * VC
            Q2, PV2 = SC, SC + VC
            O1W, O2W = SC + 2 * VC + VF, SC + VC + VF
            K1, K2, K3 = 16, 13, 4
            with ExitStack() as ctx:
                def pair(name, shape, dt=F32):
                    return [sbuf(ctx, f"att_{name}{s}", shape, dt) for s in range(2)]

                w_rbf = sbuf(ctx, "att_w_rbf", [16, WW])
                w_att = sbuf(ctx, "att_w_att", [MID, SC])
                w_dot = sbuf(ctx, "att_w_dot", [SC, 3 * HEADS])
                w_lin = sbuf(ctx, "att_w_lin", [MID, HEADS])
                w_alpha_T = sbuf(ctx, "att_w_alpha_T", [SC, MID])
                w_val_T = sbuf(ctx, "att_w_val_T", [SC, MID])
                w_gate = sbuf(ctx, "att_w_gate", [SC, VC])
                w_o1s = sbuf(ctx, "att_w_o1s", [MID, MID])
                w_o1v = [sbuf(ctx, f"att_w_o1v{n}", [P, 2 * VC]) for n in range(2)]
                w_o2s = sbuf(ctx, "att_w_o2s", [MID, SC])
                w_o2v = [sbuf(ctx, f"att_w_o2v{n}", [P, 2 * VC]) for n in range(2)]
                w2 = sbuf(ctx, "att_w2", [P, 3])
                ends = pair("ends", [P, 2 * TG], I32)
                ea = pair("ea", [16, GE])
                y_all = sums_T[:, 0:NG * TG * YC]
                g_src = pair("g_src", [P, TG, FEAT])
                g_dst = pair("g_dst", [P, TG, FEAT])
                at = NG * TG * YC
                feat = [sums_T[:, at + n * TG * FW:at + (n + 1) * TG * FW].rearrange("p (t f) -> p t f", t=TG) for n in range(2)]
                at += 2 * TG * FW
                feat_T = [sums_T[:, at + n * 3 * GE:at + (n + 1) * 3 * GE].rearrange("p (k e) -> p k e", k=3) for n in range(2)]
                act_T = sbuf(ctx, "att_act_T", [SC, GE])
                score = pair("score", [HEADS, GE])
                gate_s = sbuf(ctx, "att_gate", [P, TG, VC])
                msg = sbuf(ctx, "att_msg", [P, TG, FEAT])
                vec2 = [sbuf(ctx, f"att_vec2{n}", [P, TG, XYZ, VC]) for n in range(3)]
                vy = sbuf(ctx, "att_vy", [P, TG, XYZ, VC])
                p1 = sbuf(ctx, "att_p1", [P, TG, XYZ, VC])
                p2 = sbuf(ctx, "att_p2", [P, TG, XYZ, VC])
                vsv = sbuf(ctx, "att_vsv", [P, TG, XYZ, VC])
                tmp = sbuf(ctx, "att_tmp", [P, TG, SC])
                dot = sbuf(ctx, "att_dot", [P, TG, VC])
                qy = sbuf(ctx, "att_qy", [P, TG, XYZ, VC])
                rows = pair("rows", [P, TG, HEADS, HF])
                w_ps = psum(ctx, "att_w_ps", [P, TG, 256])
                o1 = psum(ctx, "att_o1", [P, TG, 256])
                o2 = psum(ctx, "att_o2", [P, TG, 256])
                turn = [psum(ctx, f"att_turn{n}", [P, GE]) for n in range(2)]

                w_zeroed = sem(ctx, "att_w_zeroed")
                w_loaded = sem(ctx, "att_w_loaded")
                w_made = sem(ctx, "att_w_made")
                w_prod = sem(ctx, "att_w_prod")
                ends_loaded = [sem(ctx, f"att_ends_loaded{s}") for s in range(2)]
                ea_loaded = [sem(ctx, f"att_ea_loaded{s}") for s in range(2)]
                y_loaded = sem(ctx, "att_y_loaded")
                fetched = [sem(ctx, f"att_fetched{s}") for s in range(2)]
                stored = [sem(ctx, f"att_stored{s}") for s in range(2)]
                scores_stored = [sem(ctx, f"att_scores_stored{s}") for s in range(2)]
                weighed = sem(ctx, "att_weighed")
                made1 = sem(ctx, "att_made1")
                made2 = sem(ctx, "att_made2")
                made3 = sem(ctx, "att_made3")
                turned1 = sem(ctx, "att_turned1")
                read1 = sem(ctx, "att_read1")
                turned2 = sem(ctx, "att_turned2")
                read2 = sem(ctx, "att_read2")
                mapped1 = sem(ctx, "att_mapped1")
                mapped2 = sem(ctx, "att_mapped2")
                gated = sem(ctx, "att_gated")
                values_out = sem(ctx, "att_values_out")
                N_LOAD = 28

                with nc.Block() as block:

                    @block.sync
                    def _(sp):
                        def put(dst, name, rows=None):
                            a = A["L2_gnn_" + name]
                            sp.dma_start(dst, a if rows is None else a[rows[0]:rows[1], :]).then_inc(w_loaded, 16)

                        sp.dma_start(y_all, A["y_all"]).then_inc(y_loaded, 16)
                        put(w_rbf[:, :], "W_rbf")
                        put(w_att[:, :], "W_alpha")
                        put(w_alpha_T[:, :], "W_alpha_T")
                        put(w_val_T[:, :], "Ws_val_T")
                        put(w_gate[:, :], "Wg")
                        put(w_o1s[:, 0:SC], "Ws_val")
                        put(w_o2s[:, :], "Ws_vlin")
                        sp.wait_ge(w_zeroed, 5)
                        for h in range(HEADS):
                            put(w_dot[h * HS:(h + 1) * HS, h:h + 1], "alpha_dot", (h * HS, (h + 1) * HS))
                        for w, name in ((w_o1v, "Wv_val"), (w_o2v, "Wv_vlin")):
                            put(w[0][0:SC, 0:VC], name, (0, SC))
                            put(w[0][SC:P, VC:2 * VC], name, (SC, P))
                            put(w[1][0:SC, 0:VC], name, (SC, P))
                            put(w[1][SC:P, VC:2 * VC], name, (SC, P))
                        put(w2[0:SC, 0:1], "w2_ss")
                        put(w2[SC:MID, 0:1], "w2_vv0")
                        put(w2[0:SC, 1:2], "w2_sv")
                        put(w2[SC:MID, 1:2], "w2_vs")
                        put(w2[MID:P, 1:2], "w2_vv1")
                        for n in range(2):
                            put(w2[n * SC:n * SC + VC, 2:3], "w2_vs")
                            put(w2[n * SC + VC:(n + 1) * SC, 2:3], "w2_vv1")

                        def load(i, s, r):
                            at_least(sp, fetched[s], 32 * TG * r)
                            sp.dma_start(ends[s][:, 0:TG], A["src_groups"][ds(i * P, P), :]).then_inc(ends_loaded[s], 16)
                            sp.dma_start(ends[s][:, TG:2 * TG], A["dst_groups"][ds(i * P, P), :]).then_inc(ends_loaded[s], 16)
                            at_least(sp, weighed, i - 1)
                            sp.dma_start(ea[s][:, :], A["edge_attr_16_T"][:, ds(i * GE, GE)]).then_inc(ea_loaded[s], 16)

                        def step(i, s, r):
                            if live(i, NG):
                                load(i, s, r)
                            if live(i - 3, NG):
                                s1, _ = back(s, r, 3)
                                at_least(sp, read1, (i - 3) * 5 + 5)
                                sp.dma_start(scores_T[:, ds((i - 3) * GE, GE)], score[s1][:, :]).then_inc(scores_stored[s1], 16)
                                gate(sp, (w_zeroed, 5),
                                     (made3, (i - 2) * K3),
                                     (values_out, i - 2))
                                sp.dma_start(messages[ds((i - 3) * GE, GE), :].rearrange("(t p) f -> p t f", p=P),
                                             rows[s1][:, :, :, :].rearrange("p t h f -> p t (h f)")).then_inc(stored[s1], 16)

                        steps(sp, NG, 3, step)
                        for s in range(2):
                            sp.wait_ge(stored[s], 16 * NG // 2)
                            sp.wait_ge(scores_stored[s], 16 * NG // 2)

                    @block.gpsimd
                    def _(pool):
                        def step(i, s, r):
                            gate(pool, (w_loaded, 16 * N_LOAD),
                                 (ends_loaded[s], 32 * (r + 1)),
                                 (made1, (i - 2) * K1 + 1))
                            for t in range(TG):
                                for rows_of, g, at in ((table[2], g_src, t), (table[3], g_dst, TG + t)):
                                    pool.indirect_dma_start(g[s][:, t, :], None, rows_of,
                                                            bass.IndirectOffsetOnAxis(ends[s][:, at:at + 1], 0)).then_inc(fetched[s], 16)

                        steps(pool, NG, 0, step)

                    @block.tensor
                    def _(pe):
                        def weigh(i, s, r):
                            at_least(pe, made1, i * K1)
                            at_least(pe, ea_loaded[s], 16 * (r + 1))
                            for t in range(TG):
                                ins = nc.tensor.matmul(w_ps[:, t, 0:WW], ea[s][:, t * P:(t + 1) * P], w_rbf[:, :])
                            ins.then_inc(weighed, 1)

                        def transpose(n, part, bank):
                            at, width = PARTS[part]
                            for t in range(TG):
                                ins = nc.tensor.transpose(turn[bank][0:width, t * P:(t + 1) * P], feat[n][:, t, at:at + width], ident[:, :])
                            return ins

                        pe.wait_ge(w_loaded, 16 * N_LOAD)
                        pe.wait_ge(w_zeroed, 7)
                        nc.tensor.matmul(turn[0][0:MID, 0:HEADS], w_alpha_T[:, :], w_dot[:, HEADS:2 * HEADS])
                        nc.tensor.matmul(turn[0][0:MID, HEADS:HEADS + VC], w_val_T[:, :], w_gate[:, :]).then_inc(w_prod, 1)
                        pe.wait_ge(w_made, 9)
                        weigh(0, 0, 0)

                        def step(i, s, r):
                            if live(i, NG):
                                at_least(pe, made1, (i + 1) * K1)
                                at_least(pe, read1, i * 5)
                                at_least(pe, read2, (i - 1) * 3)
                                transpose(0, 0, 0).then_inc(turned1, 1)
                                transpose(0, 1, 1).then_inc(turned1, 1)
                                if live(i + 1, NG):
                                    s1, r1 = (s + 1) % 2, r + (s + 1) // 2
                                    weigh(i + 1, s1, r1)
                                at_least(pe, read1, i * 5 + 1)
                                transpose(0, 2, 0).then_inc(turned1, 1)
                                at_least(pe, read1, i * 5 + 2)
                                nc.tensor.matmul(turn[1][0:SC, :], w_att[:, :], feat_T[0][0:MID, 0, :]).then_inc(turned1, 1)
                                at_least(pe, read1, i * 5 + 3)
                                at_least(pe, made2, (i - 1) * K2 + 2)
                                at_least(pe, gated, i * 2)
                                for t in range(TG):
                                    e = slice(t * P, (t + 1) * P)
                                    nc.tensor.matmul(o1[:, t, 0:MID], feat_T[0][0:MID, 0, e], w_o1s[:, :])
                                    nc.tensor.matmul(o1[:, t, Q:PV + VC], feat_T[0][:, 1, e], w_o1v[0][:, :])
                                    ins = nc.tensor.matmul(o1[:, t, PV + VC:O1W], feat_T[0][:, 2, e], w_o1v[1][:, :])
                                ins.then_inc(mapped1, 1)
                                at_least(pe, read1, i * 5 + 4)
                                nc.tensor.matmul(turn[0][0:HEADS, :], w_lin[:, :], feat_T[0][0:MID, 0, :], start=True, stop=False)
                                nc.tensor.matmul(turn[0][0:HEADS, :], w_dot[:, 2 * HEADS:3 * HEADS], act_T[:, :], start=False, stop=True
                                                 ).then_inc(turned1, 1)
                            if live(i - 1, NG):
                                done1 = i * 5 if not live(i, NG) else i * 5 + 4
                                at_least(pe, made2, i * K2)
                                at_least(pe, read1, done1)
                                transpose(1, 0, 1).then_inc(turned2, 1)
                                at_least(pe, read1, i * 5 if not live(i, NG) else i * 5 + 5)
                                transpose(1, 1, 0).then_inc(turned2, 1)
                                at_least(pe, read2, (i - 1) * 3 + 1)
                                transpose(1, 2, 1).then_inc(turned2, 1)
                                at_least(pe, read2, i * 3)
                                at_least(pe, made3, (i - 1) * K3)
                                at_least(pe, values_out, i - 1)
                                for t in range(TG):
                                    e = slice(t * P, (t + 1) * P)
                                    nc.tensor.matmul(o2[:, t, 0:SC], feat_T[1][0:MID, 0, e], w_o2s[:, :])
                                    nc.tensor.matmul(o2[:, t, Q2:PV2 + VC], feat_T[1][:, 1, e], w_o2v[0][:, :])
                                    ins = nc.tensor.matmul(o2[:, t, PV2 + VC:O2W], feat_T[1][:, 2, e], w_o2v[1][:, :])
                                ins.then_inc(mapped2, 1)

                        steps(pe, NG - 1, 2, step)

                    @block.scalar
                    def _(act):
                        def step(i, s, r):
                            if live(i, NG):
                                at_least(act, mapped1, i)
                                at_least(act, turned1, i * 5)
                                for part, (_, width) in enumerate(PARTS):
                                    at_least(act, turned1, i * 5 + part + 1)
                                    nc.scalar.activation(feat_T[0][0:width, part, :], turn[part % 2][0:width, :], ACT.Copy).then_inc(read1, 1)
                                at_least(act, turned1, i * 5 + 4)
                                nc.scalar.activation(act_T[:, :], turn[1][0:SC, :], ACT.Relu).then_inc(read1, 1)
                                at_least(act, turned1, i * 5 + 5)
                                at_least(act, scores_stored[s], 16 * r)
                                nc.scalar.activation(score[s][:, :], turn[0][0:HEADS, :], ACT.Copy).then_inc(read1, 1)
                            if live(i - 1, NG):
                                s1, r1 = back(s, r, 1)
                                at_least(act, mapped2, i - 1)
                                for part, (_, width) in enumerate(PARTS):
                                    at_least(act, turned2, (i - 1) * 3 + part + 1)
                                    nc.scalar.activation(feat_T[1][0:width, part, :], turn[1 - part % 2][0:width, :], ACT.Copy).then_inc(read2, 1)
                            if live(i, NG):
                                at_least(act, mapped1, i + 1)
                                at_least(act, turned2, i * 3)
                                at_least(act, made2, i * K2)
                                nc.scalar.activation(feat[1][:, :, MID:MID + SC], o1[:, :, 0:SC], ACT.Sigmoid).then_inc(gated, 1)
                                nc.scalar.activation(gate_s[:, :, :], o1[:, :, GATE:Q], ACT.Sigmoid).then_inc(gated, 1)
                            if live(i - 1, NG):
                                at_least(act, mapped2, i)
                                at_least(act, stored[s1], 16 * r1)
                                nc.scalar.activation(rows[s1][:, :, :, 0:HS], o2[:, :, 0:SC].rearrange("p t (h f) -> p t h f", h=HEADS),
                                                     ACT.Copy).then_inc(values_out, 1)

                        steps(act, NG, 1, step)

                    @block.vector
                    def _(dve):
                        for a in (w_dot, *w_o1v, *w_o2v):
                            nc.vector.memset(a[:, :], 0.0).then_inc(w_zeroed, 1)
                        dve.wait_ge(w_loaded, 16 * N_LOAD)
                        nc.vector.tensor_scalar(w_dot[:, HEADS:2 * HEADS], w_dot[:, 0:HEADS], 0.2, None, ALU.mult).then_inc(w_zeroed, 1)
                        nc.vector.tensor_scalar(w_dot[:, 2 * HEADS:3 * HEADS], w_dot[:, 0:HEADS], 0.8, None, ALU.mult).then_inc(w_zeroed, 1)
                        dots = row_scale[0:MID, 0:1]
                        nc.vector.tensor_scalar(w_att[:, :], w_att[:, :], dots, None, ALU.mult).then_inc(w_made, 1)
                        dve.wait_ge(w_prod, 1)
                        nc.vector.tensor_scalar(w_lin[:, :], turn[0][0:MID, 0:HEADS], dots, None, ALU.mult).then_inc(w_made, 1)
                        nc.vector.tensor_scalar(w_o1s[:, SC:MID], turn[0][0:MID, HEADS:HEADS + VC], dots, None, ALU.mult).then_inc(w_made, 1)
                        nc.vector.tensor_scalar(w_o1s[:, 0:SC], w_o1s[:, 0:SC], dots, None, ALU.mult).then_inc(w_made, 1)
                        nc.vector.tensor_scalar(w_o2s[:, :], w_o2s[:, :], dots, w2[0:MID, 0:1], ALU.mult, ALU.mult).then_inc(w_made, 1)
                        for n in range(2):
                            cross = row_scale[:, 1 + n:2 + n]
                            nc.vector.tensor_scalar(w_o1v[n][:, :], w_o1v[n][:, :], cross, None, ALU.mult).then_inc(w_made, 1)
                            nc.vector.tensor_scalar(w_o2v[n][:, :], w_o2v[n][:, :], cross, w2[:, 1 + n:2 + n], ALU.mult, ALU.mult).then_inc(w_made, 1)

                        dve.wait_ge(y_loaded, 16)

                        def y_of(i):
                            return y_all[:, ds(i * (TG * YC), TG * YC)].rearrange("p (t c) -> p t c", c=YC)

                        def xyz(yy, lo, hi, width):
                            return yy[:, :, lo:hi].unsqueeze(3).to_broadcast([P, TG, hi - lo, width])

                        def tt(out, a, b, op, count):
                            nc.vector.tensor_tensor(out, a, b, op).then_inc(count, 1)

                        def cross_parts(v, yy, count):
                            tt(p1[:, :, 0:2, :], v[:, :, 1:3, :], xyz(yy, 3, 5, VC), ALU.mult, count)
                            tt(p1[:, :, 2:3, :], v[:, :, 0:1, :], xyz(yy, 5, 6, VC), ALU.mult, count)
                            tt(p2[:, :, 0:1, :], v[:, :, 2:3, :], xyz(yy, 2, 3, VC), ALU.mult, count)
                            tt(p2[:, :, 1:3, :], v[:, :, 0:2, :], xyz(yy, 3, 5, VC), ALU.mult, count)

                        def pairs_of(f, lo):
                            return f[:, :, MID + SC:FW].rearrange("p t (c k) -> p t c k", c=XYZ)[:, :, :, lo:lo + VC]

                        def first(i, s, r):
                            k = i * K1
                            f, yy, w = feat[0], y_of(i), w_ps
                            vec = msg[:, :, SC:FEAT].rearrange("p t (c u) -> p t c u", c=XYZ)
                            y0 = yy[:, :, 0:1]
                            at_least(dve, made1, k)
                            at_least(dve, fetched[s], 32 * TG * (r + 1))
                            tt(msg[:, :, :], g_src[s][:, :, :], g_dst[s][:, :, :], ALU.add, made1)
                            at_least(dve, weighed, i + 1)
                            at_least(dve, turned1, (i - 1) * 5 + 3)
                            dve.wait_ge(made1, k + 1)
                            tt(vy[:, :, :, :], vec, xyz(yy, 1, 4, VC), ALU.mult, made1)
                            tt(tmp[:, :, :], w[:, :, 0:SC], msg[:, :, 0:SC], ALU.mult, made1)
                            tt(f[:, :, MID:MID + SC], w[:, :, SC:2 * SC], msg[:, :, 0:SC], ALU.mult, made1)
                            tt(vsv[:, :, :, :], vec, w[:, :, VS:VV0].unsqueeze(2).to_broadcast([P, TG, XYZ, VC]), ALU.mult, made1)
                            dve.wait_ge(made1, k + 2)
                            tt(dot[:, :, :], vy[:, :, 0, :], vy[:, :, 1, :], ALU.add, made1)
                            cross_parts(vec, yy, made1)
                            dve.wait_ge(made1, k + 6)
                            tt(dot[:, :, :], dot[:, :, :], vy[:, :, 2, :], ALU.add, made1)
                            tt(f[:, :, 0:SC], tmp[:, :, :], y0.to_broadcast([P, TG, SC]), ALU.mult, made1)
                            dve.wait_ge(made1, k + 10)
                            tt(p1[:, :, :, :], p1[:, :, :, :], p2[:, :, :, :], ALU.subtract, made1)
                            tt(pairs_of(f, 0), vsv[:, :, :, :], xyz(yy, 0, 1, VC).to_broadcast([P, TG, XYZ, VC]), ALU.mult, made1)
                            dve.wait_ge(made1, k + 11)
                            tt(f[:, :, SC:MID], w[:, :, VV0:VV1], dot[:, :, :], ALU.mult, made1)
                            dve.wait_ge(made1, k + 13)
                            tt(pairs_of(f, VC), p1[:, :, :, :], w[:, :, VV1:WW].unsqueeze(2).to_broadcast([P, TG, XYZ, VC]), ALU.mult, made1)

                        def second(i, s, r):
                            k = i * K2
                            f, yy = feat[1], y_of(i)
                            y0 = yy[:, :, 0:1]
                            v = vec2[2]
                            at_least(dve, made2, k)
                            at_least(dve, gated, (i + 1) * 2)
                            tt(vec2[0][:, :, :, :], o1[:, :, Q:PV].unsqueeze(2).to_broadcast([P, TG, XYZ, VC]), xyz(yy, 1, 4, VC), ALU.mult, made2)
                            dve.wait_ge(made2, k + 1)
                            tt(vec2[1][:, :, :, :], vec2[0][:, :, :, :], o1[:, :, PV:O1W].rearrange("p t (c u) -> p t c u", c=XYZ), ALU.add, made2)
                            dve.wait_ge(made2, k + 2)
                            tt(v[:, :, :, :], vec2[1][:, :, :, :], gate_s[:, :, :].unsqueeze(2).to_broadcast([P, TG, XYZ, VC]), ALU.mult, made2)
                            at_least(dve, turned2, i * 3)
                            tt(f[:, :, 0:SC], f[:, :, MID:MID + SC], y0.to_broadcast([P, TG, SC]), ALU.mult, made2)
                            dve.wait_ge(made2, k + 3)
                            tt(vy[:, :, :, :], v[:, :, :, :], xyz(yy, 1, 4, VC), ALU.mult, made2)
                            cross_parts(v, yy, made2)
                            dve.wait_ge(made2, k + 5)
                            tt(dot[:, :, :], vy[:, :, 0, :], vy[:, :, 1, :], ALU.add, made2)
                            tt(pairs_of(f, 0), v[:, :, :, :], xyz(yy, 0, 1, VC).to_broadcast([P, TG, XYZ, VC]), ALU.mult, made2)
                            dve.wait_ge(made2, k + 10)
                            tt(pairs_of(f, VC), p1[:, :, :, :], p2[:, :, :, :], ALU.subtract, made2)
                            tt(f[:, :, SC:MID], dot[:, :, :], vy[:, :, 2, :], ALU.add, made2)

                        def message(i, s, r):
                            k = i * K3
                            yy = y_of(i)
                            at_least(dve, made3, k)
                            at_least(dve, values_out, i + 1)
                            tt(qy[:, :, :, :], o2[:, :, Q2:PV2].unsqueeze(2).to_broadcast([P, TG, XYZ, VC]), xyz(yy, 1, 4, VC), ALU.mult, made3)
                            at_least(dve, stored[s], 16 * r)
                            dve.wait_ge(made3, k + 1)
                            for c in range(XYZ):
                                lo = HS + c * HV
                                tt(rows[s][:, :, :, lo:lo + HV], qy[:, :, c, :].rearrange("p t (h a) -> p t h a", h=HEADS),
                                   o2[:, :, PV2 + c * VC:PV2 + (c + 1) * VC].rearrange("p t (h a) -> p t h a", h=HEADS), ALU.add, made3)

                        def step(i, s, r):
                            if live(i, NG):
                                first(i, s, r)
                            if live(i - 2, NG):
                                s2, r2 = back(s, r, 2)
                                message(i - 2, s2, r2)
                            if live(i - 1, NG):
                                s1, r1 = back(s, r, 1)
                                second(i - 1, s1, r1)

                        steps(dve, NG, 2, step)

        def softmax_pass():
            with ExitStack() as ctx:
                big = [sums_T[:, n * (CHUNK + 2):(n + 1) * (CHUNK + 2)] for n in range(6)]
                score, fwd, bwd = (big[n][:, 0:CHUNK] for n in (0, 2, 3))
                dst_i = big[4].bitcast(I32)
                dst_f = big[5]
                pen = big[1][:, 0:CHUNK + 1]
                ends_i = sbuf(ctx, "soft_ends_i", [HEADS, 2, CHUNKS], I32)
                ends_f = sbuf(ctx, "soft_ends_f", [HEADS, 2, CHUNKS])
                pen_c = sbuf(ctx, "soft_pen_c", [HEADS, 2, CHUNKS])
                state = sbuf(ctx, "soft_state", [HEADS, 2, CHUNKS])
                carry = sbuf(ctx, "soft_carry", [HEADS, 2, CHUNKS + 1])
                start = sbuf(ctx, "soft_start", [P, 2])
                loaded = sem(ctx, "soft_loaded")
                done = sem(ctx, "soft_done")
                moved = sem(ctx, "soft_moved")
                exped = sem(ctx, "soft_exped")
                stored = sem(ctx, "soft_stored")
                line = A["dst_line"]
                flat_in = scores_T.rearrange("h (k n) -> (h k) n", n=CHUNK)
                flat_out = exps_T.rearrange("h (k n) -> (h k) n", n=CHUNK)
                ENDS, CARRIES = [10, 13], [11, 14]

                with nc.Block() as block:

                    @block.sync
                    def _(sp):
                        with nc.allow_non_contiguous_dma(reason="the nodes at the chunks' ends, once"):
                            for h in range(HEADS):
                                src = bass.AP(line.tensor, line.offset, [[CHUNK, CHUNKS], [1, CHUNK + 2]])
                                sp.dma_start(dst_i[h * CHUNKS:(h + 1) * CHUNKS, :], src).then_inc(loaded, 16)
                                for n in range(2):
                                    ends = bass.AP(line.tensor, line.offset + (CHUNK if n else 1), [[1, 1], [CHUNK, CHUNKS]])
                                    sp.dma_start(ends_i[h:h + 1, n, :], ends).then_inc(loaded, 16)
                            sp.dma_start(score, flat_in).then_inc(loaded, 16)
                            for n, last in enumerate((fwd[:, CHUNK - 1:CHUNK], bwd[:, 0:1])):
                                sp.wait_ge(done, ENDS[n])
                                sp.dma_start(chunk_ends[n, :].unsqueeze(1), last).then_inc(moved, 16)
                                sp.wait_ge(moved, 64 * n + 16)
                                sp.dma_start(state[:, n, :], chunk_ends[n, :].rearrange("(h k) -> h k", h=HEADS)).then_inc(moved, 16)
                                sp.wait_ge(done, CARRIES[n])
                                sp.dma_start(chunk_carries[n, :].rearrange("(h k) -> h k", h=HEADS), carry[:, n, n:n + CHUNKS]).then_inc(moved, 16)
                                sp.wait_ge(moved, 64 * n + 48)
                                sp.dma_start(start[:, n:n + 1], chunk_carries[n, :].unsqueeze(1)).then_inc(moved, 16)
                        sp.wait_ge(exped, 1)
                        sp.dma_start(flat_out, score).then_inc(stored, 16)
                        sp.wait_ge(stored, 16)

                    @block.vector
                    def _(dve):
                        count = [0]

                        def then(ins):
                            count[0] += 1
                            ins.then_inc(done, 1)
                            dve.wait_ge(done, count[0])

                        def scan(out, p, v, initial):
                            return nc.vector.tensor_tensor_scan(out, p, v, initial, ALU.add, ALU.max)

                        dve.wait_ge(loaded, 16 * (3 * HEADS + 1))
                        then(nc.vector.tensor_copy(dst_f, dst_i))
                        then(nc.vector.tensor_copy(ends_f[:, :, :], ends_i[:, :, :]))
                        then(nc.vector.tensor_tensor(pen, dst_f[:, 1:CHUNK + 2], dst_f[:, 0:CHUNK + 1], ALU.not_equal))
                        then(nc.vector.tensor_scalar(pen, pen, LOWEST, None, ALU.mult))
                        then(nc.vector.memset(carry[:, :, :], LOWEST))
                        then(nc.vector.memset(pen_c[:, :, :], 0.0))
                        then(nc.vector.tensor_tensor(pen_c[:, 0, 1:CHUNKS], ends_f[:, 1, 0:CHUNKS - 1], ends_f[:, 1, 1:CHUNKS], ALU.not_equal))
                        then(nc.vector.tensor_tensor(pen_c[:, 1, 0:CHUNKS - 1], ends_f[:, 0, 0:CHUNKS - 1], ends_f[:, 0, 1:CHUNKS], ALU.not_equal))
                        then(nc.vector.tensor_scalar(pen_c[:, :, :], pen_c[:, :, :], LOWEST, None, ALU.mult))
                        then(scan(fwd, pen[:, 0:CHUNK], score, LOWEST))
                        dve.wait_ge(moved, 32)
                        then(scan(carry[:, 0, 1:CHUNKS + 1], pen_c[:, 0, :], state[:, 0, :], LOWEST))
                        dve.wait_ge(moved, 64)
                        then(scan(fwd, pen[:, 0:CHUNK], score, start[:, 0:1]))
                        back_pen, back_fwd, back_out = pen[:, 1:CHUNK + 1][:, ::-1], fwd[:, ::-1], bwd[:, ::-1]
                        then(scan(back_out, back_pen, back_fwd, LOWEST))
                        dve.wait_ge(moved, 96)
                        then(scan(carry[:, 1, 0:CHUNKS][:, ::-1], pen_c[:, 1, :][:, ::-1], state[:, 1, :][:, ::-1], LOWEST))
                        dve.wait_ge(moved, 128)
                        then(scan(back_out, back_pen, back_fwd, start[:, 1:2]))
                        then(nc.vector.tensor_tensor(score, score, bwd, ALU.subtract))

                    @block.scalar
                    def _(act):
                        act.wait_ge(done, 16)
                        nc.scalar.activation(score, score, ACT.Exp).then_inc(exped, 1)

        def gather_messages():
            BW = 2 * HF + HEADS
            K = 3
            with ExitStack() as ctx:
                msg = [sbuf(ctx, f"sum_msg{s}", [P, TG, FEAT]) for s in range(2)]
                ex = [sbuf(ctx, f"sum_ex{s}", [HEADS, GE]) for s in range(2)]
                prod = [sbuf(ctx, f"sum_prod{s}", [P, TG, 2, BW]) for s in range(2)]
                hot = [sbuf(ctx, f"sum_hot{s}", [P, TG, WIN]) for s in range(2)]
                ex_ps = [psum(ctx, f"sum_ex_ps{s}", [P, 512]) for s in range(2)]
                win_ps = [psum(ctx, f"sum_win_ps{s}", [P, 512]) for s in range(2)]
                zeroed = sem(ctx, "sum_zeroed")
                msg_loaded = [sem(ctx, f"sum_msg_loaded{s}") for s in range(2)]
                ex_loaded = [sem(ctx, f"sum_ex_loaded{s}") for s in range(2)]
                turned = sem(ctx, "sum_turned")
                made = sem(ctx, "sum_made")
                summed = sem(ctx, "sum_summed")
                added = sem(ctx, "sum_added")

                with nc.Block() as block:

                    @block.sync
                    def _(sp):
                        def step(i, s, r):
                            at_least(sp, made, (i - 1) * K)
                            sp.dma_start(msg[s][:, :, :], messages[ds(i * GE, GE), :].rearrange("(t p) f -> p t f", p=P)
                                         ).then_inc(msg_loaded[s], 16)
                            sp.dma_start(ex[s][:, :], exps_T[:, ds(i * GE, GE)]).then_inc(ex_loaded[s], 16)

                        steps(sp, NG, 0, step)

                    @block.gpsimd
                    def _(pool):
                        for b in range(2):
                            nc.gpsimd.memset(sums_T[:, b * COLS:(b + 1) * COLS], 0.0).then_inc(zeroed, 1)

                    @block.tensor
                    def _(pe):
                        pe.wait_ge(zeroed, 1)

                        def step(i, s, r):
                            if live(i, NG):
                                gate(pe, (zeroed, 1),
                                     (ex_loaded[s], 16 * (r + 1)),
                                     (made, (i - 1) * K))
                                for t in range(TG):
                                    ins = nc.tensor.matmul(ex_ps[s][:, t * HEADS:(t + 1) * HEADS], ex[s][:, t * P:(t + 1) * P],
                                                           ident[0:HEADS, 0:HEADS])
                                ins.then_inc(turned, 1)
                            if live(i - 1, NG):
                                s1, _ = back(s, r, 1)
                                at_least(pe, made, i * K)
                                at_least(pe, added, i - 2)
                                for b in range(2):
                                    for t in range(TG):
                                        ins = nc.tensor.matmul(win_ps[s1][0:BW, b * WIN:(b + 1) * WIN], prod[s1][:, t, b, :],
                                                               hot[s1][:, t, :], start=t == 0, stop=t == TG - 1)
                                ins.then_inc(summed, 1)

                        steps(pe, NG, 1, step)

                    @block.vector
                    def _(dve):
                        dve.wait_ge(zeroed, 2)

                        def products(i, s, r):
                            at_least(dve, made, i * K)
                            at_least(dve, summed, i - 1)
                            nc.vector.tensor_tensor(hot[s][:, :, :], iota_win[:, :].unsqueeze(1).to_broadcast([P, TG, WIN]),
                                                    dst_rel[:, ds(i * TG, TG)].unsqueeze(2).to_broadcast([P, TG, WIN]),
                                                    ALU.is_equal).then_inc(made, 1)
                            at_least(dve, turned, i + 1)
                            at_least(dve, msg_loaded[s], 16 * (r + 1))
                            e = ex_ps[s][:, 0:TG * HEADS].rearrange("p (k h) -> p k h", h=2)
                            nc.vector.tensor_tensor(prod[s][:, :, :, 0:2 * HF].rearrange("p t b (h f) -> p (t b) h f", h=2),
                                                    msg[s][:, :, :].rearrange("p t (b h f) -> p (t b) h f", b=2, h=2),
                                                    e.unsqueeze(3).to_broadcast([P, 2 * TG, 2, HF]), ALU.mult).then_inc(made, 1)
                            e = ex_ps[s][:, 0:TG * HEADS].rearrange("p (t h) -> p t h", h=HEADS)
                            nc.vector.tensor_copy(prod[s][:, :, :, 2 * HF:BW], e.unsqueeze(2).to_broadcast([P, TG, 2, HEADS])).then_inc(made, 1)

                        def step(i, s, r):
                            if live(i, NG):
                                products(i, s, r)
                            if live(i - 2, NG):
                                add_window(dve, i - 2, win_ps[s], BW, 2, summed, added)

                        steps(dve, NG, 2, step)

        def post_l2():
            BW, HB = 2 * HF + HEADS, 2 * HF
            N_LOAD = 2 * 2 * (1 + XYZ)
            n_fin = 5
            with ExitStack() as ctx:
                w = sbuf(ctx, "l2_post_w", [HB, 2, FEAT])
                head_i = sbuf(ctx, "l2_post_head_i", [BW, 2, HB], I32)
                head = sbuf(ctx, "l2_post_head", [BW, 2, HB])
                inv = [sbuf(ctx, f"l2_post_inv{s}", [HB, 2, P]) for s in range(2)]
                sums = [sbuf(ctx, f"l2_post_sums{s}", [HB, 2, P]) for s in range(2)]
                den_ps = [psum(ctx, f"l2_post_den{s}", [P, 512]) for s in range(2)]
                ps = [psum(ctx, f"l2_post_ps{s}", [P, 512]) for s in range(2)]
                zeroed = sem(ctx, "l2_post_zeroed")
                w_loaded = sem(ctx, "l2_post_w_loaded")
                heads_ready = sem(ctx, "l2_post_heads_ready")
                spread = sem(ctx, "l2_post_spread")
                mapped = sem(ctx, "l2_post_mapped")
                fin = sem(ctx, "l2_post_fin")

                with nc.Block() as block:

                    @block.sync
                    def _(sp):
                        sp.wait_ge(zeroed, 3)
                        for b in range(2):
                            for k in range(2):
                                h, at = 2 * b + k, k * HF
                                sp.dma_start(w[at:at + HS, b, 0:SC], A["L2_gnn_Wps"][h * HS:(h + 1) * HS, :]).then_inc(w_loaded, 16)
                                for c in range(XYZ):
                                    lo = at + HS + c * HV
                                    sp.dma_start(w[lo:lo + HV, b, SC + c * VC:SC + (c + 1) * VC],
                                                 A["L2_gnn_Wpv"][h * HV:(h + 1) * HV, :]).then_inc(w_loaded, 16)

                    @block.gpsimd
                    def _(pool):
                        for b in range(2):
                            nc.gpsimd.iota(head_i[:, b, :].rearrange("p (h f) -> p h f", h=2), pattern=[[-1, 2], [0, HF]],
                                           base=-HB - 2 * b, channel_multiplier=1).then_inc(zeroed, 1)

                    @block.tensor
                    def _(pe):
                        pe.wait_ge(heads_ready, 1)
                        pe.wait_ge(w_loaded, 16 * N_LOAD)

                        def step(i, s, r):
                            if live(i, NT):
                                gate(pe, (heads_ready, 1), (fin, (i - 1) * n_fin))
                                for b in range(2):
                                    ins = nc.tensor.matmul(den_ps[s][0:HB, b * P:(b + 1) * P], head[:, b, :], sums4[0:BW, b, ds(i * P, P)])
                                ins.then_inc(spread, 1)
                            if live(i - 1, NT):
                                s1, _ = back(s, r, 1)
                                at_least(pe, fin, (i - 1) * n_fin + 3)
                                for b in range(2):
                                    ins = nc.tensor.matmul(ps[s1][:, 0:FEAT], sums[s1][:, b, :], w[:, b, :], start=b == 0, stop=b == 1)
                                ins.then_inc(mapped, 1)

                        steps(pe, NT, 1, step)

                    @block.vector
                    def _(dve):
                        dve.wait_ge(zeroed, 2)
                        nc.vector.memset(w[:, :, :], 0.0).then_inc(zeroed, 1)
                        nc.vector.tensor_scalar(head[:, :, :], head_i[:, :, :], 0.0, None, ALU.is_equal).then_inc(heads_ready, 1)

                        def step(i, s, r):
                            k = i * n_fin
                            at_least(dve, fin, k)
                            at_least(dve, spread, i + 1)
                            nc.vector.tensor_scalar(inv[s][:, :, :], den_ps[s][0:HB, 0:2 * P].rearrange("p (b n) -> p b n", b=2),
                                                    1e-16, None, ALU.add).then_inc(fin, 1)
                            dve.wait_ge(fin, k + 1)
                            nc.vector.reciprocal(inv[s][:, :, :], inv[s][:, :, :]).then_inc(fin, 1)
                            dve.wait_ge(fin, k + 2)
                            nc.vector.tensor_tensor(sums[s][:, :, :], sums4[0:HB, 0:2, ds(i * P, P)], inv[s][:, :, :], ALU.mult).then_inc(fin, 1)
                            at_least(dve, mapped, i + 1)
                            nc.vector.tensor_tensor(xs_at(i), xs_at(i), ps[s][:, 0:SC], ALU.add).then_inc(fin, 1)
                            nc.vector.tensor_tensor(xv_at(i), xv_at(i), by_component(ps[s][:, SC:FEAT]), ALU.add).then_inc(fin, 1)

                        steps(dve, NT, 0, step)

        def layer_2():
            node_pass("l2", ["L2_gnn_Ws_src", "L2_gnn_Ws_dst"], ["L2_gnn_Wv_src", "L2_gnn_Wv_dst"], [table[2], table[3]], finish_l2, 4,
                      gamma=("L2_gnn_gamma_s", "L2_gnn_beta_s", "L2_gnn_gamma_v"))
            attention_pass()
            softmax_pass()
            gather_messages()
            post_l2()

        def store_x():
            with ExitStack() as ctx:
                stored = sem(ctx, "result_stored")
                full = NODES // P
                with nc.Block() as block:

                    @block.sync
                    def _(sp):
                        sp.dma_start(out[0:full * P, :].rearrange("(t p) f -> p t f", p=P), x3[:, 0:full, :]).then_inc(stored, 16)
                        sp.dma_start(out[full * P:NODES, :], x3[0:NODES - full * P, full, :]).then_inc(stored, 16)
                        sp.wait_ge(stored, 32)

        import math
        c_self = math.sin(math.pi / 8)
        setup()
        norm_all("l0", False)
        node_pass("l0", ["L0_gnn_Wl1_0", "L0_gnn_Wsc0"], ["L0_gnn_Wl1_1", "L0_gnn_Wsc1"], [table[0]], finish_l0, 4,
                  [(0, SC ** -0.5), (0, VC ** -0.5)])
        edge_pass("l0", table[0], "edge_attr_8_T", "L0_gnn_Wfc1", "L0_gnn_Wfc2", "L0_gnn_Wfc3", ACT.Gelu_apprx_tanh,
                  [8.0 ** -0.5, SC ** -0.5])
        post_l0()
        end_layer()
        if LAYERS > 1:
            norm_all("l1", False)
            node_pass("l1", ["L1_gnn_W1_s", "L1_gnn_W_sc_s"], ["L1_gnn_W1_v", "L1_gnn_W_sc_v"], [table[1], self_rows], finish_l1, 4,
                      [(0, SC ** -0.5), (0, VC ** -0.5)])
            edge_pass("l1", table[1], "edge_attr_8_T", "L1_gnn_fcW1", None, "L1_gnn_fcW2", ACT.Silu, [8.0 ** -0.5])
            post_l1()
            end_layer()
        if LAYERS > 2:
            norm_all("l2", True)
            layer_2()
            end_layer()
        if LAYERS > 3:
            norm_all("l3", False)
            node_pass("l3", ["L3_gnn_Ws_l1_a", "L3_gnn_Ws_l1_c", "L3_gnn_Ws_sc_a", "L3_gnn_Ws_sc_c"],
                      ["L3_gnn_Wv_l1_a", "L3_gnn_Wv_l1_c", "L3_gnn_Wv_sc_a", "L3_gnn_Wv_sc_c"], [table[4]], finish_l3, 8,
                      [(0, 1.0), (1, 1.0), (0, c_self), (1, c_self)])
            edge_pass("l3", table[4], "edge_attr_10_T", "L3_gnn_W_fc1", None, "L3_gnn_W_fc2", ACT.Silu, [1.0])
            post_l3()
        store_x()


LAYERS = 4


def kernel(**inputs):
    import numpy as np
    import concourse.bacc as bacc
    from concourse import mybir
    from concourse.bass_utils import run_bass_kernel_spmd

    given = {n: np.asarray(v) for n, v in inputs.items()}

    def padded(a, rows, fill=0):
        return np.concatenate([a, np.full((rows - a.shape[0],) + a.shape[1:], fill, a.dtype)])

    def grouped(a):
        a = a.reshape((NG, TG, P) + a.shape[1:])
        a = np.moveaxis(a, 1, 2)
        return np.ascontiguousarray(a.reshape(NG * P, -1))

    src = padded(given.pop("src").astype(np.int32), EPAD)
    dst = padded(given.pop("dst").astype(np.int32), EPAD, NODES)
    y = padded(given.pop("edge_attr_4"), EPAD)
    arrays = {
        "x": padded(given.pop("x"), NPAD),
        "src_groups": grouped(src),
        "dst_groups": grouped(dst),
        "dst_tiles": dst.reshape(NG * TG, P).T,
        "dst_first": dst[::GE][None, :],
        "dst_line": np.concatenate([np.full(1, -1, np.int32), dst, np.full(1, NODES + 1, np.int32)])[None, :],
        "y_all": grouped(y[:, [0, 1, 2, 3, 1, 2]]).reshape(NG, P, TG * YC).transpose(1, 0, 2).reshape(P, -1),
        "y4": y.reshape(NG * TG, P, 4).transpose(1, 0, 2).reshape(P, -1),
    }
    for n, name in enumerate(["node_vec1", "node_vec1_n2", "node_vec1_n3"]):
        arrays[f"attr_{n}"] = padded(given.pop(name), NPAD).reshape(NT, P).T
    for name in ["edge_attr_8", "edge_attr_10", "edge_attr_16"]:
        arrays[f"{name}_T"] = padded(given.pop(name), EPAD).T
    for name, a in given.items():
        arrays[name] = a[:, None] if a.ndim == 1 else a.reshape(-1, 1) if a.ndim == 3 else a
    for name in ["L3_gnn_Ws_l2_a", "L3_gnn_Ws_l2_c", "L3_gnn_Wv_l2_a", "L3_gnn_Wv_l2_c", "L2_gnn_W_alpha", "L2_gnn_Ws_val"]:
        arrays[f"{name}_T"] = given[name].T
    arrays = {f"in_{n}": np.ascontiguousarray(a) for n, a in arrays.items()}

    nc = bacc.Bacc("TRN2", target_bir_lowering=False, num_devices=1)
    A = {n[3:]: nc.dram_tensor(n, a.shape, mybir.dt.from_np(a.dtype), kind="ExternalInput").ap() for n, a in arrays.items()}
    out = nc.dram_tensor("out", (NODES, FEAT), mybir.dt.float32, kind="ExternalOutput").ap()
    build(nc, A, out)
    return run_bass_kernel_spmd(nc, [arrays], core_ids=[0]).results[0]["out"]
```

```python
NODES, EDGES, FEAT = 6250, 100000, 160
P = 128
SC, VC, XYZ = 64, 32, 3
VF = VC * XYZ
NT = -(-NODES // P)
NPAD = NT * P
TG = 4
GE = TG * P
NG = 196
EPAD = NG * GE
WIN = 64
COLS = NPAD + WIN
SHIFTS = -(-NPAD // WIN)
MID = SC + VC
YC = 6
HEADS, HS, HV = 4, 16, 8
HF = HS + XYZ * HV
CHUNKS = P // HEADS
CHUNK = EPAD // CHUNKS
EPS = 1e-5
LOWEST = -1.5e38


def build(nc, A, out):
    from contextlib import ExitStack

    import concourse.bass as bass
    from concourse import mybir

    F32, I32 = mybir.dt.float32, mybir.dt.int32
    ALU, ACT, AX = mybir.AluOpType, mybir.ActivationFunctionType, mybir.AxisListType
    ds = bass.ds

    def at_least(eng, sem, value):
        if isinstance(value, int) and value <= 0:
            return
        eng.wait_ge(sem, value)

    def gate(eng, settled, *waits):
        waits = [(sem, v if isinstance(v, int) else eng.to_reg(v)) for sem, v in waits if not isinstance(v, int) or v > 0]
        eng.wait_ge(*settled)
        for sem, v in waits:
            eng.wait_ge(sem, v)

    def steps(eng, n, lag, emit, warm=4, unroll=2):
        for i in range(warm):
            emit(i, i % unroll, i // unroll)
        turns = (n - warm) // unroll
        with eng.Fori(0, turns) as j:
            for k in range(unroll):
                emit(j * unroll + (warm + k), (warm + k) % unroll, j + (warm + k) // unroll)
        for i in range(warm + turns * unroll, n + lag):
            emit(i, i % unroll, i // unroll)

    def live(i, n):
        return not isinstance(i, int) or 0 <= i < n

    def back(s, r, lag, unroll=2):
        return (s - lag) % unroll, r + (s - lag) // unroll

    table = [nc.dram_tensor(f"node_table_{n}", (NPAD, FEAT), F32).ap() for n in range(5)]
    self_rows = nc.dram_tensor("l1_self_rows", (NPAD, FEAT), F32).ap()
    messages = nc.dram_tensor("l2_messages", (EPAD, FEAT), F32).ap()
    scores_T = nc.dram_tensor("l2_scores", (HEADS, EPAD), F32).ap()
    exps_T = nc.dram_tensor("l2_exps", (HEADS, EPAD), F32).ap()
    chunk_ends = nc.dram_tensor("l2_chunk_ends", (2, P), F32).ap()
    chunk_carries = nc.dram_tensor("l2_chunk_carries", (2, P), F32).ap()
    turn_row = nc.dram_tensor("l1_turn_row", (1, NPAD), F32).ap()

    whole = ExitStack()

    def sbuf(ctx, name, shape, dt=F32):
        return ctx.enter_context(nc.sbuf_tensor(name, shape, dt))

    def psum(ctx, name, shape):
        return ctx.enter_context(nc.psum_tensor(name, shape, F32))

    layer_sems = []

    def sem(ctx, name):
        layer_sems.append(nc.alloc_semaphore(name))
        return layer_sems[-1]

    def clear_sems(first, last):
        nc.clear_and_free_semaphores(layer_sems[first:last])
        del layer_sems[first:last]

    def all_windows(sums):
        sums("", True)
        widest = nc.values_load(span[0:1, 0:1], min_val=0, max_val=NODES)
        with nc.If(widest >= WIN):
            own = len(layer_sems)
            with nc.Fori(1, SHIFTS) as shift:
                with nc.If(widest >= shift * WIN):
                    sums("wide_", False)
                    clear_sems(own, len(layer_sems))
                    nc.all_engine_barrier()

    with whole:
        x = sbuf(whole, "x", [P, NT * FEAT])
        y4 = sbuf(whole, "y4", [P, NG * TG * 4])
        sums_T = sbuf(whole, "sums_T", [P, 4 * COLS])
        dst_rel = sbuf(whole, "dst_rel", [P, NG * TG])
        first_row = sbuf(whole, "first_row", [1, NG])
        span = sbuf(whole, "span", [1, 1], I32)
        window_row = sbuf(whole, "window_row", [1, NG], I32)
        iota_win = sbuf(whole, "iota_win", [P, WIN])
        iota_home = sbuf(whole, "iota_home", [P, WIN])
        ident = sbuf(whole, "ident", [P, P])
        attr = sbuf(whole, "attr", [P, 3, NT])
        row_scale = sbuf(whole, "row_scale", [P, 4])

        x3 = x[:, :].rearrange("p (t f) -> p t f", t=NT)
        sums4 = sums_T[:, :].rearrange("p (b n) -> p b n", b=4)
        exps = sums_T[:, 2 * COLS:2 * COLS + NG * TG * HEADS]

        def setup():
            with ExitStack() as ctx:
                dst_i = sbuf(ctx, "dst_i", [P, NG * TG], I32)
                dst_f = sbuf(ctx, "dst_f", [P, NG * TG])
                last_i = sbuf(ctx, "last_i", [1, NG], I32)
                span_f = sbuf(ctx, "span_f", [1, 2 * NG + 1])
                ones_row = sbuf(ctx, "ones_row", [1, P])
                iota_i = sbuf(ctx, "iota_i", [P, WIN], I32)
                diag_i = sbuf(ctx, "diag_i", [P, P], I32)
                first_ps = psum(ctx, "first_ps", [P, NG])
                loaded = sem(ctx, "setup_loaded")
                iotas = sem(ctx, "setup_iotas")
                firsts = sem(ctx, "setup_firsts")
                spread = sem(ctx, "setup_spread")
                made = sem(ctx, "setup_made")
                with nc.Block() as block:

                    @block.sync
                    def _(sp):
                        sp.dma_start(x3, A["x"].rearrange("(t p) f -> p t f", p=P)).then_inc(loaded, 16)
                        sp.dma_start(dst_i[:, :], A["dst_tiles"]).then_inc(loaded, 16)
                        sp.dma_start(window_row[:, :], A["dst_first"]).then_inc(loaded, 16)
                        sp.dma_start(last_i[:, :], A["dst_last"]).then_inc(loaded, 16)
                        sp.dma_start(y4[:, :], A["y4"]).then_inc(loaded, 16)
                        for n in range(3):
                            sp.dma_start(attr[:, n, :], A[f"attr_{n}"]).then_inc(loaded, 16)

                    @block.gpsimd
                    def _(pool):
                        nc.gpsimd.iota(iota_i[:, :], pattern=[[1, WIN]], base=0, channel_multiplier=0).then_inc(iotas, 1)
                        nc.gpsimd.iota(diag_i[:, :], pattern=[[1, P]], base=0, channel_multiplier=-1).then_inc(iotas, 1)

                    @block.vector
                    def _(dve):
                        nc.vector.memset(ones_row[:, :], 1.0).then_inc(made, 1)
                        nc.vector.memset(row_scale[:, :], 1.0).then_inc(made, 1)
                        dve.wait_ge(made, 2)
                        nc.vector.memset(row_scale[SC:MID, 0:1], 3.0 ** -0.5).then_inc(made, 1)
                        nc.vector.memset(row_scale[MID:P, 1:2], 2.0 ** -0.5).then_inc(made, 1)
                        nc.vector.memset(row_scale[VC:SC, 2:3], 2.0 ** -0.5).then_inc(made, 1)
                        nc.vector.memset(row_scale[MID:P, 2:3], 2.0 ** -0.5).then_inc(made, 1)
                        dve.wait_ge(iotas, 2)
                        nc.vector.tensor_copy(iota_win[:, :], iota_i[:, :]).then_inc(made, 1)
                        nc.vector.tensor_copy(iota_home[:, :], iota_i[:, :]).then_inc(made, 1)
                        nc.vector.tensor_scalar(ident[:, :], diag_i[:, :], 0.0, None, ALU.is_equal).then_inc(made, 1)
                        dve.wait_ge(loaded, 16 * 8)
                        nc.vector.tensor_copy(first_row[:, :], window_row[:, :]).then_inc(firsts, 1)
                        nc.vector.tensor_copy(dst_f[:, :], dst_i[:, :]).then_inc(made, 1)
                        nc.vector.tensor_copy(span_f[:, 0:NG], last_i[:, :]).then_inc(made, 1)
                        dve.wait_ge(made, 11)
                        dve.wait_ge(firsts, 1)
                        nc.vector.tensor_tensor(span_f[:, NG:2 * NG], span_f[:, 0:NG], first_row[:, :], ALU.subtract).then_inc(made, 1)
                        dve.wait_ge(made, 12)
                        nc.vector.tensor_reduce(span_f[:, 2 * NG:2 * NG + 1], span_f[:, NG:2 * NG], AX.X, ALU.max).then_inc(made, 1)
                        dve.wait_ge(made, 13)
                        nc.vector.tensor_copy(span[:, :], span_f[:, 2 * NG:2 * NG + 1]).then_inc(made, 1)
                        dve.wait_ge(spread, 1)
                        nc.vector.tensor_tensor(
                            dst_rel[:, :].rearrange("p (g t) -> p g t", t=TG),
                            dst_f[:, :].rearrange("p (g t) -> p g t", t=TG),
                            first_ps[:, :].unsqueeze(2).to_broadcast([P, NG, TG]),
                            ALU.subtract).then_inc(made, 1)

                    @block.tensor
                    def _(pe):
                        pe.wait_ge(made, 1)
                        pe.wait_ge(firsts, 1)
                        nc.tensor.matmul(first_ps[:, :], ones_row[:, :], first_row[:, :]).then_inc(spread, 1)

        def place_windows(dve, first, placed):
            if first:
                nc.vector.tensor_copy(iota_win[:, :], iota_home[:, :]).then_inc(placed, 1)
                nc.vector.tensor_copy(window_row[:, :], first_row[:, :]).then_inc(placed, 1)
            else:
                nc.vector.tensor_scalar(iota_win[:, :], iota_win[:, :], float(WIN), None, ALU.add).then_inc(placed, 1)
                nc.vector.tensor_scalar(window_row[:, :], window_row[:, :], float(WIN), float(NPAD), ALU.add, ALU.min).then_inc(placed, 1)
            dve.wait_ge(placed, 2)

        def norm_all(tag, equivariant):
            h = sums_T[:, 0:NT * FEAT]
            sq = sums_T[:, NT * FEAT:2 * NT * FEAT]
            h3 = h.rearrange("p (t f) -> p t f", t=NT)
            sq3 = sq.rearrange("p (t f) -> p t f", t=NT)
            with ExitStack() as ctx:
                stat = sbuf(ctx, f"{tag}_stat", [P, 8, NT])
                dve_at = sem(ctx, f"{tag}_norm_dve")
                act_at = sem(ctx, f"{tag}_norm_act")
                clear_sems(0, len(layer_sems) - 2)

                def wide(n, width):
                    return stat[:, n, :].unsqueeze(2).to_broadcast([P, NT, width])

                with nc.Block() as block:

                    @block.vector
                    def _(dve):
                        count = [0]

                        def then(ins):
                            count[0] += 1
                            ins.then_inc(dve_at, 1)
                            dve.wait_ge(dve_at, count[0])

                        then(nc.vector.tensor_reduce(stat[:, 0, :], x3, AX.X, ALU.add))
                        then(nc.vector.tensor_scalar(stat[:, 1, :], stat[:, 0, :], 1.0 / FEAT, None, ALU.mult))
                        then(nc.vector.tensor_tensor(h3, x3, wide(1, FEAT), ALU.subtract))
                        dve.wait_ge(act_at, 1)
                        then(nc.vector.tensor_reduce(stat[:, 2, :], sq3, AX.X, ALU.add))
                        then(nc.vector.tensor_scalar(stat[:, 3, :], stat[:, 2, :], 1.0 / FEAT, EPS, ALU.mult, ALU.add))
                        dve.wait_ge(act_at, 2)
                        then(nc.vector.reciprocal(stat[:, 5, :], stat[:, 4, :]))
                        then(nc.vector.tensor_tensor(h3, h3, wide(5, FEAT), ALU.mult))
                        then(nc.vector.tensor_scalar(h, h, 0.0, None, ALU.max))
                        if equivariant:
                            then(nc.vector.tensor_tensor(x[:, :], x[:, :], h, ALU.add))
                            hs, hv = h3[:, :, 0:SC], h3[:, :, SC:FEAT]
                            then(nc.vector.tensor_reduce(stat[:, 0, :], hs, AX.X, ALU.add))
                            then(nc.vector.tensor_scalar(stat[:, 1, :], stat[:, 0, :], 1.0 / SC, None, ALU.mult))
                            then(nc.vector.tensor_tensor(hs, hs, wide(1, SC), ALU.subtract))
                            dve.wait_ge(act_at, 3)
                            then(nc.vector.tensor_reduce(stat[:, 2, :], sq3[:, :, 0:SC], AX.X, ALU.add))
                            then(nc.vector.tensor_reduce(stat[:, 3, :], sq3[:, :, SC:FEAT], AX.X, ALU.add))
                            then(nc.vector.tensor_scalar(stat[:, 2, :], stat[:, 2, :], 1.0 / SC, EPS, ALU.mult, ALU.add))
                            then(nc.vector.tensor_scalar(stat[:, 3, :], stat[:, 3, :], 1.0 / VC, EPS, ALU.mult, ALU.add))
                            dve.wait_ge(act_at, 4)
                            then(nc.vector.reciprocal(stat[:, 6:8, :], stat[:, 4:6, :]))
                            then(nc.vector.tensor_tensor(hs, hs, wide(6, SC), ALU.mult))
                            then(nc.vector.tensor_tensor(hv, hv, wide(7, VF), ALU.mult))

                    @block.scalar
                    def _(act):
                        act.wait_ge(dve_at, 3)
                        nc.scalar.activation(sq, h, ACT.Square).then_inc(act_at, 1)
                        act.wait_ge(dve_at, 5)
                        nc.scalar.activation(stat[:, 4, :], stat[:, 3, :], ACT.Sqrt).then_inc(act_at, 1)
                        if equivariant:
                            act.wait_ge(dve_at, 12)
                            nc.scalar.activation(sq, h, ACT.Square).then_inc(act_at, 1)
                            act.wait_ge(dve_at, 16)
                            nc.scalar.activation(stat[:, 4:6, :], stat[:, 2:4, :], ACT.Sqrt).then_inc(act_at, 1)

        def node_pass(tag, scalar_maps, vector_maps, tables, finish, n_fin, coefs=(), gamma=None):
            ns, nv, n_tab = SC * len(scalar_maps), VF * len(vector_maps), len(tables)
            norm = sums_T[:, 0:NT * FEAT]
            with ExitStack() as ctx:
                w_s = sbuf(ctx, f"{tag}_w_s", [SC, ns])
                w_v = sbuf(ctx, f"{tag}_w_v", [VF, nv])
                coef = sbuf(ctx, f"{tag}_coef", [P, 8, NT])
                gam = sbuf(ctx, f"{tag}_gam", [VF, 4])
                tile = [sbuf(ctx, f"{tag}_tile{s}", [P, FEAT]) for s in range(2)]
                tile_T = [sbuf(ctx, f"{tag}_tile_T{s}", [VF, 2 * P]) for s in range(2)]
                rows = [[sbuf(ctx, f"{tag}_rows{k}_{s}", [P, FEAT]) for k in range(n_tab)] for s in range(2)]
                temp = sbuf(ctx, f"{tag}_temp", [P, 2 * FEAT])
                ps_t = [psum(ctx, f"{tag}_ps_t{s}", [P, 512]) for s in range(2)]
                ps_s = [psum(ctx, f"{tag}_ps_s{s}", [P, 512]) for s in range(2)]
                ps_v = [psum(ctx, f"{tag}_ps_v{s}", [P, 512]) for s in range(2)]
                zeroed = sem(ctx, f"{tag}_zeroed")
                w_loaded = sem(ctx, f"{tag}_w_loaded")
                w_ready = sem(ctx, f"{tag}_w_ready")
                coef_ready = sem(ctx, f"{tag}_coef_ready")
                copied = sem(ctx, f"{tag}_copied")
                turned = sem(ctx, f"{tag}_turned")
                tile_ready = sem(ctx, f"{tag}_tile_ready")
                mapped = sem(ctx, f"{tag}_mapped")
                fin = sem(ctx, f"{tag}_fin")
                stored = [sem(ctx, f"{tag}_stored{s}") for s in range(2)]
                n_w = len(scalar_maps) + XYZ * len(vector_maps) + (2 + XYZ if gamma else 0)

                with nc.Block() as block:

                    @block.sync
                    def _(sp):
                        for n, w in enumerate(scalar_maps):
                            sp.dma_start(w_s[:, n * SC:(n + 1) * SC], A[w]).then_inc(w_loaded, 16)
                        sp.wait_ge(zeroed, 1)
                        for n, w in enumerate(vector_maps):
                            for c in range(XYZ):
                                at = n * VF + c * VC
                                sp.dma_start(w_v[c:VF:XYZ, at:at + VC], A[w]).then_inc(w_loaded, 16)
                        if gamma:
                            sp.dma_start(gam[0:SC, 0:1], A[gamma[0]]).then_inc(w_loaded, 16)
                            sp.dma_start(gam[0:SC, 1:2], A[gamma[1]]).then_inc(w_loaded, 16)
                            for c in range(XYZ):
                                sp.dma_start(gam[c:VF:XYZ, 2:3], A[gamma[2]]).then_inc(w_loaded, 16)

                        def store(i, s, r):
                            sp.wait_ge(fin, (i + 1) * n_fin)
                            for k in range(n_tab):
                                sp.dma_start(tables[k][ds(i * P, P), :], rows[s][k][:, :]).then_inc(stored[s], 16)

                        steps(sp, NT, 0, store)
                        for s in range(2):
                            sp.wait_ge(stored[s], 16 * n_tab * ((NT + 1 - s) // 2))

                    @block.scalar
                    def _(act):
                        if gamma:
                            act.wait_ge(w_loaded, 16 * n_w)

                        def step(i, s, r):
                            if live(i, NT):
                                at_least(act, turned, i - 1)
                                nc.scalar.activation(tile[s][:, :], norm[:, ds(i * FEAT, FEAT)], ACT.Copy).then_inc(copied, 1)
                            if live(i - 1, NT):
                                s1, _ = back(s, r, 1)
                                at_least(act, turned, i)
                                at_least(act, mapped, i - 2)
                                if gamma:
                                    nc.scalar.activation(tile_T[s1][0:SC, 0:P], ps_t[s1][0:SC, 0:P], ACT.Identity,
                                                         bias=gam[0:SC, 1:2], scale=gam[0:SC, 0:1]).then_inc(tile_ready, 1)
                                else:
                                    nc.scalar.activation(tile_T[s1][0:SC, 0:P], ps_t[s1][0:SC, 0:P], ACT.Copy).then_inc(tile_ready, 1)
                                nc.scalar.activation(tile_T[s1][0:VF, P:2 * P], ps_t[s1][0:VF, P:2 * P], ACT.Copy).then_inc(tile_ready, 1)

                        steps(act, NT, 1, step)

                    @block.tensor
                    def _(pe):
                        pe.wait_ge(w_loaded, 16 * n_w)
                        if gamma:
                            pe.wait_ge(w_ready, 1)

                        def step(i, s, r):
                            if live(i, NT):
                                at_least(pe, copied, i + 1)
                                at_least(pe, tile_ready, 2 * (i - 1))
                                nc.tensor.transpose(ps_t[s][0:VF, P:2 * P], tile[s][:, SC:FEAT], ident[:, :])
                                nc.tensor.transpose(ps_t[s][0:SC, 0:P], tile[s][:, 0:SC], ident[:, :]).then_inc(turned, 1)
                            if live(i - 1, NT):
                                s1, _ = back(s, r, 1)
                                at_least(pe, tile_ready, 2 * i)
                                at_least(pe, fin, (i - 2) * n_fin)
                                nc.tensor.matmul(ps_s[s1][:, 0:ns], tile_T[s1][0:SC, 0:P], w_s[:, :])
                                nc.tensor.matmul(ps_v[s1][:, 0:nv], tile_T[s1][0:VF, P:2 * P], w_v[:, :]).then_inc(mapped, 1)

                        steps(pe, NT, 1, step)

                    @block.vector
                    def _(dve):
                        nc.vector.memset(w_v[:, :], 0.0).then_inc(zeroed, 1)
                        for n, (k, factor) in enumerate(coefs):
                            nc.vector.tensor_scalar(coef[:, n, :], attr[:, k, :], factor, None, ALU.mult).then_inc(coef_ready, 1)
                        if gamma:
                            dve.wait_ge(w_loaded, 16 * n_w)
                            nc.vector.tensor_scalar(w_v[:, :], w_v[:, :], gam[0:VF, 2:3], None, ALU.mult).then_inc(w_ready, 1)
                        dve.wait_ge(coef_ready, len(coefs))

                        def step(i, s, r):
                            at_least(dve, mapped, i + 1)
                            at_least(dve, stored[s], 16 * n_tab * r)
                            at_least(dve, fin, i * n_fin)
                            finish(dve, i, ps_s[s], ps_v[s], rows[s], coef, temp, fin, i * n_fin)

                        steps(dve, NT, 0, step)

        def xs_at(t):
            return x[:, ds(t * FEAT, SC)]

        def xv_at(t):
            return x[:, ds(t * FEAT + SC, VF)].rearrange("p (u c) -> p c u", c=XYZ)

        def by_component(ap):
            return ap.rearrange("p (c u) -> p c u", c=XYZ)

        def finish_l0(dve, t, ps_s, ps_v, rows, coef, temp, fin, k):
            a_s, a_v = coef[:, 0, ds(t, 1)], coef[:, 1, ds(t, 1)]
            nc.vector.tensor_scalar(rows[0][:, 0:SC], ps_s[:, 0:SC], a_s, None, ALU.mult).then_inc(fin, 1)
            nc.vector.tensor_scalar(rows[0][:, SC:FEAT], ps_v[:, 0:VF], a_v, None, ALU.mult).then_inc(fin, 1)
            nc.vector.scalar_tensor_tensor(xs_at(t), ps_s[:, SC:2 * SC], a_s, xs_at(t), ALU.mult, ALU.add).then_inc(fin, 1)
            nc.vector.scalar_tensor_tensor(xv_at(t), by_component(ps_v[:, VF:2 * VF]), a_v, xv_at(t),
                                           ALU.mult, ALU.add).then_inc(fin, 1)

        def finish_l1(dve, t, ps_s, ps_v, rows, coef, temp, fin, k):
            a_s, a_v = coef[:, 0, ds(t, 1)], coef[:, 1, ds(t, 1)]
            for n in range(2):
                nc.vector.tensor_scalar(rows[n][:, 0:SC], ps_s[:, n * SC:(n + 1) * SC], a_s, None, ALU.mult).then_inc(fin, 1)
                nc.vector.tensor_scalar(rows[n][:, SC:FEAT], ps_v[:, n * VF:(n + 1) * VF], a_v, None, ALU.mult).then_inc(fin, 1)

        def finish_l2(dve, t, ps_s, ps_v, rows, coef, temp, fin, k):
            for n in range(2):
                nc.vector.tensor_copy(rows[n][:, 0:SC], ps_s[:, n * SC:(n + 1) * SC]).then_inc(fin, 1)
                nc.vector.tensor_copy(rows[n][:, SC:FEAT], ps_v[:, n * VF:(n + 1) * VF]).then_inc(fin, 1)

        def finish_l3(dve, t, ps_s, ps_v, rows, coef, temp, fin, k):
            a0, a1, c0, c1 = (coef[:, n, ds(t, 1)] for n in range(4))
            nc.vector.tensor_scalar(temp[:, 0:SC], ps_s[:, 0:SC], a0, None, ALU.mult).then_inc(fin, 1)
            nc.vector.tensor_scalar(temp[:, SC:FEAT], ps_v[:, 0:VF], a0, None, ALU.mult).then_inc(fin, 1)
            nc.vector.scalar_tensor_tensor(xs_at(t), ps_s[:, 2 * SC:3 * SC], c0, xs_at(t), ALU.mult, ALU.add).then_inc(fin, 1)
            nc.vector.scalar_tensor_tensor(xv_at(t), by_component(ps_v[:, 2 * VF:3 * VF]), c0, xv_at(t),
                                           ALU.mult, ALU.add).then_inc(fin, 1)
            dve.wait_ge(fin, k + 4)
            nc.vector.scalar_tensor_tensor(rows[0][:, 0:SC], ps_s[:, SC:2 * SC], a1, temp[:, 0:SC], ALU.mult, ALU.add).then_inc(fin, 1)
            nc.vector.scalar_tensor_tensor(rows[0][:, SC:FEAT], ps_v[:, VF:2 * VF], a1, temp[:, SC:FEAT],
                                           ALU.mult, ALU.add).then_inc(fin, 1)
            nc.vector.scalar_tensor_tensor(xs_at(t), ps_s[:, 3 * SC:4 * SC], c1, xs_at(t), ALU.mult, ALU.add).then_inc(fin, 1)
            nc.vector.scalar_tensor_tensor(xv_at(t), by_component(ps_v[:, 3 * VF:4 * VF]), c1, xv_at(t),
                                           ALU.mult, ALU.add).then_inc(fin, 1)

        def warm_up(bank):
            for _ in range(6):
                nc.tensor.matmul(bank[:, 0:512], ident[:, :], x[:, 0:512])

        def edge_pass(tag, first, rows_of, edge_T, w_in, w_mid, w_out, act_fn, scales):
            k_in, hid = A[w_in].shape
            layers = 2 if w_mid else 1
            wn = 2 * SC + 2 * VC
            SS, SV, VS, VV = 0, SC, 2 * SC, 2 * SC + VC
            K = 9
            U = 4
            FETCH = 4
            lag = layers + 1
            with ExitStack() as ctx:
                def slots(n, name, shape, dt=F32):
                    return [sbuf(ctx, f"{tag}_edge_{name}{s}", shape, dt) for s in range(n)]

                wi = sbuf(ctx, f"{tag}_edge_wi", [k_in, hid])
                wm = sbuf(ctx, f"{tag}_edge_wm", [hid, hid])
                wo = sbuf(ctx, f"{tag}_edge_wo", [hid, wn])
                idx = slots(FETCH, "idx", [P, TG], I32)
                g = slots(FETCH, "g", [P, TG, FEAT])
                ea = slots(2, "ea", [k_in, GE])
                h = [slots(2, f"h{n}_", [hid, GE]) for n in range(layers)]
                gy = slots(2, "gy", [P, TG, FEAT])
                prod = slots(2, "prod", [P, TG, 4, MID])
                hot = slots(2, "hot", [P, TG, WIN])
                pw = sbuf(ctx, f"{tag}_edge_pw", [P, TG, SC])
                vy = sbuf(ctx, f"{tag}_edge_vy", [P, TG, XYZ, VC])
                dot = sbuf(ctx, f"{tag}_edge_dot", [P, 2, TG, VC])
                h_ps = [psum(ctx, f"{tag}_edge_h_ps{n}", [P, GE]) for n in range(2)]
                w_ps = [psum(ctx, f"{tag}_edge_w_ps{s}", [P, TG, 256]) for s in range(2)]
                win_ps = [psum(ctx, f"{tag}_edge_win_ps{s}", [P, 512]) for s in range(2)]
                zeroed = sem(ctx, f"{tag}_edge_zeroed")
                placed = sem(ctx, f"{tag}_edge_placed")
                w_loaded = sem(ctx, f"{tag}_edge_w_loaded")
                idx_loaded = [sem(ctx, f"{tag}_edge_idx_loaded{s}") for s in range(FETCH)]
                fetched = [sem(ctx, f"{tag}_edge_fetched{s}") for s in range(FETCH)]
                ea_loaded = [sem(ctx, f"{tag}_edge_ea_loaded{s}") for s in range(2)]
                hidden = [sem(ctx, f"{tag}_edge_hidden{n}") for n in range(layers)]
                active = [sem(ctx, f"{tag}_edge_active{n}") for n in range(layers)]
                scaled = sem(ctx, f"{tag}_edge_scaled")
                weighed = sem(ctx, f"{tag}_edge_weighed")
                made = sem(ctx, f"{tag}_edge_made")
                summed = sem(ctx, f"{tag}_edge_summed")
                added = sem(ctx, f"{tag}_edge_added")
                last = layers - 1

                def half(s, r):
                    return s % 2, r * 2 + s // 2

                with nc.Block() as block:

                    @block.sync
                    def _(sp):
                        sp.dma_start(wi[:, :], A[w_in]).then_inc(w_loaded, 16)
                        if w_mid:
                            sp.dma_start(wm[:, :], A[w_mid]).then_inc(w_loaded, 16)
                        sp.dma_start(wo[:, :], A[w_out]).then_inc(w_loaded, 16)

                        def step(i, s, r):
                            at_least(sp, fetched[s], 16 * TG * r)
                            sp.dma_start(idx[s][:, :], A["src_groups"][ds(i * P, P), :]).then_inc(idx_loaded[s], 16)
                            at_least(sp, hidden[0], i - 1)
                            sp.dma_start(ea[s % 2][:, :], A[edge_T][:, ds(i * GE, GE)]).then_inc(ea_loaded[s % 2], 16)

                        steps(sp, NG, 0, step, unroll=U)

                    @block.gpsimd
                    def _(pool):
                        for b in range(4 if first else 0):
                            nc.gpsimd.memset(sums_T[:, b * COLS:(b + 1) * COLS], 0.0).then_inc(zeroed, 1)

                        def step(i, s, r):
                            gate(pool, (w_loaded, 16 * (layers + 1)),
                                 (idx_loaded[s], 16 * (r + 1)),
                                 (made, (i - 3) * K))
                            for t in range(TG):
                                pool.indirect_dma_start(g[s][:, t, :], None, rows_of,
                                                        bass.IndirectOffsetOnAxis(idx[s][:, t:t + 1], 0)).then_inc(fetched[s], 16)

                        steps(pool, NG, 0, step, unroll=U)

                    @block.tensor
                    def _(pe):
                        pe.wait_ge(w_loaded, 16 * (layers + 1))

                        def step(i, s, r):
                            if isinstance(i, int) and i == lag + 2:
                                pe.wait_ge(active[last], i - last)
                                warm_up(h_ps[1])
                            if live(i, NG):
                                s0, r0 = half(s, r)
                                at_least(pe, ea_loaded[s0], 16 * (r0 + 1))
                                at_least(pe, active[0], i)
                                nc.tensor.matmul(h_ps[0][0:hid, :], wi[:, :], ea[s0][:, :]).then_inc(hidden[0], 1)
                            if w_mid and live(i - 1, NG):
                                s1 = (s - 1) % 2
                                gate(pe, (w_loaded, 16 * (layers + 1)),
                                     (active[0], i),
                                     (active[1], i - 1))
                                nc.tensor.matmul(h_ps[1][0:hid, :], wm[:, :], h[0][s1][:, :]).then_inc(hidden[1], 1)
                            if live(i - layers, NG):
                                s2 = (s - layers) % 2
                                at_least(pe, active[last], i - layers + 1)
                                at_least(pe, made, (i - layers - 1) * K)
                                for t in range(TG):
                                    ins = nc.tensor.matmul(w_ps[s2][:, t, 0:wn], h[last][s2][:, t * P:(t + 1) * P], wo[:, :])
                                ins.then_inc(weighed, 1)
                            if live(i - lag, NG):
                                s3 = (s - lag) % 2
                                at_least(pe, made, (i - lag + 1) * K)
                                at_least(pe, added, i - lag - 1)
                                for b in range(4):
                                    for t in range(TG):
                                        ins = nc.tensor.matmul(win_ps[s3][0:MID, b * WIN:(b + 1) * WIN], prod[s3][:, t, b, :],
                                                               hot[s3][:, t, :], start=t == 0, stop=t == TG - 1)
                                ins.then_inc(summed, 1)

                        steps(pe, NG, lag, step, warm=8, unroll=U)

                    @block.scalar
                    def _(act):
                        def step(i, s, r):
                            for n in range(layers):
                                if live(i - n, NG):
                                    s1 = (s - n) % 2
                                    after = hidden[n + 1] if n < last else weighed
                                    at_least(act, hidden[n], i - n + 1)
                                    at_least(act, after, i - n - 1)
                                    nc.scalar.activation(h[n][s1][:, :], h_ps[n][0:hid, :], act_fn,
                                                         scale=scales[n]).then_inc(active[n], 1)
                            if live(i - last, NG):
                                k = i - last
                                sk, rk = back(s, r, last, U)
                                at_least(act, made, (k - 1) * K)
                                at_least(act, fetched[sk], 16 * TG * (rk + 1))
                                for t in range(TG):
                                    ins = nc.scalar.activation(gy[sk % 2][:, t, :], g[sk][:, t, :], ACT.Copy,
                                                               scale=y4[:, ds((k * TG + t) * 4, 1)])
                                ins.then_inc(scaled, 1)

                        steps(act, NG, last, step, warm=8, unroll=U)

                    @block.vector
                    def _(dve):
                        place_windows(dve, first, placed)
                        if first:
                            dve.wait_ge(zeroed, 4)

                        def products(i, s, r):
                            def done(n):
                                return i * K + n

                            s0, _ = half(s, r)
                            w, rows, q = w_ps[s0], g[s], prod[s0]
                            xyz = y4[:, ds(i * TG * 4, TG * 4)].rearrange("p (t c) -> p t c", c=4)[:, :, 1:4].unsqueeze(3)
                            vec = rows[:, :, SC:FEAT].rearrange("p t (c u) -> p t c u", c=XYZ)
                            vec0 = gy[s0][:, :, SC:FEAT].rearrange("p t (c u) -> p t c u", c=XYZ)
                            at_least(dve, summed, i - 1)
                            at_least(dve, made, done(0))
                            nc.vector.tensor_tensor(hot[s0][:, :, :], iota_win[:, :].unsqueeze(1).to_broadcast([P, TG, WIN]),
                                                    dst_rel[:, ds(i * TG, TG)].unsqueeze(2).to_broadcast([P, TG, WIN]),
                                                    ALU.is_equal).then_inc(made, 1)
                            at_least(dve, fetched[s], 16 * TG * (r + 1))
                            nc.vector.tensor_tensor(vy[:, :, :, :], vec, xyz.to_broadcast([P, TG, XYZ, VC]), ALU.mult).then_inc(made, 1)
                            at_least(dve, weighed, i + 1)
                            nc.vector.tensor_tensor(pw[:, :, :], w[:, :, SV:VS], rows[:, :, 0:SC], ALU.mult).then_inc(made, 1)
                            dve.wait_ge(made, done(2))
                            nc.vector.tensor_tensor(dot[:, 0, :, :], vy[:, :, 0, :], vy[:, :, 1, :], ALU.add).then_inc(made, 1)
                            at_least(dve, scaled, i + 1)
                            nc.vector.tensor_tensor(q[:, :, 0, 0:SC], w[:, :, SS:SV], gy[s0][:, :, 0:SC], ALU.mult).then_inc(made, 1)
                            dve.wait_ge(made, done(4))
                            nc.vector.tensor_tensor(dot[:, 1, :, :], dot[:, 0, :, :], vy[:, :, 2, :], ALU.add).then_inc(made, 1)
                            nc.vector.tensor_tensor(q[:, :, 1:4, 0:SC], pw[:, :, :].unsqueeze(2).to_broadcast([P, TG, XYZ, SC]),
                                                    xyz.to_broadcast([P, TG, XYZ, SC]), ALU.mult).then_inc(made, 1)
                            nc.vector.tensor_tensor(q[:, :, 1:4, SC:MID], vec0, w[:, :, VS:VV].unsqueeze(2).to_broadcast([P, TG, XYZ, VC]),
                                                    ALU.mult).then_inc(made, 1)
                            dve.wait_ge(made, done(6))
                            nc.vector.tensor_tensor(q[:, :, 0, SC:MID], w[:, :, VV:wn], dot[:, 1, :, :], ALU.mult).then_inc(made, 1)

                        def step(i, s, r):
                            if live(i, NG):
                                products(i, s, r)
                            if live(i - 2, NG):
                                add_window(dve, i - 2, win_ps[s % 2], MID, 4, summed, added)

                        steps(dve, NG, 2, step, unroll=U)

        def add_window(dve, i, bank, rows, blocks, summed, added):
            first = dve.value_load(window_row[0:1, ds(i, 1)], min_val=0, max_val=NPAD)
            at = sums4[0:rows, 0:blocks, ds(first, WIN)]
            at_least(dve, added, i)
            at_least(dve, summed, i + 1)
            nc.vector.tensor_tensor(at, at, bank[0:rows, 0:blocks * WIN].rearrange("p (b n) -> p b n", b=blocks),
                                    ALU.add).then_inc(added, 1)

        def post_pass(tag, load_weights, n_loads, prepare, cols, finish, n_fin, self_loads=False):
            c_s, c_v = cols
            with ExitStack() as ctx:
                w = sbuf(ctx, f"{tag}_post_w", [P, 1024])
                coef = sbuf(ctx, f"{tag}_post_coef", [P, 8, NT])
                sums = [sbuf(ctx, f"{tag}_post_sums{s}", [MID, 4, P]) for s in range(2)]
                own = [sbuf(ctx, f"{tag}_post_own{s}", [P, FEAT]) for s in range(2)]
                small = sbuf(ctx, f"{tag}_post_small", [P, 2])
                line = sbuf(ctx, f"{tag}_post_line", [1, NPAD if self_loads else 2])
                ps = [psum(ctx, f"{tag}_post_ps{s}", [P, 512]) for s in range(2)]
                pw = [psum(ctx, f"{tag}_post_pw{s}", [P, 512]) for s in range(2)]
                w_loaded = sem(ctx, f"{tag}_post_w_loaded")
                w_ready = sem(ctx, f"{tag}_post_w_ready")
                prep = sem(ctx, f"{tag}_post_prep")
                prep_act = sem(ctx, f"{tag}_post_prep_act")
                prep_pe = sem(ctx, f"{tag}_post_prep_pe")
                prep_dma = sem(ctx, f"{tag}_post_prep_dma")
                copied = sem(ctx, f"{tag}_post_copied")
                mapped = sem(ctx, f"{tag}_post_mapped")
                fin = sem(ctx, f"{tag}_post_fin")
                own_loaded = [sem(ctx, f"{tag}_post_own_loaded{s}") for s in range(2)]
                B = dict(w=w, coef=coef, small=small, line=line, ps=ps, pw=pw, w_loaded=w_loaded, w_ready=w_ready, prep=prep,
                         prep_act=prep_act, prep_pe=prep_pe, prep_dma=prep_dma, n_loads=n_loads, fin=fin)

                with nc.Block() as block:

                    @block.sync
                    def _(sp):
                        load_weights(sp, B)
                        if "sp" in prepare:
                            prepare["sp"](sp, B)
                        if self_loads:
                            def step(i, s, r):
                                at_least(sp, fin, (i - 1) * n_fin)
                                sp.dma_start(own[s][:, :], self_rows[ds(i * P, P), :]).then_inc(own_loaded[s], 16)

                            steps(sp, NT, 0, step)

                    @block.scalar
                    def _(act):
                        if "act" in prepare:
                            prepare["act"](act, B)

                        def step(i, s, r):
                            at_least(act, mapped, i - 1)
                            nc.scalar.activation(sums[s][:, :, :], sums4[0:MID, :, ds(i * P, P)], ACT.Copy).then_inc(copied, 1)

                        steps(act, NT, 0, step)

                    @block.tensor
                    def _(pe):
                        if "pe" in prepare:
                            prepare["pe"](pe, B)
                        pe.wait_ge(w_ready, 1)

                        def step(i, s, r):
                            at_least(pe, copied, i + 1)
                            at_least(pe, fin, (i - 1) * n_fin)
                            nc.tensor.matmul(ps[s][:, 0:c_s], sums[s][:, 0, :], w[0:MID, 0:c_s])
                            for c in range(XYZ):
                                ins = nc.tensor.matmul(ps[s][:, c_s + c * c_v:c_s + (c + 1) * c_v], sums[s][:, 1 + c, :],
                                                       w[0:MID, c_s:c_s + c_v])
                            ins.then_inc(mapped, 1)

                        steps(pe, NT, 0, step)

                    @block.vector
                    def _(dve):
                        prepare["dve"](dve, B)

                        def step(i, s, r):
                            at_least(dve, mapped, i + 1)
                            at_least(dve, fin, i * n_fin)
                            if self_loads:
                                at_least(dve, own_loaded[s], 16 * (r + 1))
                            finish(dve, i, ps[s], own[s], coef, small, fin, i * n_fin)

                        steps(dve, NT, 0, step)

        def vectors_of(ps, at, width, col, n):
            return ps[:, at:at + XYZ * width].rearrange("p (c w) -> p c w", c=XYZ)[:, :, col:col + n]

        def post_l0():
            k = (SC ** -0.5) * (32.0 ** -0.5) * (MID ** -0.5)
            cs = SC + 1

            def load(sp, B):
                sp.dma_start(B["w"][0:MID, 0:SC], A["L0_gnn_Wl2_s"]).then_inc(B["w_loaded"], 16)
                sp.dma_start(B["w"][0:MID, SC:cs], A["L0_gnn_Wa"]).then_inc(B["w_loaded"], 16)
                sp.dma_start(B["w"][0:MID, cs:cs + VC], A["L0_gnn_Wl2_v"]).then_inc(B["w_loaded"], 16)

            def prep(dve, B):
                nc.vector.tensor_scalar(B["coef"][:, 1, :], attr[:, 0, :], k, None, ALU.mult).then_inc(B["prep"], 1)
                dve.wait_ge(B["prep"], 1)
                nc.vector.tensor_tensor(B["coef"][:, 0, :], B["coef"][:, 1, :], B["coef"][:, 1, :], ALU.mult).then_inc(B["prep"], 1)
                dve.wait_ge(B["w_loaded"], 48)
                nc.vector.tensor_scalar(B["w"][0:MID, 0:cs], B["w"][0:MID, 0:cs], row_scale[0:MID, 0:1], None, ALU.mult).then_inc(B["w_ready"], 1)
                dve.wait_ge(B["prep"], 2)

            def finish(dve, t, ps, own, coef, small, fin, k0):
                nc.vector.tensor_scalar(small[:, 0:1], ps[:, SC:cs], coef[:, 0, ds(t, 1)], None, ALU.mult).then_inc(fin, 1)
                dve.wait_ge(fin, k0 + 1)
                nc.vector.scalar_tensor_tensor(xs_at(t), ps[:, 0:SC], small[:, 0:1], xs_at(t), ALU.mult, ALU.add).then_inc(fin, 1)
                nc.vector.scalar_tensor_tensor(xv_at(t), vectors_of(ps, cs, VC, 0, VC), small[:, 0:1], xv_at(t),
                                               ALU.mult, ALU.add).then_inc(fin, 1)

            post_pass("l0", load, 3, {"dve": prep}, (cs, VC), finish, 3)

        def post_l1():
            k = (SC ** -0.5) * (10.0 ** -0.5) * (MID ** -0.5)
            ROUND = 1.5 * 2.0 ** 23
            pieces = [(n, min(512, NPAD - n)) for n in range(0, NPAD, 512)]

            def load(sp, B):
                sp.dma_start(B["w"][0:MID, 0:SC], A["L1_gnn_W2_s"]).then_inc(B["w_loaded"], 16)
                sp.dma_start(B["w"][0:MID, SC:MID], A["L1_gnn_W2_v"]).then_inc(B["w_loaded"], 16)
                sp.dma_start(B["w"][0:MID, 512:513], A["L1_gnn_W3"]).then_inc(B["w_loaded"], 16)

            def prep_pe(pe, B):
                pe.wait_ge(B["w_ready"], 1)
                for n, (at, width) in enumerate(pieces):
                    at_least(pe, B["prep_act"], n - 1)
                    nc.tensor.matmul(B["pw"][n % 2][0:1, 0:width], B["w"][0:MID, 512:513], sums4[0:MID, 0, at:at + width]
                                     ).then_inc(B["prep_pe"], 1)

            def prep_act(act, B):
                for n, (at, width) in enumerate(pieces):
                    act.wait_ge(B["prep_pe"], n + 1)
                    nc.scalar.activation(B["line"][0:1, at:at + width], B["pw"][n % 2][0:1, 0:width], ACT.Copy).then_inc(B["prep_act"], 1)
                act.wait_ge(B["prep"], 6)
                nc.scalar.activation(B["coef"][:, 5:7, :], B["coef"][:, 3:5, :], ACT.Sin, scale=6.2831850).then_inc(B["prep_act"], 1)

            def prep_sp(sp, B):
                sp.wait_ge(B["prep_act"], len(pieces))
                sp.dma_start(turn_row, B["line"][0:1, :]).then_inc(B["prep_dma"], 16)
                sp.wait_ge(B["prep_dma"], 16)
                with nc.allow_non_contiguous_dma(reason="a row of node values onto partitions, once"):
                    sp.dma_start(B["coef"][:, 0, :], turn_row[0, :].rearrange("(t p) -> p t", p=P)).then_inc(B["prep_dma"], 16)

            def prep(dve, B):
                c, prep = B["coef"], B["prep"]
                dve.wait_ge(B["w_loaded"], 48)
                nc.vector.tensor_scalar(B["w"][0:MID, 512:513], B["w"][0:MID, 512:513], row_scale[0:MID, 0:1], None, ALU.mult).then_inc(B["w_ready"], 1)
                nc.vector.tensor_scalar(B["w"][0:MID, 0:SC], B["w"][0:MID, 0:SC], row_scale[0:MID, 0:1], None, ALU.mult).then_inc(B["w_ready"], 1)
                nc.vector.tensor_scalar(c[:, 7, :], attr[:, 0, :], k, None, ALU.mult).then_inc(prep, 1)
                dve.wait_ge(B["prep_dma"], 32)
                dve.wait_ge(prep, 1)
                nc.vector.scalar_tensor_tensor(c[:, 1, :], c[:, 0, :], 0.1 / 6.283185307179586, c[:, 7, :], ALU.mult, ALU.mult).then_inc(prep, 1)
                dve.wait_ge(prep, 2)
                nc.vector.tensor_scalar(c[:, 2, :], c[:, 1, :], 0.25, None, ALU.add).then_inc(prep, 1)
                dve.wait_ge(prep, 3)
                nc.vector.tensor_scalar(c[:, 5:7, :], c[:, 1:3, :], ROUND, None, ALU.add).then_inc(prep, 1)
                dve.wait_ge(prep, 4)
                nc.vector.tensor_scalar(c[:, 3:5, :], c[:, 5:7, :], ROUND, None, ALU.subtract).then_inc(prep, 1)
                dve.wait_ge(prep, 5)
                nc.vector.tensor_tensor(c[:, 3:5, :], c[:, 1:3, :], c[:, 3:5, :], ALU.subtract).then_inc(prep, 1)
                dve.wait_ge(B["prep_act"], len(pieces) + 1)
                nc.vector.tensor_tensor(c[:, 0, :], c[:, 5, :], c[:, 7, :], ALU.mult).then_inc(prep, 1)
                dve.wait_ge(prep, 7)

            def finish(dve, t, ps, own, coef, small, fin, k0):
                sin, cos = coef[:, 0, ds(t, 1)], coef[:, 6, ds(t, 1)]
                nc.vector.scalar_tensor_tensor(xs_at(t), ps[:, 0:SC], sin, xs_at(t), ALU.mult, ALU.add).then_inc(fin, 1)
                nc.vector.scalar_tensor_tensor(xv_at(t), vectors_of(ps, SC, VC, 0, VC), sin, xv_at(t), ALU.mult, ALU.add).then_inc(fin, 1)
                dve.wait_ge(fin, k0 + 2)
                nc.vector.scalar_tensor_tensor(xs_at(t), own[:, 0:SC], cos, xs_at(t), ALU.mult, ALU.add).then_inc(fin, 1)
                nc.vector.scalar_tensor_tensor(xv_at(t), by_component(own[:, SC:FEAT]), cos, xv_at(t), ALU.mult, ALU.add).then_inc(fin, 1)

            post_pass("l1", load, 3, {"dve": prep, "pe": prep_pe, "act": prep_act, "sp": prep_sp}, (SC, VC), finish, 4,
                      self_loads=True)

        def post_l3():
            import math
            k = math.cos(math.pi / 8) / math.sqrt(16.0)
            T = {"L3_gnn_Ws_l2_a": 192, "L3_gnn_Ws_l2_c": 288, "L3_gnn_Wv_l2_a": 384, "L3_gnn_Wv_l2_c": 480}
            L = {"L3_gnn_Ws_l3": (576, SC), "L3_gnn_Wv_l3": (640, VC)}
            outs = [("L3_gnn_Ws_l2_a", "L3_gnn_Ws_l3", 0), ("L3_gnn_Ws_l2_c", "L3_gnn_Ws_l3", SC),
                    ("L3_gnn_Wv_l2_a", "L3_gnn_Wv_l3", 2 * SC), ("L3_gnn_Wv_l2_c", "L3_gnn_Wv_l3", 2 * SC + VC)]

            def load(sp, B):
                for n, at in T.items():
                    sp.dma_start(B["w"][0:MID, at:at + MID], A[n + "_T"]).then_inc(B["w_loaded"], 16)
                for n, (at, width) in L.items():
                    sp.dma_start(B["w"][0:MID, at:at + width], A[n]).then_inc(B["w_loaded"], 16)

            def prep_pe(pe, B):
                pe.wait_ge(B["w_loaded"], 16 * 6)
                for l2, l3, at in outs:
                    src, width = L[l3]
                    ins = nc.tensor.matmul(B["pw"][0][0:MID, at:at + width], B["w"][0:MID, T[l2]:T[l2] + MID], B["w"][0:MID, src:src + width])
                ins.then_inc(B["prep_pe"], 1)

            def prep(dve, B):
                c, prep = B["coef"], B["prep"]
                for n in range(2):
                    nc.vector.scalar_tensor_tensor(c[:, n, :], attr[:, n, :], k, attr[:, 2, :], ALU.mult, ALU.mult).then_inc(prep, 1)
                dve.wait_ge(B["prep_pe"], 1)
                nc.vector.tensor_copy(B["w"][0:MID, 2 * SC:192], B["pw"][0][0:MID, 2 * SC:192]).then_inc(prep, 1)
                dve.wait_ge(prep, 3)
                nc.vector.tensor_scalar(B["w"][0:MID, 0:2 * SC], B["pw"][0][0:MID, 0:2 * SC], row_scale[0:MID, 0:1], None,
                                        ALU.mult).then_inc(B["w_ready"], 1)

            def finish(dve, t, ps, own, coef, small, fin, k0):
                for n in range(2):
                    f = coef[:, n, ds(t, 1)]
                    if n:
                        dve.wait_ge(fin, k0 + 2)
                    nc.vector.scalar_tensor_tensor(xs_at(t), ps[:, n * SC:(n + 1) * SC], f, xs_at(t), ALU.mult, ALU.add).then_inc(fin, 1)
                    nc.vector.scalar_tensor_tensor(xv_at(t), vectors_of(ps, 2 * SC, 2 * VC, n * VC, VC), f, xv_at(t),
                                                   ALU.mult, ALU.add).then_inc(fin, 1)

            post_pass("l3", load, 6, {"dve": prep, "pe": prep_pe}, (2 * SC, 2 * VC), finish, 4)

        def attention_pass():
            FW = MID + SC + XYZ * 2 * VC
            PARTS = [(0, MID), (MID, P), (MID + P, P)]
            WW = 2 * SC + 3 * VC
            VS, VV0, VV1 = 2 * SC, 2 * SC + VC, 2 * SC + 2 * VC
            GATE, Q, PV = SC, SC + VC, SC + 2 * VC
            Q2, PV2 = SC, SC + VC
            O1W, O2W = SC + 2 * VC + VF, SC + VC + VF
            K1, K2, K3 = 13, 11, 4
            FETCH = U = 4
            with ExitStack() as ctx:
                def pair(name, shape, dt=F32, n=2):
                    return [sbuf(ctx, f"att_{name}{s}", shape, dt) for s in range(n)]

                w_rbf = sbuf(ctx, "att_w_rbf", [16, WW])
                w_att = sbuf(ctx, "att_w_att", [MID, 2 * SC])
                w_dot = sbuf(ctx, "att_w_dot", [2 * SC, HEADS])
                w_val_T = sbuf(ctx, "att_w_val_T", [SC, MID])
                w_gate = sbuf(ctx, "att_w_gate", [SC, VC])
                w_o1s = sbuf(ctx, "att_w_o1s", [MID, MID])
                w_o1v = [sbuf(ctx, f"att_w_o1v{n}", [P, 2 * VC]) for n in range(2)]
                w_o2s = sbuf(ctx, "att_w_o2s", [MID, SC])
                w_o2v = [sbuf(ctx, f"att_w_o2v{n}", [P, 2 * VC]) for n in range(2)]
                w2 = sbuf(ctx, "att_w2", [P, 3])
                ends = pair("ends", [P, 2 * TG], I32, FETCH)
                ea = pair("ea", [16, GE])
                y_all = sums_T[:, 0:NG * TG * YC]
                g = pair("g", [P, TG, FEAT], n=FETCH)
                gy = pair("gy", [P, TG, FEAT])
                at = NG * TG * YC
                feat = [sums_T[:, at + n * TG * FW:at + (n + 1) * TG * FW].rearrange("p (t f) -> p t f", t=TG) for n in range(4)]
                at += 4 * TG * FW
                feat_T = [sums_T[:, at + n * 3 * GE:at + (n + 1) * 3 * GE].rearrange("p (k e) -> p k e", k=3) for n in range(2)]
                act_T = sbuf(ctx, "att_act_T", [2 * SC, GE])
                score = pair("score", [HEADS, GE])
                gate_s = pair("gate", [P, TG, VC])
                vec2 = [sbuf(ctx, f"att_vec2{n}", [P, TG, XYZ, VC]) for n in range(3)]
                vy = sbuf(ctx, "att_vy", [P, TG, XYZ, VC])
                p1 = sbuf(ctx, "att_p1", [P, TG, XYZ, VC])
                p2 = sbuf(ctx, "att_p2", [P, TG, XYZ, VC])
                dot = sbuf(ctx, "att_dot", [P, TG, VC])
                qy = sbuf(ctx, "att_qy", [P, TG, XYZ, VC])
                rows = pair("rows", [P, TG, HEADS, HF], n=U)
                w_ps = psum(ctx, "att_w_ps", [P, TG, 256])
                o1 = psum(ctx, "att_o1", [P, TG, 256])
                o2 = psum(ctx, "att_o2", [P, TG, 256])
                turn = [psum(ctx, f"att_turn{n}", [P, GE]) for n in range(2)]

                w_zeroed = sem(ctx, "att_w_zeroed")
                w_loaded = sem(ctx, "att_w_loaded")
                w_made = sem(ctx, "att_w_made")
                w_prod = sem(ctx, "att_w_prod")
                ends_loaded = [sem(ctx, f"att_ends_loaded{s}") for s in range(FETCH)]
                ea_loaded = [sem(ctx, f"att_ea_loaded{s}") for s in range(2)]
                y_loaded = sem(ctx, "att_y_loaded")
                fetched = [sem(ctx, f"att_fetched{s}") for s in range(FETCH)]
                joined = [sem(ctx, f"att_joined{s}") for s in range(FETCH)]
                scaled = sem(ctx, "att_scaled")
                y0_done = sem(ctx, "att_y0_done")
                stored = [sem(ctx, f"att_stored{s}") for s in range(U)]
                scores_stored = [sem(ctx, f"att_scores_stored{s}") for s in range(2)]
                weighed = sem(ctx, "att_weighed")
                made1 = sem(ctx, "att_made1")
                made2 = sem(ctx, "att_made2")
                made3 = sem(ctx, "att_made3")
                turned1 = sem(ctx, "att_turned1")
                read1 = sem(ctx, "att_read1")
                turned2 = sem(ctx, "att_turned2")
                read2 = sem(ctx, "att_read2")
                mapped1 = sem(ctx, "att_mapped1")
                mapped2 = sem(ctx, "att_mapped2")
                gated = sem(ctx, "att_gated")
                values_out = sem(ctx, "att_values_out")
                N_LOAD = 32

                def pairs_of(f, lo):
                    return f[:, :, MID + SC:FW].rearrange("p t (c k) -> p t c k", c=XYZ)[:, :, :, lo:lo + VC]

                with nc.Block() as block:

                    @block.sync
                    def _(sp):
                        def put(dst, name, rows=None):
                            a = A["L2_gnn_" + name]
                            sp.dma_start(dst, a if rows is None else a[rows[0]:rows[1], :]).then_inc(w_loaded, 16)

                        sp.dma_start(y_all, A["y_all"]).then_inc(y_loaded, 16)
                        put(w_rbf[:, :], "W_rbf")
                        put(w_att[:, 0:SC], "W_alpha")
                        put(w_att[:, SC:2 * SC], "W_alpha")
                        put(w_val_T[:, :], "Ws_val_T")
                        put(w_gate[:, :], "Wg")
                        put(w_o1s[:, 0:SC], "Ws_val")
                        put(w_o2s[:, :], "Ws_vlin")
                        sp.wait_ge(w_zeroed, 5)
                        for h in range(HEADS):
                            for at in (h * HS, SC + h * HS):
                                put(w_dot[at:at + HS, h:h + 1], "alpha_dot", (h * HS, (h + 1) * HS))
                        for w, name in ((w_o1v, "Wv_val"), (w_o2v, "Wv_vlin")):
                            put(w[0][0:SC, 0:VC], name, (0, SC))
                            put(w[0][SC:P, VC:2 * VC], name, (SC, P))
                            put(w[1][0:SC, 0:VC], name, (SC, P))
                            put(w[1][SC:P, VC:2 * VC], name, (SC, P))
                        put(w2[0:SC, 0:1], "w2_ss")
                        put(w2[SC:MID, 0:1], "w2_vv0")
                        put(w2[0:SC, 1:2], "w2_sv")
                        put(w2[SC:MID, 1:2], "w2_vs")
                        put(w2[MID:P, 1:2], "w2_vv1")
                        for n in range(2):
                            put(w2[n * SC:n * SC + VC, 2:3], "w2_vs")
                            put(w2[n * SC + VC:(n + 1) * SC, 2:3], "w2_vv1")

                        def step(i, s, r):
                            if live(i, NG):
                                at_least(sp, joined[s], 16 * TG * r)
                                sp.dma_start(ends[s][:, 0:TG], A["src_groups"][ds(i * P, P), :]).then_inc(ends_loaded[s], 16)
                                sp.dma_start(ends[s][:, TG:2 * TG], A["dst_groups"][ds(i * P, P), :]).then_inc(ends_loaded[s], 16)
                            k = i - 2
                            if live(k, NG):
                                at_least(sp, weighed, k - 1)
                                sp.dma_start(ea[s % 2][:, :], A["edge_attr_16_T"][:, ds(k * GE, GE)]).then_inc(ea_loaded[s % 2], 16)
                            k = i - 4
                            if live(k, NG):
                                at_least(sp, read1, k * 5 + 5)
                                sp.dma_start(scores_T[:, ds(k * GE, GE)], score[s % 2][:, :]).then_inc(scores_stored[s % 2], 16)
                            k = i - 7
                            if live(k, NG):
                                gate(sp, (w_zeroed, 5),
                                     (made3, (k + 1) * K3),
                                     (values_out, k + 1))
                                sp.dma_start(messages[ds(k * GE, GE), :].rearrange("(t p) f -> p t f", p=P),
                                             rows[(s + 1) % U][:, :, :, :].rearrange("p t h f -> p t (h f)")).then_inc(stored[(s + 1) % U], 16)

                        steps(sp, NG, 7, step, warm=8, unroll=U)
                        for s in range(U):
                            sp.wait_ge(stored[s], 16 * NG // U)
                        for s in range(2):
                            sp.wait_ge(scores_stored[s], 16 * NG // 2)

                    @block.gpsimd
                    def _(pool):
                        def step(i, s, r):
                            if live(i, NG):
                                gate(pool, (w_loaded, 16 * N_LOAD),
                                     (ends_loaded[s], 32 * (r + 1)),
                                     (made1, (i - 3) * K1))
                                for t in range(TG):
                                    pool.indirect_dma_start(g[s][:, t, :], None, table[2],
                                                            bass.IndirectOffsetOnAxis(ends[s][:, t:t + 1], 0)).then_inc(fetched[s], 16)
                            if live(i - 1, NG):
                                s1, r1 = back(s, r, 1, U)
                                gate(pool, (w_loaded, 16 * N_LOAD),
                                     (fetched[s1], 16 * TG * (r1 + 1)))
                                for t in range(TG):
                                    pool.indirect_dma_start(g[s1][:, t, :], None, table[3],
                                                            bass.IndirectOffsetOnAxis(ends[s1][:, TG + t:TG + t + 1], 0),
                                                            compute_op=ALU.add).then_inc(joined[s1], 16)

                        steps(pool, NG, 1, step, warm=8, unroll=U)

                    @block.tensor
                    def _(pe):
                        def weigh(i, s, r):
                            at_least(pe, made1, i * K1)
                            at_least(pe, ea_loaded[s % 2], 16 * (r * 2 + s // 2 + 1))
                            for t in range(TG):
                                ins = nc.tensor.matmul(w_ps[:, t, 0:WW], ea[s % 2][:, t * P:(t + 1) * P], w_rbf[:, :])
                            ins.then_inc(weighed, 1)

                        def transpose(f, part, bank):
                            at, width = PARTS[part]
                            for t in range(TG):
                                ins = nc.tensor.transpose(turn[bank][0:width, t * P:(t + 1) * P], f[:, t, at:at + width], ident[:, :])
                            return ins

                        pe.wait_ge(w_loaded, 16 * N_LOAD)
                        pe.wait_ge(w_zeroed, 6)
                        nc.tensor.matmul(turn[0][0:MID, 0:VC], w_val_T[:, :], w_gate[:, :]).then_inc(w_prod, 1)
                        pe.wait_ge(w_made, 9)
                        weigh(0, 0, 0)

                        def step(i, s, r):
                            k = i - 2
                            both = live(k, NG)
                            f2 = feat[2 + s % 2]
                            if both:
                                at_least(pe, made2, (k + 1) * K2)
                                at_least(pe, y0_done, k + 1)
                                at_least(pe, read1, (i - 1) * 5 + 4 if live(i - 1, NG) else NG * 5)
                                transpose(f2, 0, 1).then_inc(turned2, 1)
                            if live(i, NG) and live(i + 1, NG):
                                weigh(i + 1, (s + 1) % U, r + (s + 1) // U)
                            if both:
                                at_least(pe, read1, i * 5 if live(i - 1, NG) else NG * 5)
                                transpose(f2, 1, 0).then_inc(turned2, 1)
                                at_least(pe, read2, k * 3 + 1)
                                transpose(f2, 2, 1).then_inc(turned2, 1)
                            if live(i, NG):
                                at_least(pe, made1, (i + 1) * K1)
                                at_least(pe, read1, i * 5)
                                at_least(pe, read2, k * 3 + 2)
                                if isinstance(i, int) and i == 4:
                                    warm_up(turn[0])
                                transpose(feat[s % 2], 0, 0).then_inc(turned1, 1)
                            if both:
                                at_least(pe, read2, k * 3 + 3)
                                at_least(pe, made3, k * K3)
                                at_least(pe, values_out, k)
                                for t in range(TG):
                                    e = slice(t * P, (t + 1) * P)
                                    nc.tensor.matmul(o2[:, t, 0:SC], feat_T[1][0:MID, 0, e], w_o2s[:, :])
                                    nc.tensor.matmul(o2[:, t, Q2:PV2 + VC], feat_T[1][:, 1, e], w_o2v[0][:, :])
                                    ins = nc.tensor.matmul(o2[:, t, PV2 + VC:O2W], feat_T[1][:, 2, e], w_o2v[1][:, :])
                                ins.then_inc(mapped2, 1)
                            if live(i, NG):
                                transpose(feat[s % 2], 1, 1).then_inc(turned1, 1)
                                at_least(pe, read1, i * 5 + 1)
                                transpose(feat[s % 2], 2, 0).then_inc(turned1, 1)
                                at_least(pe, made2, (i - 1) * K2 + 2)
                                at_least(pe, gated, i * 2)
                                tiles = [slice(t * P, (t + 1) * P) for t in range(TG)]
                                for t, e in enumerate(tiles):
                                    nc.tensor.matmul(o1[:, t, 0:MID], feat_T[0][0:MID, 0, e], w_o1s[:, :])
                                at_least(pe, read1, i * 5 + 2)
                                nc.tensor.matmul(turn[1][:, :], w_att[:, :], feat_T[0][0:MID, 0, :]).then_inc(turned1, 1)
                                at_least(pe, read1, i * 5 + 3)
                                for t, e in enumerate(tiles):
                                    nc.tensor.matmul(o1[:, t, Q:PV + VC], feat_T[0][:, 1, e], w_o1v[0][:, :])
                                    ins = nc.tensor.matmul(o1[:, t, PV + VC:O1W], feat_T[0][:, 2, e], w_o1v[1][:, :])
                                ins.then_inc(mapped1, 1)
                                at_least(pe, read1, i * 5 + 4)
                                nc.tensor.matmul(turn[0][0:HEADS, :], w_dot[:, :], act_T[:, :]).then_inc(turned1, 1)

                        steps(pe, NG - 1, 3, step, warm=8, unroll=U)

                    @block.scalar
                    def _(act):
                        def scale_rows(i, s, r):
                            gate(act, (w_made, 9),
                                 (made1, (i - 1) * K1),
                                 (joined[s], 16 * TG * (r + 1)))
                            for t in range(TG):
                                ins = nc.scalar.activation(gy[s % 2][:, t, :], g[s][:, t, :], ACT.Copy, scale=y0_of(i, t))
                            ins.then_inc(scaled, 1)

                        def y0_of(i, t):
                            return y4[:, ds((i * TG + t) * 4, 1)]

                        scale_rows(0, 0, 0)

                        def turn_out(n, part, bank, count):
                            width = PARTS[part][1]
                            nc.scalar.activation(feat_T[n][0:width, part, :], turn[bank][0:width, :], ACT.Copy).then_inc(count, 1)

                        def step(i, s, r):
                            k = i - 2
                            if live(k, NG):
                                at_least(act, mapped2, k)
                                for part in range(3):
                                    at_least(act, turned2, k * 3 + part + 1)
                                    turn_out(1, part, 1 - part % 2, read2)
                            if live(i, NG):
                                at_least(act, mapped1, i)
                                at_least(act, turned1, i * 5 + 1)
                                turn_out(0, 0, 0, read1)
                            if live(i + 1, NG):
                                scale_rows(i + 1, (s + 1) % U, r + (s + 1) // U)
                            if live(i, NG):
                                for part in range(1, 3):
                                    at_least(act, turned1, i * 5 + part + 1)
                                    turn_out(0, part, part % 2, read1)
                                at_least(act, turned1, i * 5 + 4)
                                nc.scalar.activation(act_T[:, :], turn[1][:, :], ACT.Relu).then_inc(read1, 1)
                            if live(k, NG):
                                s2, r2 = back(s, r, 2, U)
                                at_least(act, mapped2, k + 1)
                                at_least(act, stored[s2], 16 * r2)
                                nc.scalar.activation(rows[s2][:, :, :, 0:HS], o2[:, :, 0:SC].rearrange("p t (h f) -> p t h f", h=HEADS),
                                                     ACT.Copy).then_inc(values_out, 1)
                            if live(i - 1, NG):
                                s1, _ = back(s, r, 1, U)
                                gate(act, (w_made, 9),
                                     (made2, (i - 1) * K2 + 3))
                                for t in range(TG):
                                    ins = nc.scalar.activation(pairs_of(feat[2 + s1 % 2], 0)[:, t, :, :], vec2[2][:, t, :, :], ACT.Copy,
                                                               scale=y0_of(i - 1, t))
                                ins.then_inc(y0_done, 1)
                            if live(i, NG):
                                f = feat[2 + s % 2]
                                at_least(act, mapped1, i + 1)
                                at_least(act, turned2, (i - 1) * 3)
                                nc.scalar.activation(f[:, :, MID:MID + SC], o1[:, :, 0:SC], ACT.Sigmoid).then_inc(gated, 1)
                                at_least(act, made2, (i - 2) * K2 + 3)
                                nc.scalar.activation(gate_s[s % 2][:, :, :], o1[:, :, GATE:Q], ACT.Sigmoid).then_inc(gated, 1)
                                at_least(act, turned1, i * 5 + 5)
                                at_least(act, scores_stored[s % 2], 16 * (r * 2 + s // 2))
                                nc.scalar.activation(score[s % 2][:, :], turn[0][0:HEADS, :], ACT.Copy).then_inc(read1, 1)
                                gate(act, (w_made, 9), (gated, i * 2 + 1))
                                for t in range(TG):
                                    nc.scalar.activation(f[:, t, 0:SC], f[:, t, MID:MID + SC], ACT.Copy, scale=y0_of(i, t))

                        steps(act, NG - 1, 3, step, warm=8, unroll=U)

                    @block.vector
                    def _(dve):
                        for a in (w_dot, *w_o1v, *w_o2v):
                            nc.vector.memset(a[:, :], 0.0).then_inc(w_zeroed, 1)
                        dve.wait_ge(w_loaded, 16 * N_LOAD)
                        nc.vector.tensor_scalar(w_dot[SC:2 * SC, :], w_dot[SC:2 * SC, :], -0.2, None, ALU.mult).then_inc(w_zeroed, 1)
                        dots = row_scale[0:MID, 0:1]
                        nc.vector.tensor_scalar(w_att[:, 0:SC], w_att[:, 0:SC], dots, None, ALU.mult).then_inc(w_made, 1)
                        nc.vector.tensor_scalar(w_att[:, SC:2 * SC], w_att[:, SC:2 * SC], dots, -1.0, ALU.mult, ALU.mult).then_inc(w_made, 1)
                        dve.wait_ge(w_prod, 1)
                        nc.vector.tensor_scalar(w_o1s[:, SC:MID], turn[0][0:MID, 0:VC], dots, None, ALU.mult).then_inc(w_made, 1)
                        nc.vector.tensor_scalar(w_o1s[:, 0:SC], w_o1s[:, 0:SC], dots, None, ALU.mult).then_inc(w_made, 1)
                        nc.vector.tensor_scalar(w_o2s[:, :], w_o2s[:, :], dots, w2[0:MID, 0:1], ALU.mult, ALU.mult).then_inc(w_made, 1)
                        for n in range(2):
                            cross = row_scale[:, 1 + n:2 + n]
                            nc.vector.tensor_scalar(w_o1v[n][:, :], w_o1v[n][:, :], cross, None, ALU.mult).then_inc(w_made, 1)
                            nc.vector.tensor_scalar(w_o2v[n][:, :], w_o2v[n][:, :], cross, w2[:, 1 + n:2 + n], ALU.mult, ALU.mult).then_inc(w_made, 1)

                        dve.wait_ge(y_loaded, 16)

                        def y_of(i):
                            return y_all[:, ds(i * (TG * YC), TG * YC)].rearrange("p (t c) -> p t c", c=YC)

                        def xyz(yy, lo, hi, width):
                            return yy[:, :, lo:hi].unsqueeze(3).to_broadcast([P, TG, hi - lo, width])

                        def tt(out, a, b, op, count):
                            nc.vector.tensor_tensor(out, a, b, op).then_inc(count, 1)

                        def cross_parts(v, yy, count):
                            tt(p1[:, :, 0:2, :], v[:, :, 1:3, :], xyz(yy, 3, 5, VC), ALU.mult, count)
                            tt(p1[:, :, 2:3, :], v[:, :, 0:1, :], xyz(yy, 5, 6, VC), ALU.mult, count)
                            tt(p2[:, :, 0:1, :], v[:, :, 2:3, :], xyz(yy, 2, 3, VC), ALU.mult, count)
                            tt(p2[:, :, 1:3, :], v[:, :, 0:2, :], xyz(yy, 3, 5, VC), ALU.mult, count)

                        def first(i, s, r):
                            k = i * K1
                            f, yy, w = feat[s % 2], y_of(i), w_ps
                            sca, vec = g[s][:, :, 0:SC], g[s][:, :, SC:FEAT].rearrange("p t (c u) -> p t c u", c=XYZ)
                            sca0, vec0 = gy[s % 2][:, :, 0:SC], gy[s % 2][:, :, SC:FEAT].rearrange("p t (c u) -> p t c u", c=XYZ)
                            at_least(dve, made1, k)
                            at_least(dve, made2, (i - 1) * K2)
                            at_least(dve, joined[s], 16 * TG * (r + 1))
                            tt(vy[:, :, :, :], vec, xyz(yy, 1, 4, VC), ALU.mult, made1)
                            cross_parts(vec, yy, made1)
                            dve.wait_ge(made1, k + 1)
                            tt(dot[:, :, :], vy[:, :, 0, :], vy[:, :, 1, :], ALU.add, made1)
                            at_least(dve, weighed, i + 1)
                            at_least(dve, turned1, (i - 2) * 5 + 3)
                            tt(f[:, :, MID:MID + SC], w[:, :, SC:2 * SC], sca, ALU.mult, made1)
                            dve.wait_ge(made1, k + 6)
                            tt(p1[:, :, :, :], p1[:, :, :, :], p2[:, :, :, :], ALU.subtract, made1)
                            tt(dot[:, :, :], dot[:, :, :], vy[:, :, 2, :], ALU.add, made1)
                            at_least(dve, scaled, i + 1)
                            tt(f[:, :, 0:SC], w[:, :, 0:SC], sca0, ALU.mult, made1)
                            tt(pairs_of(f, 0), vec0, w[:, :, VS:VV0].unsqueeze(2).to_broadcast([P, TG, XYZ, VC]), ALU.mult, made1)
                            dve.wait_ge(made1, k + 9)
                            tt(f[:, :, SC:MID], w[:, :, VV0:VV1], dot[:, :, :], ALU.mult, made1)
                            tt(pairs_of(f, VC), p1[:, :, :, :], w[:, :, VV1:WW].unsqueeze(2).to_broadcast([P, TG, XYZ, VC]), ALU.mult, made1)

                        def second(i, s, r):
                            k = i * K2
                            f, yy = feat[2 + s % 2], y_of(i)
                            v = vec2[2]
                            at_least(dve, made2, k)
                            at_least(dve, gated, (i + 1) * 2)
                            tt(vec2[0][:, :, :, :], o1[:, :, Q:PV].unsqueeze(2).to_broadcast([P, TG, XYZ, VC]), xyz(yy, 1, 4, VC), ALU.mult, made2)
                            dve.wait_ge(made2, k + 1)
                            tt(vec2[1][:, :, :, :], vec2[0][:, :, :, :], o1[:, :, PV:O1W].rearrange("p t (c u) -> p t c u", c=XYZ), ALU.add, made2)
                            at_least(dve, y0_done, i)
                            dve.wait_ge(made2, k + 2)
                            tt(v[:, :, :, :], vec2[1][:, :, :, :], gate_s[s % 2][:, :, :].unsqueeze(2).to_broadcast([P, TG, XYZ, VC]), ALU.mult, made2)
                            dve.wait_ge(made2, k + 3)
                            tt(vy[:, :, :, :], v[:, :, :, :], xyz(yy, 1, 4, VC), ALU.mult, made2)
                            cross_parts(v, yy, made2)
                            dve.wait_ge(made2, k + 4)
                            tt(dot[:, :, :], vy[:, :, 0, :], vy[:, :, 1, :], ALU.add, made2)
                            at_least(dve, turned2, (i - 1) * 3)
                            dve.wait_ge(made2, k + 9)
                            tt(pairs_of(f, VC), p1[:, :, :, :], p2[:, :, :, :], ALU.subtract, made2)
                            tt(f[:, :, SC:MID], dot[:, :, :], vy[:, :, 2, :], ALU.add, made2)

                        def message(i, s, r):
                            k = i * K3
                            yy = y_of(i)
                            at_least(dve, made3, k)
                            at_least(dve, values_out, i + 1)
                            tt(qy[:, :, :, :], o2[:, :, Q2:PV2].unsqueeze(2).to_broadcast([P, TG, XYZ, VC]), xyz(yy, 1, 4, VC), ALU.mult, made3)
                            at_least(dve, stored[s], 16 * r)
                            dve.wait_ge(made3, k + 1)
                            for c in range(XYZ):
                                lo = HS + c * HV
                                tt(rows[s][:, :, :, lo:lo + HV], qy[:, :, c, :].rearrange("p t (h a) -> p t h a", h=HEADS),
                                   o2[:, :, PV2 + c * VC:PV2 + (c + 1) * VC].rearrange("p t (h a) -> p t h a", h=HEADS), ALU.add, made3)

                        def step(i, s, r):
                            if live(i, NG):
                                first(i, s, r)
                            if live(i - 3, NG):
                                s3, r3 = back(s, r, 3, U)
                                message(i - 3, s3, r3)
                            if live(i - 1, NG):
                                s1, r1 = back(s, r, 1, U)
                                at_least(dve, made1, ((i + 1) if live(i, NG) else NG) * K1)
                                second(i - 1, s1, r1)

                        steps(dve, NG, 3, step, warm=8, unroll=U)

        def softmax_pass():
            with ExitStack() as ctx:
                big = [sums_T[:, n * (CHUNK + 2):(n + 1) * (CHUNK + 2)] for n in range(6)]
                score, fwd, bwd = (big[n][:, 0:CHUNK] for n in (0, 2, 3))
                dst_i = big[4].bitcast(I32)
                dst_f = big[5]
                pen = big[1][:, 0:CHUNK + 1]
                ends_i = sbuf(ctx, "soft_ends_i", [HEADS, 2, CHUNKS], I32)
                ends_f = sbuf(ctx, "soft_ends_f", [HEADS, 2, CHUNKS])
                pen_c = sbuf(ctx, "soft_pen_c", [HEADS, 2, CHUNKS])
                state = sbuf(ctx, "soft_state", [HEADS, 2, CHUNKS])
                carry = sbuf(ctx, "soft_carry", [HEADS, 2, CHUNKS + 1])
                start = sbuf(ctx, "soft_start", [P, 2])
                loaded = sem(ctx, "soft_loaded")
                done = sem(ctx, "soft_done")
                moved = sem(ctx, "soft_moved")
                exped = sem(ctx, "soft_exped")
                stored = sem(ctx, "soft_stored")
                line = A["dst_line"]
                flat_in = scores_T.rearrange("h (k n) -> (h k) n", n=CHUNK)
                flat_out = exps_T.rearrange("h (k n) -> (h k) n", n=CHUNK)
                ENDS, CARRIES = [10, 13], [11, 14]

                with nc.Block() as block:

                    @block.sync
                    def _(sp):
                        with nc.allow_non_contiguous_dma(reason="the nodes at the chunks' ends, once"):
                            for h in range(HEADS):
                                src = bass.AP(line.tensor, line.offset, [[CHUNK, CHUNKS], [1, CHUNK + 2]])
                                sp.dma_start(dst_i[h * CHUNKS:(h + 1) * CHUNKS, :], src).then_inc(loaded, 16)
                                for n in range(2):
                                    ends = bass.AP(line.tensor, line.offset + (CHUNK if n else 1), [[1, 1], [CHUNK, CHUNKS]])
                                    sp.dma_start(ends_i[h:h + 1, n, :], ends).then_inc(loaded, 16)
                            sp.dma_start(score, flat_in).then_inc(loaded, 16)
                            for n, last in enumerate((fwd[:, CHUNK - 1:CHUNK], bwd[:, 0:1])):
                                sp.wait_ge(done, ENDS[n])
                                sp.dma_start(chunk_ends[n, :].unsqueeze(1), last).then_inc(moved, 16)
                                sp.wait_ge(moved, 64 * n + 16)
                                sp.dma_start(state[:, n, :], chunk_ends[n, :].rearrange("(h k) -> h k", h=HEADS)).then_inc(moved, 16)
                                sp.wait_ge(done, CARRIES[n])
                                sp.dma_start(chunk_carries[n, :].rearrange("(h k) -> h k", h=HEADS), carry[:, n, n:n + CHUNKS]).then_inc(moved, 16)
                                sp.wait_ge(moved, 64 * n + 48)
                                sp.dma_start(start[:, n:n + 1], chunk_carries[n, :].unsqueeze(1)).then_inc(moved, 16)
                        sp.wait_ge(exped, 1)
                        sp.dma_start(flat_out, score).then_inc(stored, 16)
                        sp.wait_ge(stored, 16)

                    @block.vector
                    def _(dve):
                        count = [0]

                        def then(ins):
                            count[0] += 1
                            ins.then_inc(done, 1)
                            dve.wait_ge(done, count[0])

                        def scan(out, p, v, initial):
                            return nc.vector.tensor_tensor_scan(out, p, v, initial, ALU.add, ALU.max)

                        dve.wait_ge(loaded, 16 * (3 * HEADS + 1))
                        then(nc.vector.tensor_copy(dst_f, dst_i))
                        then(nc.vector.tensor_copy(ends_f[:, :, :], ends_i[:, :, :]))
                        then(nc.vector.tensor_tensor(pen, dst_f[:, 1:CHUNK + 2], dst_f[:, 0:CHUNK + 1], ALU.not_equal))
                        then(nc.vector.tensor_scalar(pen, pen, LOWEST, None, ALU.mult))
                        then(nc.vector.memset(carry[:, :, :], LOWEST))
                        then(nc.vector.memset(pen_c[:, :, :], 0.0))
                        then(nc.vector.tensor_tensor(pen_c[:, 0, 1:CHUNKS], ends_f[:, 1, 0:CHUNKS - 1], ends_f[:, 1, 1:CHUNKS], ALU.not_equal))
                        then(nc.vector.tensor_tensor(pen_c[:, 1, 0:CHUNKS - 1], ends_f[:, 0, 0:CHUNKS - 1], ends_f[:, 0, 1:CHUNKS], ALU.not_equal))
                        then(nc.vector.tensor_scalar(pen_c[:, :, :], pen_c[:, :, :], LOWEST, None, ALU.mult))
                        then(scan(fwd, pen[:, 0:CHUNK], score, LOWEST))
                        dve.wait_ge(moved, 32)
                        then(scan(carry[:, 0, 1:CHUNKS + 1], pen_c[:, 0, :], state[:, 0, :], LOWEST))
                        dve.wait_ge(moved, 64)
                        then(scan(fwd, pen[:, 0:CHUNK], score, start[:, 0:1]))
                        back_pen, back_fwd, back_out = pen[:, 1:CHUNK + 1][:, ::-1], fwd[:, ::-1], bwd[:, ::-1]
                        then(scan(back_out, back_pen, back_fwd, LOWEST))
                        dve.wait_ge(moved, 96)
                        then(scan(carry[:, 1, 0:CHUNKS][:, ::-1], pen_c[:, 1, :][:, ::-1], state[:, 1, :][:, ::-1], LOWEST))
                        dve.wait_ge(moved, 128)
                        then(scan(back_out, back_pen, back_fwd, start[:, 1:2]))
                        then(nc.vector.tensor_tensor(score, score, bwd, ALU.subtract))

                    @block.scalar
                    def _(act):
                        act.wait_ge(done, 16)
                        nc.scalar.activation(score, score, ACT.Exp).then_inc(exped, 1)

        def spread_exps():
            J = P // HEADS
            BLOCKS, REST = divmod(NG * TG, J)
            with ExitStack() as ctx:
                rows = sbuf(ctx, "spread_rows", [P, (BLOCKS + 1) * P])
                ps = [psum(ctx, f"spread_ps{s}", [P, 512]) for s in range(2)]
                zeroed = sem(ctx, "spread_zeroed")
                loaded = sem(ctx, "spread_loaded")
                turned = sem(ctx, "spread_turned")
                copied = sem(ctx, "spread_copied")

                with nc.Block() as block:

                    @block.sync
                    def _(sp):
                        for h in range(HEADS):
                            sp.dma_start(rows[h * J:(h + 1) * J, 0:BLOCKS * P].rearrange("j (b e) -> j b e", e=P),
                                         exps_T[h, 0:BLOCKS * J * P].rearrange("(b j e) -> j b e", j=J, e=P)).then_inc(loaded, 16)
                        sp.wait_ge(zeroed, 1)
                        for h in range(HEADS):
                            sp.dma_start(rows[h * J:h * J + REST, BLOCKS * P:],
                                         exps_T[h, BLOCKS * J * P:].rearrange("(j e) -> j e", e=P)).then_inc(loaded, 16)

                    @block.vector
                    def _(dve):
                        nc.vector.memset(rows[:, BLOCKS * P:], 0.0).then_inc(zeroed, 1)

                    @block.tensor
                    def _(pe):
                        pe.wait_ge(loaded, 2 * HEADS * 16)

                        for b in range(BLOCKS + 1):
                            at_least(pe, copied, b - 1)
                            nc.tensor.transpose(ps[b % 2][:, 0:P], rows[:, b * P:(b + 1) * P], ident[:, :]).then_inc(turned, 1)

                    @block.scalar
                    def _(act):
                        def step(b, s, r, tiles=J):
                            at_least(act, turned, b + 1)
                            nc.scalar.activation(exps[:, ds(b * J * HEADS, tiles * HEADS)].rearrange("p (j h) -> p h j", h=HEADS),
                                                 ps[s][:, 0:P].rearrange("p (h j) -> p h j", h=HEADS)[:, :, 0:tiles], ACT.Copy).then_inc(copied, 1)

                        steps(act, BLOCKS, 0, step)
                        step(BLOCKS, BLOCKS % 2, 0, REST)

        def gather_messages(tag, first):
            BW = 2 * HF + HEADS
            K = 3
            U = 4
            with ExitStack() as ctx:
                msg = [sbuf(ctx, f"{tag}sum_msg{s}", [P, TG, FEAT]) for s in range(U)]
                prod = [sbuf(ctx, f"{tag}sum_prod{s}", [P, TG, 2, BW]) for s in range(2)]
                hot = [sbuf(ctx, f"{tag}sum_hot{s}", [P, TG, WIN]) for s in range(2)]
                spare_ps = psum(ctx, f"{tag}sum_spare_ps", [P, 512])
                spare = sbuf(ctx, f"{tag}sum_spare", [1, 2])
                win_ps = [psum(ctx, f"{tag}sum_win_ps{s}", [P, 512]) for s in range(2)]
                zeroed = sem(ctx, f"{tag}sum_zeroed")
                placed = sem(ctx, f"{tag}sum_placed")
                msg_loaded = [sem(ctx, f"{tag}sum_msg_loaded{s}") for s in range(U)]
                made = sem(ctx, f"{tag}sum_made")
                summed = sem(ctx, f"{tag}sum_summed")
                added = sem(ctx, f"{tag}sum_added")

                with nc.Block() as block:

                    @block.sync
                    def _(sp):
                        def step(i, s, r):
                            at_least(sp, made, (i - 3) * K)
                            sp.dma_start(msg[s][:, :, :], messages[ds(i * GE, GE), :].rearrange("(t p) f -> p t f", p=P)
                                         ).then_inc(msg_loaded[s], 16)

                        steps(sp, NG, 0, step, unroll=U)

                    @block.gpsimd
                    def _(pool):
                        for b in range(2):
                            if first:
                                nc.gpsimd.memset(sums_T[:, b * COLS:(b + 1) * COLS], 0.0).then_inc(zeroed, 1)
                            else:
                                nc.gpsimd.memset(spare[:, b:b + 1], 0.0).then_inc(zeroed, 1)

                    @block.tensor
                    def _(pe):
                        pe.wait_ge(zeroed, 1)

                        def step(i, s, r):
                            if isinstance(i, int) and i == 4:
                                warm_up(spare_ps)
                            if live(i - 1, NG):
                                s1 = (s - 1) % 2
                                at_least(pe, made, i * K)
                                at_least(pe, added, i - 2)
                                for b in range(2):
                                    for t in range(TG):
                                        ins = nc.tensor.matmul(win_ps[s1][0:BW, b * WIN:(b + 1) * WIN], prod[s1][:, t, b, :],
                                                               hot[s1][:, t, :], start=t == 0, stop=t == TG - 1)
                                ins.then_inc(summed, 1)

                        steps(pe, NG, 1, step, warm=8, unroll=U)

                    @block.scalar
                    def _(act):
                        act.wait_ge(zeroed, 2)

                    @block.vector
                    def _(dve):
                        place_windows(dve, first, placed)
                        dve.wait_ge(zeroed, 2)

                        def products(i, s, r):
                            at_least(dve, made, i * K)
                            at_least(dve, summed, i - 1)
                            nc.vector.tensor_tensor(hot[s % 2][:, :, :], iota_win[:, :].unsqueeze(1).to_broadcast([P, TG, WIN]),
                                                    dst_rel[:, ds(i * TG, TG)].unsqueeze(2).to_broadcast([P, TG, WIN]),
                                                    ALU.is_equal).then_inc(made, 1)
                            at_least(dve, msg_loaded[s], 16 * (r + 1))
                            e = exps[:, ds(i * TG * HEADS, TG * HEADS)].rearrange("p (k h) -> p k h", h=2)
                            nc.vector.tensor_tensor(prod[s % 2][:, :, :, 0:2 * HF].rearrange("p t b (h f) -> p (t b) h f", h=2),
                                                    msg[s][:, :, :].rearrange("p t (b h f) -> p (t b) h f", b=2, h=2),
                                                    e.unsqueeze(3).to_broadcast([P, 2 * TG, 2, HF]), ALU.mult).then_inc(made, 1)
                            e = exps[:, ds(i * TG * HEADS, TG * HEADS)].rearrange("p (t h) -> p t h", h=HEADS)
                            nc.vector.tensor_copy(prod[s % 2][:, :, :, 2 * HF:BW], e.unsqueeze(2).to_broadcast([P, TG, 2, HEADS])).then_inc(made, 1)

                        def step(i, s, r):
                            if live(i, NG):
                                products(i, s, r)
                            if live(i - 2, NG):
                                add_window(dve, i - 2, win_ps[s % 2], BW, 2, summed, added)

                        steps(dve, NG, 2, step, warm=8, unroll=U)

        def post_l2():
            BW, HB = 2 * HF + HEADS, 2 * HF
            N_LOAD = 2 * 2 * (1 + XYZ)
            with ExitStack() as ctx:
                w = sbuf(ctx, "l2_post_w", [HB, 2, FEAT])
                head_i = sbuf(ctx, "l2_post_head_i", [BW, 2, HB], I32)
                head = sbuf(ctx, "l2_post_head", [BW, 2, HB])
                inv = [sbuf(ctx, f"l2_post_inv{s}", [HB, 2, P]) for s in range(2)]
                sums = [sbuf(ctx, f"l2_post_sums{s}", [HB, 2, P]) for s in range(2)]
                den_ps = [psum(ctx, f"l2_post_den{s}", [P, 512]) for s in range(2)]
                ps = [psum(ctx, f"l2_post_ps{s}", [P, 512]) for s in range(2)]
                zeroed = sem(ctx, "l2_post_zeroed")
                w_loaded = sem(ctx, "l2_post_w_loaded")
                heads_ready = sem(ctx, "l2_post_heads_ready")
                spread = sem(ctx, "l2_post_spread")
                mapped = sem(ctx, "l2_post_mapped")
                ready = sem(ctx, "l2_post_ready")
                fin = sem(ctx, "l2_post_fin")

                with nc.Block() as block:

                    @block.sync
                    def _(sp):
                        sp.wait_ge(zeroed, 3)
                        for b in range(2):
                            for k in range(2):
                                h, at = 2 * b + k, k * HF
                                sp.dma_start(w[at:at + HS, b, 0:SC], A["L2_gnn_Wps"][h * HS:(h + 1) * HS, :]).then_inc(w_loaded, 16)
                                for c in range(XYZ):
                                    lo = at + HS + c * HV
                                    sp.dma_start(w[lo:lo + HV, b, SC + c * VC:SC + (c + 1) * VC],
                                                 A["L2_gnn_Wpv"][h * HV:(h + 1) * HV, :]).then_inc(w_loaded, 16)

                    @block.gpsimd
                    def _(pool):
                        for b in range(2):
                            nc.gpsimd.iota(head_i[:, b, :].rearrange("p (h f) -> p h f", h=2), pattern=[[-1, 2], [0, HF]],
                                           base=-HB - 2 * b, channel_multiplier=1).then_inc(zeroed, 1)

                    @block.tensor
                    def _(pe):
                        pe.wait_ge(heads_ready, 1)
                        pe.wait_ge(w_loaded, 16 * N_LOAD)

                        def step(i, s, r):
                            if live(i, NT):
                                gate(pe, (heads_ready, 1), (ready, (i - 2) * 3 + 1))
                                for b in range(2):
                                    ins = nc.tensor.matmul(den_ps[s][0:HB, b * P:(b + 1) * P], head[:, b, :], sums4[0:BW, b, ds(i * P, P)])
                                ins.then_inc(spread, 1)
                            if live(i - 1, NT):
                                s1, _ = back(s, r, 1)
                                at_least(pe, fin, (i - 2) * 2)
                                at_least(pe, ready, i * 3)
                                for b in range(2):
                                    ins = nc.tensor.matmul(ps[s1][:, 0:FEAT], sums[s1][:, b, :], w[:, b, :], start=b == 0, stop=b == 1)
                                ins.then_inc(mapped, 1)

                        steps(pe, NT, 1, step)

                    @block.vector
                    def _(dve):
                        dve.wait_ge(zeroed, 2)
                        nc.vector.memset(w[:, :, :], 0.0).then_inc(zeroed, 1)
                        nc.vector.tensor_scalar(head[:, :, :], head_i[:, :, :], 0.0, None, ALU.is_equal).then_inc(heads_ready, 1)

                        def step(i, s, r):
                            if live(i, NT):
                                k = i * 3
                                at_least(dve, ready, k)
                                at_least(dve, spread, i + 1)
                                nc.vector.tensor_scalar(inv[s][:, :, :], den_ps[s][0:HB, 0:2 * P].rearrange("p (b n) -> p b n", b=2),
                                                        1e-16, None, ALU.add).then_inc(ready, 1)
                                dve.wait_ge(ready, k + 1)
                                nc.vector.reciprocal(inv[s][:, :, :], inv[s][:, :, :]).then_inc(ready, 1)
                                dve.wait_ge(ready, k + 2)
                                at_least(dve, mapped, i - 1)
                                nc.vector.tensor_tensor(sums[s][:, :, :], sums4[0:HB, 0:2, ds(i * P, P)], inv[s][:, :, :], ALU.mult).then_inc(ready, 1)
                            if live(i - 1, NT):
                                t = i - 1
                                s1 = (s - 1) % 2
                                at_least(dve, mapped, i)
                                nc.vector.tensor_tensor(xs_at(t), xs_at(t), ps[s1][:, 0:SC], ALU.add).then_inc(fin, 1)
                                nc.vector.tensor_tensor(xv_at(t), xv_at(t), by_component(ps[s1][:, SC:FEAT]), ALU.add).then_inc(fin, 1)

                        steps(dve, NT, 1, step)

        def layer_2():
            node_pass("l2", ["L2_gnn_Ws_src", "L2_gnn_Ws_dst"], ["L2_gnn_Wv_src", "L2_gnn_Wv_dst"], [table[2], table[3]], finish_l2, 4,
                      gamma=("L2_gnn_gamma_s", "L2_gnn_beta_s", "L2_gnn_gamma_v"))
            attention_pass()
            softmax_pass()
            spread_exps()
            all_windows(gather_messages)
            post_l2()

        def store_x():
            with ExitStack() as ctx:
                stored = sem(ctx, "result_stored")
                full = NODES // P
                with nc.Block() as block:

                    @block.sync
                    def _(sp):
                        sp.dma_start(out[0:full * P, :].rearrange("(t p) f -> p t f", p=P), x3[:, 0:full, :]).then_inc(stored, 16)
                        sp.dma_start(out[full * P:NODES, :], x3[0:NODES - full * P, full, :]).then_inc(stored, 16)
                        sp.wait_ge(stored, 32)

        import math
        c_self = math.sin(math.pi / 8)
        setup()
        norm_all("l0", False)
        node_pass("l0", ["L0_gnn_Wl1_0", "L0_gnn_Wsc0"], ["L0_gnn_Wl1_1", "L0_gnn_Wsc1"], [table[0]], finish_l0, 4,
                  [(0, SC ** -0.5), (0, VC ** -0.5)])
        all_windows(lambda tag, first: edge_pass(
            tag + "l0", first, table[0], "edge_attr_8_T", "L0_gnn_Wfc1", "L0_gnn_Wfc2", "L0_gnn_Wfc3",
            ACT.Gelu_apprx_tanh, [8.0 ** -0.5, SC ** -0.5]))
        post_l0()
        norm_all("l1", False)
        node_pass("l1", ["L1_gnn_W1_s", "L1_gnn_W_sc_s"], ["L1_gnn_W1_v", "L1_gnn_W_sc_v"], [table[1], self_rows], finish_l1, 4,
                  [(0, SC ** -0.5), (0, VC ** -0.5)])
        all_windows(lambda tag, first: edge_pass(
            tag + "l1", first, table[1], "edge_attr_8_T", "L1_gnn_fcW1", None, "L1_gnn_fcW2", ACT.Silu, [8.0 ** -0.5]))
        post_l1()
        norm_all("l2", True)
        layer_2()
        norm_all("l3", False)
        node_pass("l3", ["L3_gnn_Ws_l1_a", "L3_gnn_Ws_l1_c", "L3_gnn_Ws_sc_a", "L3_gnn_Ws_sc_c"],
                  ["L3_gnn_Wv_l1_a", "L3_gnn_Wv_l1_c", "L3_gnn_Wv_sc_a", "L3_gnn_Wv_sc_c"], [table[4]], finish_l3, 8,
                  [(0, 1.0), (1, 1.0), (0, c_self), (1, c_self)])
        all_windows(lambda tag, first: edge_pass(
            tag + "l3", first, table[4], "edge_attr_10_T", "L3_gnn_W_fc1", None, "L3_gnn_W_fc2", ACT.Silu, [1.0]))
        post_l3()
        store_x()


def kernel(**inputs):
    import numpy as np
    import concourse.bacc as bacc
    from concourse import mybir
    from concourse.bass_utils import run_bass_kernel_spmd

    given = {n: np.asarray(v) for n, v in inputs.items()}

    def padded(a, rows, fill=0):
        return np.concatenate([a, np.full((rows - a.shape[0],) + a.shape[1:], fill, a.dtype)])

    def grouped(a):
        a = a.reshape((NG, TG, P) + a.shape[1:])
        a = np.moveaxis(a, 1, 2)
        return np.ascontiguousarray(a.reshape(NG * P, -1))

    src = padded(given.pop("src"), EPAD)
    dst = padded(given.pop("dst"), EPAD, NODES)
    y = padded(given.pop("edge_attr_4"), EPAD)
    arrays = {
        "x": padded(given.pop("x"), NPAD),
        "src_groups": grouped(src),
        "dst_groups": grouped(dst),
        "dst_tiles": dst.reshape(NG * TG, P).T,
        "dst_first": dst[::GE][None, :],
        "dst_last": dst[GE - 1::GE][None, :],
        "dst_line": np.concatenate([np.full(1, -1, np.int32), dst, np.full(1, NODES + 1, np.int32)])[None, :],
        "y_all": grouped(y[:, [0, 1, 2, 3, 1, 2]]).reshape(NG, P, TG * YC).transpose(1, 0, 2).reshape(P, -1),
        "y4": y.reshape(NG * TG, P, 4).transpose(1, 0, 2).reshape(P, -1),
    }
    for n, name in enumerate(["node_vec1", "node_vec1_n2", "node_vec1_n3"]):
        arrays[f"attr_{n}"] = padded(given.pop(name), NPAD).reshape(NT, P).T
    for name in ["edge_attr_8", "edge_attr_10", "edge_attr_16"]:
        arrays[f"{name}_T"] = padded(given.pop(name), EPAD).T
    for name, a in given.items():
        arrays[name] = a[:, None] if a.ndim == 1 else a.reshape(-1, 1) if a.ndim == 3 else a
    for name in ["L3_gnn_Ws_l2_a", "L3_gnn_Ws_l2_c", "L3_gnn_Wv_l2_a", "L3_gnn_Wv_l2_c", "L2_gnn_Ws_val"]:
        arrays[f"{name}_T"] = given[name].T
    arrays = {f"in_{n}": np.ascontiguousarray(a) for n, a in arrays.items()}

    nc = bacc.Bacc("TRN2", target_bir_lowering=False, num_devices=1)
    A = {n[3:]: nc.dram_tensor(n, a.shape, mybir.dt.from_np(a.dtype), kind="ExternalInput").ap() for n, a in arrays.items()}
    out = nc.dram_tensor("out", (NODES, FEAT), mybir.dt.float32, kind="ExternalOutput").ap()
    build(nc, A, out)
    return run_bass_kernel_spmd(nc, [arrays], core_ids=[0]).results[0]["out"]
```

```python
NODES, EDGES, FEAT = 6250, 100000, 160
P = 128
SC, VC, XYZ = 64, 32, 3
VF = VC * XYZ
NT = -(-NODES // P)
NPAD = NT * P
TG = 4
GE = TG * P
NG = 196
EPAD = NG * GE
EDGE_WIN, SUM_WIN = 40, 64
COLS = NPAD + SUM_WIN
MID = SC + VC
YC = 6
QUARTER = P // 4
HEADS, HS, HV = 4, 16, 8
HF = HS + XYZ * HV
CHUNKS = P // HEADS
CHUNK = EPAD // CHUNKS
EPS = 1e-5
LOWEST = -1.5e38


def build(nc, A, out):
    from contextlib import ExitStack

    import concourse.bass as bass
    from concourse import mybir

    F32, I32 = mybir.dt.float32, mybir.dt.int32
    ALU, ACT, AX = mybir.AluOpType, mybir.ActivationFunctionType, mybir.AxisListType
    ds = bass.ds

    def at_least(eng, sem, value):
        if isinstance(value, int) and value <= 0:
            return
        eng.wait_ge(sem, value)

    def gate(eng, settled, *waits):
        waits = [(sem, v if isinstance(v, int) else eng.to_reg(v)) for sem, v in waits if not isinstance(v, int) or v > 0]
        eng.wait_ge(*settled)
        for sem, v in waits:
            eng.wait_ge(sem, v)

    def steps(eng, n, lag, emit, warm=4, unroll=2):
        for i in range(warm):
            emit(i, i % unroll, i // unroll)
        turns = (n - warm) // unroll
        with eng.Fori(0, turns) as j:
            for k in range(unroll):
                emit(j * unroll + (warm + k), (warm + k) % unroll, j + (warm + k) // unroll)
        for i in range(warm + turns * unroll, n + lag):
            emit(i, i % unroll, i // unroll)

    def live(i, n):
        return not isinstance(i, int) or 0 <= i < n

    def back(s, r, lag, unroll=2):
        return (s - lag) % unroll, r + (s - lag) // unroll

    table = [nc.dram_tensor(f"node_table_{n}", (NPAD, FEAT), F32).ap() for n in range(5)]
    self_rows = nc.dram_tensor("l1_self_rows", (NPAD, FEAT), F32).ap()
    messages = nc.dram_tensor("l2_messages", (EPAD, FEAT), F32).ap()
    scores_T = nc.dram_tensor("l2_scores", (HEADS, EPAD), F32).ap()
    exps_T = nc.dram_tensor("l2_exps", (HEADS, EPAD), F32).ap()
    chunk_ends = nc.dram_tensor("l2_chunk_ends", (2, P), F32).ap()
    chunk_carries = nc.dram_tensor("l2_chunk_carries", (2, P), F32).ap()
    turn_row = nc.dram_tensor("l1_turn_row", (1, NPAD), F32).ap()

    whole = ExitStack()

    def sbuf(ctx, name, shape, dt=F32):
        return ctx.enter_context(nc.sbuf_tensor(name, shape, dt))

    def psum(ctx, name, shape):
        return ctx.enter_context(nc.psum_tensor(name, shape, F32))

    layer_sems = []

    def sem(ctx, name):
        layer_sems.append(nc.alloc_semaphore(name))
        return layer_sems[-1]

    def clear_sems(first, last):
        nc.clear_and_free_semaphores(layer_sems[first:last])
        del layer_sems[first:last]

    def all_windows(width, sums):
        sums("", True)
        widest = nc.values_load(span[0:1, 0:1], min_val=0, max_val=NODES)
        with nc.If(widest >= width):
            own = len(layer_sems)
            with nc.Fori(1, -(-NPAD // width)) as shift:
                with nc.If(widest >= shift * width):
                    sums("wide_", False)
                    clear_sems(own, len(layer_sems))
                    nc.all_engine_barrier()

    with whole:
        x = sbuf(whole, "x", [P, NT * FEAT])
        y4 = sbuf(whole, "y4", [P, NG * TG * 4])
        sums_T = sbuf(whole, "sums_T", [P, 4 * COLS])
        dst_rel = sbuf(whole, "dst_rel", [P, NG * TG])
        first_row = sbuf(whole, "first_row", [1, NG])
        span = sbuf(whole, "span", [1, 1], I32)
        window_row = sbuf(whole, "window_row", [1, NG], I32)
        iota_win = sbuf(whole, "iota_win", [P, SUM_WIN])
        iota_home = sbuf(whole, "iota_home", [P, SUM_WIN])
        ident = sbuf(whole, "ident", [P, P])
        attr = sbuf(whole, "attr", [P, 3, NT])
        row_scale = sbuf(whole, "row_scale", [P, 4])
        norm = sbuf(whole, "norm", [P, 3, NT])

        x3 = x[:, :].rearrange("p (t f) -> p t f", t=NT)
        sums4 = sums_T[:, :].rearrange("p (b n) -> p b n", b=4)
        h = sums_T[:, 0:NT * FEAT]
        exps = sums_T[:, 2 * COLS:2 * COLS + NG * TG * HEADS]

        def setup():
            with ExitStack() as ctx:
                dst_i = sbuf(ctx, "dst_i", [P, NG * TG], I32)
                dst_f = sbuf(ctx, "dst_f", [P, NG * TG])
                last_i = sbuf(ctx, "last_i", [1, NG], I32)
                span_f = sbuf(ctx, "span_f", [1, 2 * NG + 1])
                ones_row = sbuf(ctx, "ones_row", [1, P])
                iota_i = sbuf(ctx, "iota_i", [P, SUM_WIN], I32)
                diag_i = sbuf(ctx, "diag_i", [P, P], I32)
                first_ps = psum(ctx, "first_ps", [P, NG])
                loaded = sem(ctx, "setup_loaded")
                iotas = sem(ctx, "setup_iotas")
                firsts = sem(ctx, "setup_firsts")
                spread = sem(ctx, "setup_spread")
                made = sem(ctx, "setup_made")
                with nc.Block() as block:

                    @block.sync
                    def _(sp):
                        sp.dma_start(x3, A["x"].rearrange("(t p) f -> p t f", p=P)).then_inc(loaded, 16)
                        sp.dma_start(dst_i[:, :], A["dst_tiles"]).then_inc(loaded, 16)
                        sp.dma_start(window_row[:, :], A["dst_first"]).then_inc(loaded, 16)
                        sp.dma_start(last_i[:, :], A["dst_last"]).then_inc(loaded, 16)
                        sp.dma_start(y4[:, :], A["y4"]).then_inc(loaded, 16)
                        for n in range(3):
                            sp.dma_start(attr[:, n, :], A[f"attr_{n}"]).then_inc(loaded, 16)

                    @block.gpsimd
                    def _(pool):
                        nc.gpsimd.iota(iota_i[:, :], pattern=[[1, SUM_WIN]], base=0, channel_multiplier=0).then_inc(iotas, 1)
                        nc.gpsimd.iota(diag_i[:, :], pattern=[[1, P]], base=0, channel_multiplier=-1).then_inc(iotas, 1)

                    @block.vector
                    def _(dve):
                        nc.vector.memset(ones_row[:, :], 1.0).then_inc(made, 1)
                        nc.vector.memset(row_scale[:, :], 1.0).then_inc(made, 1)
                        dve.wait_ge(made, 2)
                        nc.vector.memset(row_scale[SC:MID, 0:1], 3.0 ** -0.5).then_inc(made, 1)
                        nc.vector.memset(row_scale[MID:P, 1:2], 2.0 ** -0.5).then_inc(made, 1)
                        nc.vector.memset(row_scale[VC:SC, 2:3], 2.0 ** -0.5).then_inc(made, 1)
                        nc.vector.memset(row_scale[MID:P, 2:3], 2.0 ** -0.5).then_inc(made, 1)
                        dve.wait_ge(iotas, 2)
                        nc.vector.tensor_copy(iota_win[:, :], iota_i[:, :]).then_inc(made, 1)
                        nc.vector.tensor_copy(iota_home[:, :], iota_i[:, :]).then_inc(made, 1)
                        nc.vector.tensor_scalar(ident[:, :], diag_i[:, :], 0.0, None, ALU.is_equal).then_inc(made, 1)
                        dve.wait_ge(loaded, 16 * 8)
                        nc.vector.tensor_copy(first_row[:, :], window_row[:, :]).then_inc(firsts, 1)
                        nc.vector.tensor_copy(dst_f[:, :], dst_i[:, :]).then_inc(made, 1)
                        nc.vector.tensor_copy(span_f[:, 0:NG], last_i[:, :]).then_inc(made, 1)
                        dve.wait_ge(made, 11)
                        dve.wait_ge(firsts, 1)
                        nc.vector.tensor_tensor(span_f[:, NG:2 * NG], span_f[:, 0:NG], first_row[:, :], ALU.subtract).then_inc(made, 1)
                        dve.wait_ge(made, 12)
                        nc.vector.tensor_reduce(span_f[:, 2 * NG:2 * NG + 1], span_f[:, NG:2 * NG], AX.X, ALU.max).then_inc(made, 1)
                        dve.wait_ge(made, 13)
                        nc.vector.tensor_copy(span[:, :], span_f[:, 2 * NG:2 * NG + 1]).then_inc(made, 1)
                        dve.wait_ge(spread, 1)
                        nc.vector.tensor_tensor(
                            dst_rel[:, :].rearrange("p (g t) -> p g t", t=TG),
                            dst_f[:, :].rearrange("p (g t) -> p g t", t=TG),
                            first_ps[:, :].unsqueeze(2).to_broadcast([P, NG, TG]),
                            ALU.subtract).then_inc(made, 1)

                    @block.tensor
                    def _(pe):
                        pe.wait_ge(made, 1)
                        pe.wait_ge(firsts, 1)
                        nc.tensor.matmul(first_ps[:, :], ones_row[:, :], first_row[:, :]).then_inc(spread, 1)

        def place_windows(dve, width, first, placed):
            if first:
                nc.vector.tensor_copy(iota_win[:, :], iota_home[:, :]).then_inc(placed, 1)
                nc.vector.tensor_copy(window_row[:, :], first_row[:, :]).then_inc(placed, 1)
            else:
                nc.vector.tensor_scalar(iota_win[:, :], iota_win[:, :], float(width), None, ALU.add).then_inc(placed, 1)
                nc.vector.tensor_scalar(window_row[:, :], window_row[:, :], float(width), float(NPAD), ALU.add, ALU.min).then_inc(placed, 1)
            dve.wait_ge(placed, 2)

        def norm_steps(ctx, tag, equivariant):
            stat = [sbuf(ctx, f"{tag}_stat{n}", [P, NT, 6]) for n in range(2)]
            part = sbuf(ctx, f"{tag}_stat_part", [P, 4, NT])
            root = sbuf(ctx, f"{tag}_stat_root", [P, 2, NT])
            rows_at = sem(ctx, f"{tag}_norm_rows")
            dve_at = sem(ctx, f"{tag}_norm_dve")
            h_at = sem(ctx, f"{tag}_norm_h")
            act_at = sem(ctx, f"{tag}_norm_act")
            added = sem(ctx, f"{tag}_norm_added")
            scale, bias, scale_v = (norm[:, n, :] for n in range(3))
            VAR, RMS = 6, 6
            H_READY = VAR + 2
            LAST = H_READY + VAR + 2 + RMS + 1 if equivariant else H_READY
            U = 7

            def dve_steps(dve):
                count = [0]

                def then(ins):
                    count[0] += 1
                    ins.then_inc(dve_at, 1)
                    dve.wait_ge(dve_at, count[0])

                def variance(st, width):
                    mean_e, sum_e, mean_o, sum_o = (st[:, :, n] for n in (1, 2, 4, 5))
                    then(nc.vector.tensor_tensor(part[:, 1, :], mean_e, mean_o, ALU.subtract))
                    then(nc.vector.tensor_tensor(part[:, 0, :], mean_e, mean_o, ALU.add))
                    then(nc.vector.scalar_tensor_tensor(part[:, 2, :], part[:, 1, :], width / 4, part[:, 1, :], ALU.mult, ALU.mult))
                    then(nc.vector.tensor_tensor(part[:, 3, :], sum_e, sum_o, ALU.add))
                    then(nc.vector.tensor_tensor(part[:, 3, :], part[:, 3, :], part[:, 2, :], ALU.add))
                    then(nc.vector.tensor_scalar(part[:, 3, :], part[:, 3, :], 1.0 / width, EPS, ALU.mult, ALU.add))

                def scale_and_bias():
                    then(nc.vector.reciprocal(scale, root[:, 0, :]))
                    then(nc.vector.scalar_tensor_tensor(bias, part[:, 0, :], -0.5, scale, ALU.mult, ALU.mult))

                def stats(i, s, r):
                    nc.vector.bn_stats(stat[0][:, ds(i, 1), :], x[:, ds(i * FEAT, FEAT)]).then_inc(rows_at, 1)

                steps(dve, NT, 0, stats, warm=0, unroll=U)
                dve.wait_ge(rows_at, NT)
                variance(stat[0], FEAT)
                dve.wait_ge(act_at, 1)
                scale_and_bias()
                if equivariant:
                    def stats_h(i, s, r):
                        dve.wait_ge(h_at, i + 1)
                        nc.vector.bn_stats(stat[0][:, ds(i, 1), :], h[:, ds(i * FEAT, SC)]).then_inc(rows_at, 1)
                        nc.vector.bn_stats(stat[1][:, ds(i, 1), :], h[:, ds(i * FEAT + SC, VF)]).then_inc(rows_at, 1)

                    steps(dve, NT, 0, stats_h, warm=0, unroll=U)
                    dve.wait_ge(rows_at, 3 * NT)
                    variance(stat[0], SC)
                    dve.wait_ge(act_at, 2)
                    scale_and_bias()
                    mean_e, sum_e, mean_o, sum_o = (stat[1][:, :, n] for n in (1, 2, 4, 5))
                    then(nc.vector.tensor_tensor(part[:, 0, :], mean_e, mean_e, ALU.mult))
                    then(nc.vector.tensor_tensor(part[:, 1, :], mean_o, mean_o, ALU.mult))
                    then(nc.vector.tensor_tensor(part[:, 0, :], part[:, 0, :], part[:, 1, :], ALU.add))
                    then(nc.vector.tensor_tensor(part[:, 1, :], sum_e, sum_o, ALU.add))
                    then(nc.vector.scalar_tensor_tensor(part[:, 1, :], part[:, 0, :], VF / 2, part[:, 1, :], ALU.mult, ALU.add))
                    then(nc.vector.tensor_scalar(part[:, 2, :], part[:, 1, :], 1.0 / VC, EPS, ALU.mult, ALU.add))
                    dve.wait_ge(act_at, 3)
                    then(nc.vector.reciprocal(scale_v, root[:, 1, :]))

            def act_steps(act):
                act.wait_ge(dve_at, VAR)
                nc.scalar.activation(root[:, 0, :], part[:, 3, :], ACT.Sqrt).then_inc(act_at, 1)
                if equivariant:
                    act.wait_ge(dve_at, H_READY)

                    def make_h(i, s, r):
                        nc.scalar.activation(h[:, ds(i * FEAT, FEAT)], x[:, ds(i * FEAT, FEAT)], ACT.Relu,
                                             scale=scale[:, ds(i, 1)], bias=bias[:, ds(i, 1)]).then_inc(h_at, 1)

                    steps(act, NT, 0, make_h, warm=0, unroll=U)
                    act.wait_ge(dve_at, H_READY + VAR)
                    nc.scalar.activation(root[:, 0, :], part[:, 3, :], ACT.Sqrt).then_inc(act_at, 1)
                    act.wait_ge(dve_at, H_READY + VAR + 2 + RMS)
                    nc.scalar.activation(root[:, 1, :], part[:, 2, :], ACT.Sqrt).then_inc(act_at, 1)

            def pool_steps(pool):
                if equivariant:
                    pool.wait_ge(h_at, NT)
                    nc.gpsimd.tensor_tensor(x[:, :], x[:, :], h, ALU.add).then_inc(added, 1)

            return dve_steps, act_steps, pool_steps, (dve_at, LAST)

        def node_pass(tag, scalar_maps, vector_maps, tables, finish, n_fin, coefs=(), gamma=None):
            ns, nv, n_tab = SC * len(scalar_maps), VF * len(vector_maps), len(tables)
            U = 4
            former = len(layer_sems)
            with ExitStack() as ctx:
                norm_dve, norm_act, norm_pool, normed = norm_steps(ctx, tag, bool(gamma))
                w_s = sbuf(ctx, f"{tag}_w_s", [SC, ns])
                w_v = sbuf(ctx, f"{tag}_w_v", [VF, nv])
                coef = sbuf(ctx, f"{tag}_coef", [P, 8, NT])
                gam = sbuf(ctx, f"{tag}_gam", [VF, 4])
                tile = [sbuf(ctx, f"{tag}_tile{s}", [P, FEAT]) for s in range(2)]
                tile_T = [sbuf(ctx, f"{tag}_tile_T{s}", [VF, 2 * P]) for s in range(2)]
                rows = [[sbuf(ctx, f"{tag}_rows{k}_{s}", [P, FEAT]) for k in range(n_tab)] for s in range(U)]
                temp = sbuf(ctx, f"{tag}_temp", [P, 2 * FEAT])
                ps_t = [psum(ctx, f"{tag}_ps_t{s}", [P, 512]) for s in range(2)]
                ps_s = [psum(ctx, f"{tag}_ps_s{s}", [P, 512]) for s in range(2)]
                ps_v = [psum(ctx, f"{tag}_ps_v{s}", [P, 512]) for s in range(2)]
                zeroed = sem(ctx, f"{tag}_zeroed")
                cleared = sem(ctx, f"{tag}_cleared")
                w_loaded = sem(ctx, f"{tag}_w_loaded")
                w_ready = sem(ctx, f"{tag}_w_ready")
                coef_ready = sem(ctx, f"{tag}_coef_ready")
                copied = sem(ctx, f"{tag}_copied")
                turned = sem(ctx, f"{tag}_turned")
                tile_ready = sem(ctx, f"{tag}_tile_ready")
                mapped = sem(ctx, f"{tag}_mapped")
                fin = sem(ctx, f"{tag}_fin")
                stored = [sem(ctx, f"{tag}_stored{s}") for s in range(U)]
                n_w = len(scalar_maps) + XYZ * len(vector_maps) + (2 + XYZ if gamma else 0)
                clear_sems(0, former)

                with nc.Block() as block:

                    @block.sync
                    def _(sp):
                        for n, w in enumerate(scalar_maps):
                            sp.dma_start(w_s[:, n * SC:(n + 1) * SC], A[w]).then_inc(w_loaded, 16)
                        sp.wait_ge(zeroed, 1)
                        for n, w in enumerate(vector_maps):
                            for c in range(XYZ):
                                at = n * VF + c * VC
                                sp.dma_start(w_v[c:VF:XYZ, at:at + VC], A[w]).then_inc(w_loaded, 16)
                        if gamma:
                            sp.dma_start(gam[0:SC, 0:1], A[gamma[0]]).then_inc(w_loaded, 16)
                            sp.dma_start(gam[0:SC, 1:2], A[gamma[1]]).then_inc(w_loaded, 16)
                            for c in range(XYZ):
                                sp.dma_start(gam[c:VF:XYZ, 2:3], A[gamma[2]]).then_inc(w_loaded, 16)

                        def store(i, s, r):
                            sp.wait_ge(fin, (i + 1) * n_fin)
                            for k in range(n_tab):
                                sp.dma_start(tables[k][ds(i * P, P), :], rows[s][k][:, :]).then_inc(stored[s], 16)

                        steps(sp, NT, 0, store, unroll=U)
                        for s in range(U):
                            sp.wait_ge(stored[s], 16 * n_tab * len(range(s, NT, U)))
                        sp.wait_ge(cleared, 1)

                    @block.gpsimd
                    def _(pool):
                        nc.gpsimd.memset(sums_T[:, (2 if gamma else 0) * COLS:4 * COLS], 0.0).then_inc(cleared, 1)
                        norm_pool(pool)

                    @block.scalar
                    def _(act):
                        norm_act(act)
                        if gamma:
                            act.wait_ge(w_loaded, 16 * n_w)
                        act.wait_ge(*normed)

                        def step(i, s, r):
                            if live(i, NT):
                                at_least(act, turned, i - 1)
                                scale, bias, scale_v = (norm[:, n, ds(i, 1)] for n in range(3))
                                if gamma:
                                    nc.scalar.activation(tile[s][:, 0:SC], h[:, ds(i * FEAT, SC)], ACT.Identity, scale=scale, bias=bias).then_inc(copied, 1)
                                    nc.scalar.activation(tile[s][:, SC:FEAT], h[:, ds(i * FEAT + SC, VF)], ACT.Copy, scale=scale_v).then_inc(copied, 1)
                                else:
                                    nc.scalar.activation(tile[s][:, :], x[:, ds(i * FEAT, FEAT)], ACT.Relu, scale=scale, bias=bias).then_inc(copied, 1)
                            if live(i - 1, NT):
                                s1, _ = back(s, r, 1)
                                at_least(act, turned, i)
                                at_least(act, mapped, i - 2)
                                if gamma:
                                    nc.scalar.activation(tile_T[s1][0:SC, 0:P], ps_t[s1][0:SC, 0:P], ACT.Identity,
                                                         bias=gam[0:SC, 1:2], scale=gam[0:SC, 0:1]).then_inc(tile_ready, 1)
                                else:
                                    nc.scalar.activation(tile_T[s1][0:SC, 0:P], ps_t[s1][0:SC, 0:P], ACT.Copy).then_inc(tile_ready, 1)
                                nc.scalar.activation(tile_T[s1][0:VF, P:2 * P], ps_t[s1][0:VF, P:2 * P], ACT.Copy).then_inc(tile_ready, 1)

                        steps(act, NT, 1, step)

                    @block.tensor
                    def _(pe):
                        pe.wait_ge(w_loaded, 16 * n_w)
                        if gamma:
                            pe.wait_ge(w_ready, 1)

                        def step(i, s, r):
                            if live(i, NT):
                                at_least(pe, copied, (i + 1) * (2 if gamma else 1))
                                at_least(pe, tile_ready, 2 * (i - 1))
                                nc.tensor.transpose(ps_t[s][0:VF, P:2 * P], tile[s][:, SC:FEAT], ident[:, :])
                                nc.tensor.transpose(ps_t[s][0:SC, 0:P], tile[s][:, 0:SC], ident[:, :]).then_inc(turned, 1)
                            if live(i - 1, NT):
                                s1, _ = back(s, r, 1)
                                at_least(pe, tile_ready, 2 * i)
                                at_least(pe, fin, (i - 2) * n_fin)
                                nc.tensor.matmul(ps_s[s1][:, 0:ns], tile_T[s1][0:SC, 0:P], w_s[:, :])
                                nc.tensor.matmul(ps_v[s1][:, 0:nv], tile_T[s1][0:VF, P:2 * P], w_v[:, :]).then_inc(mapped, 1)

                        steps(pe, NT, 1, step)

                    @block.vector
                    def _(dve):
                        nc.vector.memset(w_v[:, :], 0.0).then_inc(zeroed, 1)
                        for n, (k, factor) in enumerate(coefs):
                            nc.vector.tensor_scalar(coef[:, n, :], attr[:, k, :], factor, None, ALU.mult).then_inc(coef_ready, 1)
                        norm_dve(dve)
                        if gamma:
                            dve.wait_ge(w_loaded, 16 * n_w)
                            nc.vector.tensor_scalar(w_v[:, :], w_v[:, :], gam[0:VF, 2:3], None, ALU.mult).then_inc(w_ready, 1)
                        dve.wait_ge(coef_ready, len(coefs))

                        def step(i, s, r):
                            at_least(dve, mapped, i + 1)
                            at_least(dve, stored[s], 16 * n_tab * r)
                            at_least(dve, fin, i * n_fin)
                            finish(dve, i, ps_s[s % 2], ps_v[s % 2], rows[s], coef, temp, fin, i * n_fin)

                        steps(dve, NT, 0, step, unroll=U)

        def xs_at(t):
            return x[:, ds(t * FEAT, SC)]

        def xv_at(t):
            return x[:, ds(t * FEAT + SC, VF)].rearrange("p (u c) -> p c u", c=XYZ)

        def by_component(ap):
            return ap.rearrange("p (c u) -> p c u", c=XYZ)

        def finish_l0(dve, t, ps_s, ps_v, rows, coef, temp, fin, k):
            a_s, a_v = coef[:, 0, ds(t, 1)], coef[:, 1, ds(t, 1)]
            nc.vector.tensor_scalar(rows[0][:, 0:SC], ps_s[:, 0:SC], a_s, None, ALU.mult).then_inc(fin, 1)
            nc.vector.tensor_scalar(rows[0][:, SC:FEAT], ps_v[:, 0:VF], a_v, None, ALU.mult).then_inc(fin, 1)
            nc.vector.scalar_tensor_tensor(xs_at(t), ps_s[:, SC:2 * SC], a_s, xs_at(t), ALU.mult, ALU.add).then_inc(fin, 1)
            nc.vector.scalar_tensor_tensor(xv_at(t), by_component(ps_v[:, VF:2 * VF]), a_v, xv_at(t),
                                           ALU.mult, ALU.add).then_inc(fin, 1)

        def finish_l1(dve, t, ps_s, ps_v, rows, coef, temp, fin, k):
            a_s, a_v = coef[:, 0, ds(t, 1)], coef[:, 1, ds(t, 1)]
            for n in range(2):
                nc.vector.tensor_scalar(rows[n][:, 0:SC], ps_s[:, n * SC:(n + 1) * SC], a_s, None, ALU.mult).then_inc(fin, 1)
                nc.vector.tensor_scalar(rows[n][:, SC:FEAT], ps_v[:, n * VF:(n + 1) * VF], a_v, None, ALU.mult).then_inc(fin, 1)

        def finish_l2(dve, t, ps_s, ps_v, rows, coef, temp, fin, k):
            for n in range(2):
                nc.vector.tensor_copy(rows[n][:, 0:SC], ps_s[:, n * SC:(n + 1) * SC]).then_inc(fin, 1)
                nc.vector.tensor_copy(rows[n][:, SC:FEAT], ps_v[:, n * VF:(n + 1) * VF]).then_inc(fin, 1)

        def finish_l3(dve, t, ps_s, ps_v, rows, coef, temp, fin, k):
            a0, a1, c0, c1 = (coef[:, n, ds(t, 1)] for n in range(4))
            nc.vector.tensor_scalar(temp[:, 0:SC], ps_s[:, 0:SC], a0, None, ALU.mult).then_inc(fin, 1)
            nc.vector.tensor_scalar(temp[:, SC:FEAT], ps_v[:, 0:VF], a0, None, ALU.mult).then_inc(fin, 1)
            nc.vector.scalar_tensor_tensor(xs_at(t), ps_s[:, 2 * SC:3 * SC], c0, xs_at(t), ALU.mult, ALU.add).then_inc(fin, 1)
            nc.vector.scalar_tensor_tensor(xv_at(t), by_component(ps_v[:, 2 * VF:3 * VF]), c0, xv_at(t),
                                           ALU.mult, ALU.add).then_inc(fin, 1)
            dve.wait_ge(fin, k + 4)
            nc.vector.scalar_tensor_tensor(rows[0][:, 0:SC], ps_s[:, SC:2 * SC], a1, temp[:, 0:SC], ALU.mult, ALU.add).then_inc(fin, 1)
            nc.vector.scalar_tensor_tensor(rows[0][:, SC:FEAT], ps_v[:, VF:2 * VF], a1, temp[:, SC:FEAT],
                                           ALU.mult, ALU.add).then_inc(fin, 1)
            nc.vector.scalar_tensor_tensor(xs_at(t), ps_s[:, 3 * SC:4 * SC], c1, xs_at(t), ALU.mult, ALU.add).then_inc(fin, 1)
            nc.vector.scalar_tensor_tensor(xv_at(t), by_component(ps_v[:, 3 * VF:4 * VF]), c1, xv_at(t),
                                           ALU.mult, ALU.add).then_inc(fin, 1)

        def warm_up(bank):
            for _ in range(6):
                nc.tensor.matmul(bank[:, 0:512], ident[:, :], x[:, 0:512])

        def edge_pass(tag, first, rows_of, edge_T, w_in, w_mid, w_out, act_fn, scales):
            k_in, hid = A[w_in].shape
            HALVES = 2 if 2 * hid <= P else 1
            HC = GE // HALVES
            layers = 2 if w_mid else 1
            wn = 2 * SC + 2 * VC
            SS, SV, VS, VV = 0, SC, 2 * SC, 2 * SC + VC
            PW, PV = MID, MID + SC
            K = 9
            U = 4
            FETCH = 4
            lag = layers + 1
            with ExitStack() as ctx:
                def slots(n, name, shape, dt=F32):
                    return [sbuf(ctx, f"{tag}_edge_{name}{s}", shape, dt) for s in range(n)]

                wi = sbuf(ctx, f"{tag}_edge_wi", [HALVES * k_in, HALVES * hid])
                wm = sbuf(ctx, f"{tag}_edge_wm", [HALVES * hid, HALVES * hid])
                wo = sbuf(ctx, f"{tag}_edge_wo", [HALVES * hid, HALVES * wn])
                maps = [(wi, w_in), (wm, w_mid), (wo, w_out)] if w_mid else [(wi, w_in), (wo, w_out)]
                idx = slots(FETCH, "idx", [P, TG], I32)
                g = slots(FETCH, "g", [P, TG, FEAT])
                ea = slots(2, "ea", [HALVES * k_in, HC])
                h = [slots(2, f"h{n}_", [HALVES * hid, HC]) for n in range(layers)]
                gy = slots(2, "gy", [P, TG, FEAT])
                prod = slots(2, "prod", [P, TG, MID + SC + VF])
                hot = slots(2, "hot", [P, TG, 1 + XYZ, EDGE_WIN])
                vy = sbuf(ctx, f"{tag}_edge_vy", [P, TG, XYZ, VC])
                dot = sbuf(ctx, f"{tag}_edge_dot", [P, 2, TG, VC])
                h_ps = [psum(ctx, f"{tag}_edge_h_ps{n}", [P, GE]) for n in range(2)]
                w_ps = [psum(ctx, f"{tag}_edge_w_ps{s}", [P, TG, 256]) for s in range(2)]
                win_ps = [psum(ctx, f"{tag}_edge_win_ps{s}", [P, 512]) for s in range(2)]
                w_zeroed = sem(ctx, f"{tag}_edge_w_zeroed")
                placed = sem(ctx, f"{tag}_edge_placed")
                w_loaded = sem(ctx, f"{tag}_edge_w_loaded")
                idx_loaded = [sem(ctx, f"{tag}_edge_idx_loaded{s}") for s in range(FETCH)]
                fetched = [sem(ctx, f"{tag}_edge_fetched{s}") for s in range(FETCH)]
                ea_loaded = [sem(ctx, f"{tag}_edge_ea_loaded{s}") for s in range(2)]
                hidden = [sem(ctx, f"{tag}_edge_hidden{n}") for n in range(layers)]
                active = [sem(ctx, f"{tag}_edge_active{n}") for n in range(layers)]
                scaled = sem(ctx, f"{tag}_edge_scaled")
                weighed = sem(ctx, f"{tag}_edge_weighed")
                made = sem(ctx, f"{tag}_edge_made")
                summed = sem(ctx, f"{tag}_edge_summed")
                added = sem(ctx, f"{tag}_edge_added")
                last = layers - 1
                W_LOAD = 16 * HALVES * len(maps)

                def half(s, r):
                    return s % 2, r * 2 + s // 2

                with nc.Block() as block:

                    @block.sync
                    def _(sp):
                        sp.wait_ge(w_zeroed, len(maps))
                        for w, name in maps:
                            rows, cols = A[name].shape
                            for n in range(HALVES):
                                sp.dma_start(w[n * rows:(n + 1) * rows, n * cols:(n + 1) * cols], A[name]).then_inc(w_loaded, 16)

                        def step(i, s, r):
                            at_least(sp, fetched[s], 16 * TG * r)
                            sp.dma_start(idx[s][:, :], A["src_groups"][ds(i * P, P), :]).then_inc(idx_loaded[s], 16)
                            at_least(sp, hidden[0], i - 1)
                            sp.dma_start(ea[s % 2][:, :], A[edge_T][:, ds(i * HC, HC)]).then_inc(ea_loaded[s % 2], 16)

                        steps(sp, NG, 0, step, unroll=U)

                    @block.gpsimd
                    def _(pool):
                        def step(i, s, r):
                            gate(pool, (w_loaded, W_LOAD),
                                 (idx_loaded[s], 16 * (r + 1)),
                                 (made, (i - 3) * K))
                            for t in range(TG):
                                pool.indirect_dma_start(g[s][:, t, :], None, rows_of,
                                                        bass.IndirectOffsetOnAxis(idx[s][:, t:t + 1], 0)).then_inc(fetched[s], 16)

                        steps(pool, NG, 0, step, unroll=U)

                    @block.tensor
                    def _(pe):
                        pe.wait_ge(w_loaded, W_LOAD)

                        def step(i, s, r):
                            if isinstance(i, int) and i == lag + 2:
                                pe.wait_ge(active[last], i - last)
                                warm_up(h_ps[1])
                            if live(i, NG):
                                s0, r0 = half(s, r)
                                at_least(pe, ea_loaded[s0], 16 * (r0 + 1))
                                at_least(pe, active[0], i)
                                nc.tensor.matmul(h_ps[0][0:HALVES * hid, 0:HC], wi[:, :], ea[s0][:, :]).then_inc(hidden[0], 1)
                            if w_mid and live(i - 1, NG):
                                s1 = (s - 1) % 2
                                gate(pe, (w_loaded, W_LOAD),
                                     (active[0], i),
                                     (active[1], i - 1))
                                nc.tensor.matmul(h_ps[1][0:HALVES * hid, 0:HC], wm[:, :], h[0][s1][:, :]).then_inc(hidden[1], 1)
                            if live(i - layers, NG):
                                s2 = (s - layers) % 2
                                at_least(pe, active[last], i - layers + 1)
                                at_least(pe, made, (i - layers - 1) * K)
                                for n in range(TG // HALVES):
                                    ins = nc.tensor.matmul(w_ps[s2][:, n * HALVES:(n + 1) * HALVES, 0:wn],
                                                           h[last][s2][:, n * P:(n + 1) * P], wo[:, :])
                                ins.then_inc(weighed, 1)
                            if live(i - lag, NG):
                                s3 = (s - lag) % 2
                                at_least(pe, made, (i - lag + 1) * K)
                                at_least(pe, added, i - lag - 1)
                                win, W, q, to = win_ps[s3], EDGE_WIN, prod[s3], hot[s3]
                                sums = [(win[0:MID, 0:W], 0, MID, slice(0, 1)), (win[0:SC, W:(1 + XYZ) * W], PW, SC, slice(1, 1 + XYZ))]
                                for c in range(XYZ):
                                    sums.append((win[SC:MID, (1 + c) * W:(2 + c) * W], PV + c * VC, VC, slice(0, 1)))
                                for at, lo, width, kinds in sums:
                                    for t in range(TG):
                                        ins = nc.tensor.matmul(at, q[:, t, lo:lo + width], to[:, t, kinds, :],
                                                               start=t == 0, stop=t == TG - 1)
                                ins.then_inc(summed, 1)

                        steps(pe, NG, lag, step, warm=8, unroll=U)

                    @block.scalar
                    def _(act):
                        def step(i, s, r):
                            for n in range(layers):
                                if live(i - n, NG):
                                    s1 = (s - n) % 2
                                    after = hidden[n + 1] if n < last else weighed
                                    at_least(act, hidden[n], i - n + 1)
                                    at_least(act, after, i - n - 1)
                                    nc.scalar.activation(h[n][s1][:, :], h_ps[n][0:HALVES * hid, 0:HC], act_fn,
                                                         scale=scales[n]).then_inc(active[n], 1)
                            if live(i - last, NG):
                                k = i - last
                                sk, rk = back(s, r, last, U)
                                at_least(act, made, (k - 1) * K)
                                at_least(act, fetched[sk], 16 * TG * (rk + 1))
                                for t in range(TG):
                                    ins = nc.scalar.activation(gy[sk % 2][:, t, :], g[sk][:, t, :], ACT.Copy,
                                                               scale=y4[:, ds((k * TG + t) * 4, 1)])
                                ins.then_inc(scaled, 1)

                        steps(act, NG, last, step, warm=8, unroll=U)

                    @block.vector
                    def _(dve):
                        for w, _ in maps:
                            nc.vector.memset(w[:, :], 0.0).then_inc(w_zeroed, 1)
                        place_windows(dve, EDGE_WIN, first, placed)

                        def products(i, s, r):
                            def done(n):
                                return i * K + n

                            s0, _ = half(s, r)
                            w, rows, q = w_ps[s0], g[s], prod[s0]
                            xyz = y4[:, ds(i * TG * 4, TG * 4)].rearrange("p (t c) -> p t c", c=4)[:, :, 1:4].unsqueeze(3)
                            vec = rows[:, :, SC:FEAT].rearrange("p t (c u) -> p t c u", c=XYZ)
                            vec0 = gy[s0][:, :, SC:FEAT].rearrange("p t (c u) -> p t c u", c=XYZ)
                            at_least(dve, summed, i - 1)
                            at_least(dve, made, done(0))
                            to = hot[s0]
                            nc.vector.tensor_tensor(to[:, :, 0, :], iota_win[:, 0:EDGE_WIN].unsqueeze(1).to_broadcast([P, TG, EDGE_WIN]),
                                                    dst_rel[:, ds(i * TG, TG)].unsqueeze(2).to_broadcast([P, TG, EDGE_WIN]),
                                                    ALU.is_equal).then_inc(made, 1)
                            at_least(dve, fetched[s], 16 * TG * (r + 1))
                            nc.vector.tensor_tensor(vy[:, :, :, :], vec, xyz.to_broadcast([P, TG, XYZ, VC]), ALU.mult).then_inc(made, 1)
                            dve.wait_ge(made, done(1))
                            nc.vector.tensor_tensor(to[:, :, 1:1 + XYZ, :], to[:, :, 0, :].unsqueeze(2).to_broadcast([P, TG, XYZ, EDGE_WIN]),
                                                    xyz.to_broadcast([P, TG, XYZ, EDGE_WIN]), ALU.mult).then_inc(made, 1)
                            dve.wait_ge(made, done(2))
                            nc.vector.tensor_tensor(dot[:, 0, :, :], vy[:, :, 0, :], vy[:, :, 1, :], ALU.add).then_inc(made, 1)
                            at_least(dve, weighed, i + 1)
                            nc.vector.tensor_tensor(q[:, :, PW:PV], w[:, :, SV:VS], rows[:, :, 0:SC], ALU.mult).then_inc(made, 1)
                            at_least(dve, scaled, i + 1)
                            nc.vector.tensor_tensor(q[:, :, 0:SC], w[:, :, SS:SV], gy[s0][:, :, 0:SC], ALU.mult).then_inc(made, 1)
                            dve.wait_ge(made, done(4))
                            nc.vector.tensor_tensor(dot[:, 1, :, :], dot[:, 0, :, :], vy[:, :, 2, :], ALU.add).then_inc(made, 1)
                            nc.vector.tensor_tensor(q[:, :, PV:PV + VF].rearrange("p t (c u) -> p t c u", c=XYZ), vec0,
                                                    w[:, :, VS:VV].unsqueeze(2).to_broadcast([P, TG, XYZ, VC]), ALU.mult).then_inc(made, 1)
                            dve.wait_ge(made, done(7))
                            nc.vector.tensor_tensor(q[:, :, SC:MID], w[:, :, VV:wn], dot[:, 1, :, :], ALU.mult).then_inc(made, 1)

                        def step(i, s, r):
                            if live(i, NG):
                                products(i, s, r)
                            if live(i - 2, NG):
                                add_window(dve, i - 2, win_ps[s % 2], MID, 4, EDGE_WIN, summed, added)

                        steps(dve, NG, 2, step, unroll=U)

        def add_window(dve, i, bank, rows, blocks, width, summed, added):
            first = dve.value_load(window_row[0:1, ds(i, 1)], min_val=0, max_val=NPAD)
            at = sums4[0:rows, 0:blocks, ds(first, width)]
            at_least(dve, added, i)
            at_least(dve, summed, i + 1)
            nc.vector.tensor_tensor(at, at, bank[0:rows, 0:blocks * width].rearrange("p (b n) -> p b n", b=blocks),
                                    ALU.add).then_inc(added, 1)

        def post_pass(tag, load_weights, n_loads, prepare, cols, finish, n_fin, self_loads=False):
            c_s, c_v = cols
            with ExitStack() as ctx:
                w = sbuf(ctx, f"{tag}_post_w", [P, 1024])
                coef = sbuf(ctx, f"{tag}_post_coef", [P, 8, NT])
                sums = [sbuf(ctx, f"{tag}_post_sums{s}", [MID, 4, P]) for s in range(2)]
                own = [sbuf(ctx, f"{tag}_post_own{s}", [P, FEAT]) for s in range(2)]
                small = sbuf(ctx, f"{tag}_post_small", [P, 2])
                line = sbuf(ctx, f"{tag}_post_line", [1, NPAD if self_loads else 2])
                ps = [psum(ctx, f"{tag}_post_ps{s}", [P, 512]) for s in range(2)]
                pw = [psum(ctx, f"{tag}_post_pw{s}", [P, 512]) for s in range(2)]
                w_loaded = sem(ctx, f"{tag}_post_w_loaded")
                w_ready = sem(ctx, f"{tag}_post_w_ready")
                prep = sem(ctx, f"{tag}_post_prep")
                prep_act = sem(ctx, f"{tag}_post_prep_act")
                prep_pe = sem(ctx, f"{tag}_post_prep_pe")
                prep_dma = sem(ctx, f"{tag}_post_prep_dma")
                copied = sem(ctx, f"{tag}_post_copied")
                mapped = sem(ctx, f"{tag}_post_mapped")
                fin = sem(ctx, f"{tag}_post_fin")
                own_loaded = [sem(ctx, f"{tag}_post_own_loaded{s}") for s in range(2)]
                B = dict(w=w, coef=coef, small=small, line=line, ps=ps, pw=pw, w_loaded=w_loaded, w_ready=w_ready, prep=prep,
                         prep_act=prep_act, prep_pe=prep_pe, prep_dma=prep_dma, n_loads=n_loads, fin=fin)

                with nc.Block() as block:

                    @block.sync
                    def _(sp):
                        load_weights(sp, B)
                        if "sp" in prepare:
                            prepare["sp"](sp, B)
                        if self_loads:
                            def step(i, s, r):
                                at_least(sp, fin, (i - 1) * n_fin)
                                sp.dma_start(own[s][:, :], self_rows[ds(i * P, P), :]).then_inc(own_loaded[s], 16)

                            steps(sp, NT, 0, step)

                    @block.scalar
                    def _(act):
                        if "act" in prepare:
                            prepare["act"](act, B)

                        def step(i, s, r):
                            at_least(act, mapped, i - 1)
                            nc.scalar.activation(sums[s][:, :, :], sums4[0:MID, :, ds(i * P, P)], ACT.Copy).then_inc(copied, 1)

                        steps(act, NT, 0, step)

                    @block.tensor
                    def _(pe):
                        if "pe" in prepare:
                            prepare["pe"](pe, B)
                        pe.wait_ge(w_ready, 1)

                        def step(i, s, r):
                            at_least(pe, copied, i + 1)
                            at_least(pe, fin, (i - 1) * n_fin)
                            nc.tensor.matmul(ps[s][:, 0:c_s], sums[s][:, 0, :], w[0:MID, 0:c_s])
                            for c in range(XYZ):
                                ins = nc.tensor.matmul(ps[s][:, c_s + c * c_v:c_s + (c + 1) * c_v], sums[s][:, 1 + c, :],
                                                       w[0:MID, c_s:c_s + c_v])
                            ins.then_inc(mapped, 1)

                        steps(pe, NT, 0, step)

                    @block.vector
                    def _(dve):
                        prepare["dve"](dve, B)

                        def step(i, s, r):
                            at_least(dve, mapped, i + 1)
                            at_least(dve, fin, i * n_fin)
                            if self_loads:
                                at_least(dve, own_loaded[s], 16 * (r + 1))
                            finish(dve, i, ps[s], own[s], coef, small, fin, i * n_fin)

                        steps(dve, NT, 0, step)

        def vectors_of(ps, at, width, col, n):
            return ps[:, at:at + XYZ * width].rearrange("p (c w) -> p c w", c=XYZ)[:, :, col:col + n]

        def post_l0():
            k = (SC ** -0.5) * (32.0 ** -0.5) * (MID ** -0.5)
            cs = SC + 1

            def load(sp, B):
                sp.dma_start(B["w"][0:MID, 0:SC], A["L0_gnn_Wl2_s"]).then_inc(B["w_loaded"], 16)
                sp.dma_start(B["w"][0:MID, SC:cs], A["L0_gnn_Wa"]).then_inc(B["w_loaded"], 16)
                sp.dma_start(B["w"][0:MID, cs:cs + VC], A["L0_gnn_Wl2_v"]).then_inc(B["w_loaded"], 16)

            def prep(dve, B):
                nc.vector.tensor_scalar(B["coef"][:, 1, :], attr[:, 0, :], k, None, ALU.mult).then_inc(B["prep"], 1)
                dve.wait_ge(B["prep"], 1)
                nc.vector.tensor_tensor(B["coef"][:, 0, :], B["coef"][:, 1, :], B["coef"][:, 1, :], ALU.mult).then_inc(B["prep"], 1)
                dve.wait_ge(B["w_loaded"], 48)
                nc.vector.tensor_scalar(B["w"][0:MID, 0:cs], B["w"][0:MID, 0:cs], row_scale[0:MID, 0:1], None, ALU.mult).then_inc(B["w_ready"], 1)
                dve.wait_ge(B["prep"], 2)

            def finish(dve, t, ps, own, coef, small, fin, k0):
                nc.vector.tensor_scalar(small[:, 0:1], ps[:, SC:cs], coef[:, 0, ds(t, 1)], None, ALU.mult).then_inc(fin, 1)
                dve.wait_ge(fin, k0 + 1)
                nc.vector.scalar_tensor_tensor(xs_at(t), ps[:, 0:SC], small[:, 0:1], xs_at(t), ALU.mult, ALU.add).then_inc(fin, 1)
                nc.vector.scalar_tensor_tensor(xv_at(t), vectors_of(ps, cs, VC, 0, VC), small[:, 0:1], xv_at(t),
                                               ALU.mult, ALU.add).then_inc(fin, 1)

            post_pass("l0", load, 3, {"dve": prep}, (cs, VC), finish, 3)

        def post_l1():
            k = (SC ** -0.5) * (10.0 ** -0.5) * (MID ** -0.5)
            ROUND = 1.5 * 2.0 ** 23
            pieces = [(n, min(512, NPAD - n)) for n in range(0, NPAD, 512)]

            def load(sp, B):
                sp.dma_start(B["w"][0:MID, 0:SC], A["L1_gnn_W2_s"]).then_inc(B["w_loaded"], 16)
                sp.dma_start(B["w"][0:MID, SC:MID], A["L1_gnn_W2_v"]).then_inc(B["w_loaded"], 16)
                sp.dma_start(B["w"][0:MID, 512:513], A["L1_gnn_W3"]).then_inc(B["w_loaded"], 16)

            def prep_pe(pe, B):
                pe.wait_ge(B["w_ready"], 1)
                for n, (at, width) in enumerate(pieces):
                    at_least(pe, B["prep_act"], n - 1)
                    nc.tensor.matmul(B["pw"][n % 2][0:1, 0:width], B["w"][0:MID, 512:513], sums4[0:MID, 0, at:at + width]
                                     ).then_inc(B["prep_pe"], 1)

            def prep_act(act, B):
                for n, (at, width) in enumerate(pieces):
                    act.wait_ge(B["prep_pe"], n + 1)
                    nc.scalar.activation(B["line"][0:1, at:at + width], B["pw"][n % 2][0:1, 0:width], ACT.Copy).then_inc(B["prep_act"], 1)
                act.wait_ge(B["prep"], 6)
                nc.scalar.activation(B["coef"][:, 5:7, :], B["coef"][:, 3:5, :], ACT.Sin, scale=6.2831850).then_inc(B["prep_act"], 1)

            def prep_sp(sp, B):
                sp.wait_ge(B["prep_act"], len(pieces))
                sp.dma_start(turn_row, B["line"][0:1, :]).then_inc(B["prep_dma"], 16)
                sp.wait_ge(B["prep_dma"], 16)
                with nc.allow_non_contiguous_dma(reason="a row of node values onto partitions, once"):
                    sp.dma_start(B["coef"][:, 0, :], turn_row[0, :].rearrange("(t p) -> p t", p=P)).then_inc(B["prep_dma"], 16)

            def prep(dve, B):
                c, prep = B["coef"], B["prep"]
                dve.wait_ge(B["w_loaded"], 48)
                nc.vector.tensor_scalar(B["w"][0:MID, 512:513], B["w"][0:MID, 512:513], row_scale[0:MID, 0:1], None, ALU.mult).then_inc(B["w_ready"], 1)
                nc.vector.tensor_scalar(B["w"][0:MID, 0:SC], B["w"][0:MID, 0:SC], row_scale[0:MID, 0:1], None, ALU.mult).then_inc(B["w_ready"], 1)
                nc.vector.tensor_scalar(c[:, 7, :], attr[:, 0, :], k, None, ALU.mult).then_inc(prep, 1)
                dve.wait_ge(B["prep_dma"], 32)
                dve.wait_ge(prep, 1)
                nc.vector.scalar_tensor_tensor(c[:, 1, :], c[:, 0, :], 0.1 / 6.283185307179586, c[:, 7, :], ALU.mult, ALU.mult).then_inc(prep, 1)
                dve.wait_ge(prep, 2)
                nc.vector.tensor_scalar(c[:, 2, :], c[:, 1, :], 0.25, None, ALU.add).then_inc(prep, 1)
                dve.wait_ge(prep, 3)
                nc.vector.tensor_scalar(c[:, 5:7, :], c[:, 1:3, :], ROUND, None, ALU.add).then_inc(prep, 1)
                dve.wait_ge(prep, 4)
                nc.vector.tensor_scalar(c[:, 3:5, :], c[:, 5:7, :], ROUND, None, ALU.subtract).then_inc(prep, 1)
                dve.wait_ge(prep, 5)
                nc.vector.tensor_tensor(c[:, 3:5, :], c[:, 1:3, :], c[:, 3:5, :], ALU.subtract).then_inc(prep, 1)
                dve.wait_ge(B["prep_act"], len(pieces) + 1)
                nc.vector.tensor_tensor(c[:, 0, :], c[:, 5, :], c[:, 7, :], ALU.mult).then_inc(prep, 1)
                dve.wait_ge(prep, 7)

            def finish(dve, t, ps, own, coef, small, fin, k0):
                sin, cos = coef[:, 0, ds(t, 1)], coef[:, 6, ds(t, 1)]
                nc.vector.scalar_tensor_tensor(xs_at(t), ps[:, 0:SC], sin, xs_at(t), ALU.mult, ALU.add).then_inc(fin, 1)
                nc.vector.scalar_tensor_tensor(xv_at(t), vectors_of(ps, SC, VC, 0, VC), sin, xv_at(t), ALU.mult, ALU.add).then_inc(fin, 1)
                dve.wait_ge(fin, k0 + 2)
                nc.vector.scalar_tensor_tensor(xs_at(t), own[:, 0:SC], cos, xs_at(t), ALU.mult, ALU.add).then_inc(fin, 1)
                nc.vector.scalar_tensor_tensor(xv_at(t), by_component(own[:, SC:FEAT]), cos, xv_at(t), ALU.mult, ALU.add).then_inc(fin, 1)

            post_pass("l1", load, 3, {"dve": prep, "pe": prep_pe, "act": prep_act, "sp": prep_sp}, (SC, VC), finish, 4,
                      self_loads=True)

        def post_l3():
            import math
            k = math.cos(math.pi / 8) / math.sqrt(16.0)
            T = {"L3_gnn_Ws_l2_a": 192, "L3_gnn_Ws_l2_c": 288, "L3_gnn_Wv_l2_a": 384, "L3_gnn_Wv_l2_c": 480}
            L = {"L3_gnn_Ws_l3": (576, SC), "L3_gnn_Wv_l3": (640, VC)}
            outs = [("L3_gnn_Ws_l2_a", "L3_gnn_Ws_l3", 0), ("L3_gnn_Ws_l2_c", "L3_gnn_Ws_l3", SC),
                    ("L3_gnn_Wv_l2_a", "L3_gnn_Wv_l3", 2 * SC), ("L3_gnn_Wv_l2_c", "L3_gnn_Wv_l3", 2 * SC + VC)]

            def load(sp, B):
                for n, at in T.items():
                    sp.dma_start(B["w"][0:MID, at:at + MID], A[n + "_T"]).then_inc(B["w_loaded"], 16)
                for n, (at, width) in L.items():
                    sp.dma_start(B["w"][0:MID, at:at + width], A[n]).then_inc(B["w_loaded"], 16)

            def prep_pe(pe, B):
                pe.wait_ge(B["w_loaded"], 16 * 6)
                for l2, l3, at in outs:
                    src, width = L[l3]
                    ins = nc.tensor.matmul(B["pw"][0][0:MID, at:at + width], B["w"][0:MID, T[l2]:T[l2] + MID], B["w"][0:MID, src:src + width])
                ins.then_inc(B["prep_pe"], 1)

            def prep(dve, B):
                c, prep = B["coef"], B["prep"]
                for n in range(2):
                    nc.vector.scalar_tensor_tensor(c[:, n, :], attr[:, n, :], k, attr[:, 2, :], ALU.mult, ALU.mult).then_inc(prep, 1)
                dve.wait_ge(B["prep_pe"], 1)
                nc.vector.tensor_copy(B["w"][0:MID, 2 * SC:192], B["pw"][0][0:MID, 2 * SC:192]).then_inc(prep, 1)
                dve.wait_ge(prep, 3)
                nc.vector.tensor_scalar(B["w"][0:MID, 0:2 * SC], B["pw"][0][0:MID, 0:2 * SC], row_scale[0:MID, 0:1], None,
                                        ALU.mult).then_inc(B["w_ready"], 1)

            def finish(dve, t, ps, own, coef, small, fin, k0):
                for n in range(2):
                    f = coef[:, n, ds(t, 1)]
                    if n:
                        dve.wait_ge(fin, k0 + 2)
                    nc.vector.scalar_tensor_tensor(xs_at(t), ps[:, n * SC:(n + 1) * SC], f, xs_at(t), ALU.mult, ALU.add).then_inc(fin, 1)
                    nc.vector.scalar_tensor_tensor(xv_at(t), vectors_of(ps, 2 * SC, 2 * VC, n * VC, VC), f, xv_at(t),
                                                   ALU.mult, ALU.add).then_inc(fin, 1)

            post_pass("l3", load, 6, {"dve": prep, "pe": prep_pe}, (2 * SC, 2 * VC), finish, 4)

        def attention_pass():
            FW = MID + SC + XYZ * 2 * VC
            PARTS = [(0, MID), (MID, P), (MID + P, P)]
            WW = 2 * SC + 3 * VC
            VS, VV0, VV1 = 2 * SC, 2 * SC + VC, 2 * SC + 2 * VC
            GATE, Q, PV = SC, SC + VC, SC + 2 * VC
            Q2, PV2 = SC, SC + VC
            O1W, O2W = SC + 2 * VC + VF, SC + VC + VF
            K1, K2, K3 = 13, 11, 4
            FETCH = U = 4
            with ExitStack() as ctx:
                def pair(name, shape, dt=F32, n=2):
                    return [sbuf(ctx, f"att_{name}{s}", shape, dt) for s in range(n)]

                w_rbf = sbuf(ctx, "att_w_rbf", [QUARTER + 16, WW])
                w_att = sbuf(ctx, "att_w_att", [MID, 2 * SC])
                w_dot = sbuf(ctx, "att_w_dot", [2 * SC, QUARTER])
                w_val_T = sbuf(ctx, "att_w_val_T", [SC, MID])
                w_gate = sbuf(ctx, "att_w_gate", [SC, VC])
                w_o1s = sbuf(ctx, "att_w_o1s", [MID, MID])
                w_o1v = [sbuf(ctx, f"att_w_o1v{n}", [P, 2 * VC]) for n in range(2)]
                w_o2s = sbuf(ctx, "att_w_o2s", [MID, SC])
                w_o2v = [sbuf(ctx, f"att_w_o2v{n}", [P, 2 * VC]) for n in range(2)]
                w2 = sbuf(ctx, "att_w2", [P, 3])
                ends = pair("ends", [P, 2 * TG], I32, FETCH)
                ea = pair("ea", [2 * QUARTER, 2 * P])
                y_all = sums_T[:, 0:NG * TG * YC]
                g = pair("g", [P, TG, FEAT], n=FETCH)
                gy = pair("gy", [P, TG, FEAT])
                at = NG * TG * YC
                feat = [sums_T[:, at + n * TG * FW:at + (n + 1) * TG * FW].rearrange("p (t f) -> p t f", t=TG) for n in range(4)]
                at += 4 * TG * FW
                feat_T = [sums_T[:, at + n * 3 * GE:at + (n + 1) * 3 * GE].rearrange("p (k e) -> p k e", k=3) for n in range(2)]
                act_T = sbuf(ctx, "att_act_T", [2 * SC, GE])
                score = pair("score", [P, P])
                gate_s = pair("gate", [P, TG, VC])
                vec2 = [sbuf(ctx, f"att_vec2{n}", [P, TG, XYZ, VC]) for n in range(3)]
                vy = sbuf(ctx, "att_vy", [P, TG, XYZ, VC])
                p1 = sbuf(ctx, "att_p1", [P, TG, XYZ, VC])
                p2 = sbuf(ctx, "att_p2", [P, TG, XYZ, VC])
                dot = sbuf(ctx, "att_dot", [P, TG, VC])
                qy = sbuf(ctx, "att_qy", [P, TG, XYZ, VC])
                rows = pair("rows", [P, TG, HEADS, HF], n=U)
                w_ps = psum(ctx, "att_w_ps", [P, TG, 256])
                o1 = psum(ctx, "att_o1", [P, TG, 256])
                o2 = psum(ctx, "att_o2", [P, TG, 256])
                turn = [psum(ctx, f"att_turn{n}", [P, GE]) for n in range(2)]

                w_zeroed = sem(ctx, "att_w_zeroed")
                w_loaded = sem(ctx, "att_w_loaded")
                w_made = sem(ctx, "att_w_made")
                w_prod = sem(ctx, "att_w_prod")
                ends_loaded = [sem(ctx, f"att_ends_loaded{s}") for s in range(FETCH)]
                ea_loaded = [sem(ctx, f"att_ea_loaded{s}") for s in range(2)]
                y_loaded = sem(ctx, "att_y_loaded")
                fetched = [sem(ctx, f"att_fetched{s}") for s in range(FETCH)]
                joined = [sem(ctx, f"att_joined{s}") for s in range(FETCH)]
                scaled = sem(ctx, "att_scaled")
                y0_done = sem(ctx, "att_y0_done")
                stored = [sem(ctx, f"att_stored{s}") for s in range(U)]
                scores_stored = [sem(ctx, f"att_scores_stored{s}") for s in range(2)]
                weighed = sem(ctx, "att_weighed")
                made1 = sem(ctx, "att_made1")
                made2 = sem(ctx, "att_made2")
                made3 = sem(ctx, "att_made3")
                turned1 = sem(ctx, "att_turned1")
                read1 = sem(ctx, "att_read1")
                turned2 = sem(ctx, "att_turned2")
                read2 = sem(ctx, "att_read2")
                mapped1 = sem(ctx, "att_mapped1")
                mapped2 = sem(ctx, "att_mapped2")
                gated = sem(ctx, "att_gated")
                values_out = sem(ctx, "att_values_out")
                N_LOAD = 33

                def pairs_of(f, lo):
                    return f[:, :, MID + SC:FW].rearrange("p t (c k) -> p t c k", c=XYZ)[:, :, :, lo:lo + VC]

                with nc.Block() as block:

                    @block.sync
                    def _(sp):
                        def put(dst, name, rows=None):
                            a = A["L2_gnn_" + name]
                            sp.dma_start(dst, a if rows is None else a[rows[0]:rows[1], :]).then_inc(w_loaded, 16)

                        sp.dma_start(y_all, A["y_all"]).then_inc(y_loaded, 16)
                        for at in (0, QUARTER):
                            put(w_rbf[at:at + 16, :], "W_rbf")
                        put(w_att[:, 0:SC], "W_alpha")
                        put(w_att[:, SC:2 * SC], "W_alpha")
                        put(w_val_T[:, :], "Ws_val_T")
                        put(w_gate[:, :], "Wg")
                        put(w_o1s[:, 0:SC], "Ws_val")
                        put(w_o2s[:, :], "Ws_vlin")
                        sp.wait_ge(w_zeroed, 5)
                        for h in range(HEADS):
                            for at in (h * HS, SC + h * HS):
                                put(w_dot[at:at + HS, h:h + 1], "alpha_dot", (h * HS, (h + 1) * HS))
                        for w, name in ((w_o1v, "Wv_val"), (w_o2v, "Wv_vlin")):
                            put(w[0][0:SC, 0:VC], name, (0, SC))
                            put(w[0][SC:P, VC:2 * VC], name, (SC, P))
                            put(w[1][0:SC, 0:VC], name, (SC, P))
                            put(w[1][SC:P, VC:2 * VC], name, (SC, P))
                        put(w2[0:SC, 0:1], "w2_ss")
                        put(w2[SC:MID, 0:1], "w2_vv0")
                        put(w2[0:SC, 1:2], "w2_sv")
                        put(w2[SC:MID, 1:2], "w2_vs")
                        put(w2[MID:P, 1:2], "w2_vv1")
                        for n in range(2):
                            put(w2[n * SC:n * SC + VC, 2:3], "w2_vs")
                            put(w2[n * SC + VC:(n + 1) * SC, 2:3], "w2_vv1")

                        def step(i, s, r):
                            if live(i, NG):
                                at_least(sp, joined[s], 16 * TG * r)
                                sp.dma_start(ends[s][:, 0:TG], A["src_groups"][ds(i * P, P), :]).then_inc(ends_loaded[s], 16)
                                sp.dma_start(ends[s][:, TG:2 * TG], A["dst_groups"][ds(i * P, P), :]).then_inc(ends_loaded[s], 16)
                            k = i - 2
                            if live(k, NG):
                                at_least(sp, weighed, k - 1)
                                sp.dma_start(ea[s % 2][:, :], A["edge_attr_16_T"][:, ds(k * 2 * P, 2 * P)]).then_inc(ea_loaded[s % 2], 16)
                            k = i - 4
                            if live(k, NG):
                                at_least(sp, read1, k * 5 + 5)
                                for t in range(TG):
                                    sp.dma_start(scores_T[:, ds(k * GE + t * P, P)], score[s % 2][t * QUARTER:t * QUARTER + HEADS, :]
                                                 ).then_inc(scores_stored[s % 2], 16)
                            k = i - 7
                            if live(k, NG):
                                gate(sp, (w_zeroed, 5),
                                     (made3, (k + 1) * K3),
                                     (values_out, k + 1))
                                sp.dma_start(messages[ds(k * GE, GE), :].rearrange("(t p) f -> p t f", p=P),
                                             rows[(s + 1) % U][:, :, :, :].rearrange("p t h f -> p t (h f)")).then_inc(stored[(s + 1) % U], 16)

                        steps(sp, NG, 7, step, warm=8, unroll=U)
                        for s in range(U):
                            sp.wait_ge(stored[s], 16 * NG // U)
                        for s in range(2):
                            sp.wait_ge(scores_stored[s], 16 * TG * NG // 2)

                    @block.gpsimd
                    def _(pool):
                        def step(i, s, r):
                            if live(i, NG):
                                gate(pool, (w_loaded, 16 * N_LOAD),
                                     (ends_loaded[s], 32 * (r + 1)),
                                     (made1, (i - 3) * K1))
                                for t in range(TG):
                                    pool.indirect_dma_start(g[s][:, t, :], None, table[2],
                                                            bass.IndirectOffsetOnAxis(ends[s][:, t:t + 1], 0)).then_inc(fetched[s], 16)
                            if live(i - 1, NG):
                                s1, r1 = back(s, r, 1, U)
                                gate(pool, (w_loaded, 16 * N_LOAD),
                                     (fetched[s1], 16 * TG * (r1 + 1)))
                                for t in range(TG):
                                    pool.indirect_dma_start(g[s1][:, t, :], None, table[3],
                                                            bass.IndirectOffsetOnAxis(ends[s1][:, TG + t:TG + t + 1], 0),
                                                            compute_op=ALU.add).then_inc(joined[s1], 16)

                        steps(pool, NG, 1, step, warm=8, unroll=U)

                    @block.tensor
                    def _(pe):
                        def weigh(i, s, r):
                            at_least(pe, made1, i * K1)
                            at_least(pe, ea_loaded[s % 2], 16 * (r * 2 + s // 2 + 1))
                            for t in (0, 2, 1, 3):
                                at, row = t // 2 * QUARTER, t % 2 * P
                                ins = nc.tensor.matmul(w_ps[:, t, 0:WW], ea[s % 2][at:at + 16, row:row + P], w_rbf[at:at + 16, :])
                            ins.then_inc(weighed, 1)

                        def transpose(f, part, bank):
                            at, width = PARTS[part]
                            for t in range(TG):
                                ins = nc.tensor.transpose(turn[bank][0:width, t * P:(t + 1) * P], f[:, t, at:at + width], ident[:, :])
                            return ins

                        pe.wait_ge(w_loaded, 16 * N_LOAD)
                        pe.wait_ge(w_zeroed, 6)
                        nc.tensor.matmul(turn[0][0:MID, 0:VC], w_val_T[:, :], w_gate[:, :]).then_inc(w_prod, 1)
                        pe.wait_ge(w_made, 9)
                        weigh(0, 0, 0)

                        def step(i, s, r):
                            k = i - 2
                            both = live(k, NG)
                            f2 = feat[2 + s % 2]
                            if both:
                                at_least(pe, made2, (k + 1) * K2)
                                at_least(pe, y0_done, k + 1)
                                at_least(pe, read1, (i - 1) * 5 + 4 if live(i - 1, NG) else NG * 5)
                                transpose(f2, 0, 1).then_inc(turned2, 1)
                            if live(i, NG) and live(i + 1, NG):
                                weigh(i + 1, (s + 1) % U, r + (s + 1) // U)
                            if both:
                                at_least(pe, read1, i * 5 if live(i - 1, NG) else NG * 5)
                                transpose(f2, 1, 0).then_inc(turned2, 1)
                                at_least(pe, read2, k * 3 + 1)
                                transpose(f2, 2, 1).then_inc(turned2, 1)
                            if live(i, NG):
                                at_least(pe, made1, (i + 1) * K1)
                                at_least(pe, read1, i * 5)
                                at_least(pe, read2, k * 3 + 2)
                                if isinstance(i, int) and i == 4:
                                    warm_up(turn[0])
                                transpose(feat[s % 2], 0, 0).then_inc(turned1, 1)
                            if both:
                                at_least(pe, read2, k * 3 + 3)
                                at_least(pe, made3, k * K3)
                                at_least(pe, values_out, k)
                                for t in range(TG):
                                    e = slice(t * P, (t + 1) * P)
                                    nc.tensor.matmul(o2[:, t, 0:SC], feat_T[1][0:MID, 0, e], w_o2s[:, :])
                                    nc.tensor.matmul(o2[:, t, Q2:PV2 + VC], feat_T[1][:, 1, e], w_o2v[0][:, :])
                                    ins = nc.tensor.matmul(o2[:, t, PV2 + VC:O2W], feat_T[1][:, 2, e], w_o2v[1][:, :])
                                ins.then_inc(mapped2, 1)
                            if live(i, NG):
                                transpose(feat[s % 2], 1, 1).then_inc(turned1, 1)
                                at_least(pe, read1, i * 5 + 1)
                                transpose(feat[s % 2], 2, 0).then_inc(turned1, 1)
                                at_least(pe, made2, (i - 1) * K2 + 2)
                                at_least(pe, gated, i * 2)
                                tiles = [slice(t * P, (t + 1) * P) for t in range(TG)]
                                for t, e in enumerate(tiles):
                                    nc.tensor.matmul(o1[:, t, 0:MID], feat_T[0][0:MID, 0, e], w_o1s[:, :])
                                at_least(pe, read1, i * 5 + 2)
                                nc.tensor.matmul(turn[1][:, :], w_att[:, :], feat_T[0][0:MID, 0, :]).then_inc(turned1, 1)
                                at_least(pe, read1, i * 5 + 3)
                                for t, e in enumerate(tiles):
                                    nc.tensor.matmul(o1[:, t, Q:PV + VC], feat_T[0][:, 1, e], w_o1v[0][:, :])
                                    ins = nc.tensor.matmul(o1[:, t, PV + VC:O1W], feat_T[0][:, 2, e], w_o1v[1][:, :])
                                ins.then_inc(mapped1, 1)
                                at_least(pe, read1, i * 5 + 4)
                                for t in range(TG):
                                    ins = nc.tensor.matmul(turn[0][t * QUARTER:(t + 1) * QUARTER, 0:P], w_dot[:, :], act_T[:, t * P:(t + 1) * P])
                                ins.then_inc(turned1, 1)

                        steps(pe, NG - 1, 3, step, warm=8, unroll=U)

                    @block.scalar
                    def _(act):
                        def scale_rows(i, s, r):
                            gate(act, (w_made, 9),
                                 (made1, (i - 1) * K1),
                                 (joined[s], 16 * TG * (r + 1)))
                            for t in range(TG):
                                ins = nc.scalar.activation(gy[s % 2][:, t, :], g[s][:, t, :], ACT.Copy, scale=y0_of(i, t))
                            ins.then_inc(scaled, 1)

                        def y0_of(i, t):
                            return y4[:, ds((i * TG + t) * 4, 1)]

                        scale_rows(0, 0, 0)

                        def turn_out(n, part, bank, count):
                            width = PARTS[part][1]
                            nc.scalar.activation(feat_T[n][0:width, part, :], turn[bank][0:width, :], ACT.Copy).then_inc(count, 1)

                        def step(i, s, r):
                            k = i - 2
                            if live(k, NG):
                                at_least(act, mapped2, k)
                                for part in range(3):
                                    at_least(act, turned2, k * 3 + part + 1)
                                    turn_out(1, part, 1 - part % 2, read2)
                            if live(i, NG):
                                at_least(act, mapped1, i)
                                at_least(act, turned1, i * 5 + 1)
                                turn_out(0, 0, 0, read1)
                            if live(i + 1, NG):
                                scale_rows(i + 1, (s + 1) % U, r + (s + 1) // U)
                            if live(k, NG):
                                s2, r2 = back(s, r, 2, U)
                                at_least(act, mapped2, k + 1)
                                at_least(act, stored[s2], 16 * r2)
                                nc.scalar.activation(rows[s2][:, :, :, 0:HS], o2[:, :, 0:SC].rearrange("p t (h f) -> p t h f", h=HEADS),
                                                     ACT.Copy).then_inc(values_out, 1)
                            if live(i, NG):
                                for part in range(1, 3):
                                    at_least(act, turned1, i * 5 + part + 1)
                                    turn_out(0, part, part % 2, read1)
                                at_least(act, turned1, i * 5 + 4)
                                nc.scalar.activation(act_T[:, :], turn[1][:, :], ACT.Relu).then_inc(read1, 1)
                            if live(i - 1, NG):
                                s1, _ = back(s, r, 1, U)
                                gate(act, (w_made, 9),
                                     (made2, (i - 1) * K2 + 3))
                                for t in range(TG):
                                    ins = nc.scalar.activation(pairs_of(feat[2 + s1 % 2], 0)[:, t, :, :], vec2[2][:, t, :, :], ACT.Copy,
                                                               scale=y0_of(i - 1, t))
                                ins.then_inc(y0_done, 1)
                            if live(i, NG):
                                f = feat[2 + s % 2]
                                at_least(act, mapped1, i + 1)
                                at_least(act, turned2, (i - 1) * 3)
                                nc.scalar.activation(f[:, :, MID:MID + SC], o1[:, :, 0:SC], ACT.Sigmoid).then_inc(gated, 1)
                                at_least(act, made2, (i - 2) * K2 + 3)
                                nc.scalar.activation(gate_s[s % 2][:, :, :], o1[:, :, GATE:Q], ACT.Sigmoid).then_inc(gated, 1)
                                at_least(act, turned1, i * 5 + 5)
                                at_least(act, scores_stored[s % 2], 16 * TG * (r * 2 + s // 2))
                                nc.scalar.activation(score[s % 2][:, :], turn[0][:, 0:P], ACT.Copy).then_inc(read1, 1)
                                gate(act, (w_made, 9), (gated, i * 2 + 1))
                                for t in range(TG):
                                    nc.scalar.activation(f[:, t, 0:SC], f[:, t, MID:MID + SC], ACT.Copy, scale=y0_of(i, t))

                        steps(act, NG - 1, 3, step, warm=8, unroll=U)

                    @block.vector
                    def _(dve):
                        for a in (w_dot, *w_o1v, *w_o2v):
                            nc.vector.memset(a[:, :], 0.0).then_inc(w_zeroed, 1)
                        dve.wait_ge(w_loaded, 16 * N_LOAD)
                        nc.vector.tensor_scalar(w_dot[SC:2 * SC, :], w_dot[SC:2 * SC, :], -0.2, None, ALU.mult).then_inc(w_zeroed, 1)
                        dots = row_scale[0:MID, 0:1]
                        nc.vector.tensor_scalar(w_att[:, 0:SC], w_att[:, 0:SC], dots, None, ALU.mult).then_inc(w_made, 1)
                        nc.vector.tensor_scalar(w_att[:, SC:2 * SC], w_att[:, SC:2 * SC], dots, -1.0, ALU.mult, ALU.mult).then_inc(w_made, 1)
                        dve.wait_ge(w_prod, 1)
                        nc.vector.tensor_scalar(w_o1s[:, SC:MID], turn[0][0:MID, 0:VC], dots, None, ALU.mult).then_inc(w_made, 1)
                        nc.vector.tensor_scalar(w_o1s[:, 0:SC], w_o1s[:, 0:SC], dots, None, ALU.mult).then_inc(w_made, 1)
                        nc.vector.tensor_scalar(w_o2s[:, :], w_o2s[:, :], dots, w2[0:MID, 0:1], ALU.mult, ALU.mult).then_inc(w_made, 1)
                        for n in range(2):
                            cross = row_scale[:, 1 + n:2 + n]
                            nc.vector.tensor_scalar(w_o1v[n][:, :], w_o1v[n][:, :], cross, None, ALU.mult).then_inc(w_made, 1)
                            nc.vector.tensor_scalar(w_o2v[n][:, :], w_o2v[n][:, :], cross, w2[:, 1 + n:2 + n], ALU.mult, ALU.mult).then_inc(w_made, 1)

                        dve.wait_ge(y_loaded, 16)

                        def y_of(i):
                            return y_all[:, ds(i * (TG * YC), TG * YC)].rearrange("p (t c) -> p t c", c=YC)

                        def xyz(yy, lo, hi, width):
                            return yy[:, :, lo:hi].unsqueeze(3).to_broadcast([P, TG, hi - lo, width])

                        def tt(out, a, b, op, count):
                            nc.vector.tensor_tensor(out, a, b, op).then_inc(count, 1)

                        def cross_parts(v, yy, count):
                            tt(p1[:, :, 0:2, :], v[:, :, 1:3, :], xyz(yy, 3, 5, VC), ALU.mult, count)
                            tt(p1[:, :, 2:3, :], v[:, :, 0:1, :], xyz(yy, 5, 6, VC), ALU.mult, count)
                            tt(p2[:, :, 0:1, :], v[:, :, 2:3, :], xyz(yy, 2, 3, VC), ALU.mult, count)
                            tt(p2[:, :, 1:3, :], v[:, :, 0:2, :], xyz(yy, 3, 5, VC), ALU.mult, count)

                        def first(i, s, r):
                            k = i * K1
                            f, yy, w = feat[s % 2], y_of(i), w_ps
                            sca, vec = g[s][:, :, 0:SC], g[s][:, :, SC:FEAT].rearrange("p t (c u) -> p t c u", c=XYZ)
                            sca0, vec0 = gy[s % 2][:, :, 0:SC], gy[s % 2][:, :, SC:FEAT].rearrange("p t (c u) -> p t c u", c=XYZ)
                            at_least(dve, made1, k)
                            at_least(dve, made2, (i - 1) * K2)
                            at_least(dve, joined[s], 16 * TG * (r + 1))
                            tt(vy[:, :, :, :], vec, xyz(yy, 1, 4, VC), ALU.mult, made1)
                            cross_parts(vec, yy, made1)
                            dve.wait_ge(made1, k + 1)
                            tt(dot[:, :, :], vy[:, :, 0, :], vy[:, :, 1, :], ALU.add, made1)
                            at_least(dve, weighed, i + 1)
                            at_least(dve, turned1, (i - 2) * 5 + 3)
                            tt(f[:, :, MID:MID + SC], w[:, :, SC:2 * SC], sca, ALU.mult, made1)
                            dve.wait_ge(made1, k + 6)
                            tt(p1[:, :, :, :], p1[:, :, :, :], p2[:, :, :, :], ALU.subtract, made1)
                            tt(dot[:, :, :], dot[:, :, :], vy[:, :, 2, :], ALU.add, made1)
                            at_least(dve, scaled, i + 1)
                            tt(f[:, :, 0:SC], w[:, :, 0:SC], sca0, ALU.mult, made1)
                            tt(pairs_of(f, 0), vec0, w[:, :, VS:VV0].unsqueeze(2).to_broadcast([P, TG, XYZ, VC]), ALU.mult, made1)
                            dve.wait_ge(made1, k + 9)
                            tt(f[:, :, SC:MID], w[:, :, VV0:VV1], dot[:, :, :], ALU.mult, made1)
                            tt(pairs_of(f, VC), p1[:, :, :, :], w[:, :, VV1:WW].unsqueeze(2).to_broadcast([P, TG, XYZ, VC]), ALU.mult, made1)

                        def second(i, s, r):
                            k = i * K2
                            f, yy = feat[2 + s % 2], y_of(i)
                            v = vec2[2]
                            at_least(dve, made2, k)
                            at_least(dve, gated, (i + 1) * 2)
                            tt(vec2[0][:, :, :, :], o1[:, :, Q:PV].unsqueeze(2).to_broadcast([P, TG, XYZ, VC]), xyz(yy, 1, 4, VC), ALU.mult, made2)
                            dve.wait_ge(made2, k + 1)
                            tt(vec2[1][:, :, :, :], vec2[0][:, :, :, :], o1[:, :, PV:O1W].rearrange("p t (c u) -> p t c u", c=XYZ), ALU.add, made2)
                            at_least(dve, y0_done, i)
                            dve.wait_ge(made2, k + 2)
                            tt(v[:, :, :, :], vec2[1][:, :, :, :], gate_s[s % 2][:, :, :].unsqueeze(2).to_broadcast([P, TG, XYZ, VC]), ALU.mult, made2)
                            dve.wait_ge(made2, k + 3)
                            tt(vy[:, :, :, :], v[:, :, :, :], xyz(yy, 1, 4, VC), ALU.mult, made2)
                            cross_parts(v, yy, made2)
                            dve.wait_ge(made2, k + 4)
                            tt(dot[:, :, :], vy[:, :, 0, :], vy[:, :, 1, :], ALU.add, made2)
                            at_least(dve, turned2, (i - 1) * 3)
                            dve.wait_ge(made2, k + 9)
                            tt(pairs_of(f, VC), p1[:, :, :, :], p2[:, :, :, :], ALU.subtract, made2)
                            tt(f[:, :, SC:MID], dot[:, :, :], vy[:, :, 2, :], ALU.add, made2)

                        def message(i, s, r):
                            k = i * K3
                            yy = y_of(i)
                            at_least(dve, made3, k)
                            at_least(dve, values_out, i + 1)
                            tt(qy[:, :, :, :], o2[:, :, Q2:PV2].unsqueeze(2).to_broadcast([P, TG, XYZ, VC]), xyz(yy, 1, 4, VC), ALU.mult, made3)
                            at_least(dve, stored[s], 16 * r)
                            dve.wait_ge(made3, k + 1)
                            for c in range(XYZ):
                                lo = HS + c * HV
                                tt(rows[s][:, :, :, lo:lo + HV], qy[:, :, c, :].rearrange("p t (h a) -> p t h a", h=HEADS),
                                   o2[:, :, PV2 + c * VC:PV2 + (c + 1) * VC].rearrange("p t (h a) -> p t h a", h=HEADS), ALU.add, made3)

                        def step(i, s, r):
                            if live(i, NG):
                                first(i, s, r)
                            if live(i - 3, NG):
                                s3, r3 = back(s, r, 3, U)
                                message(i - 3, s3, r3)
                            if live(i - 1, NG):
                                s1, r1 = back(s, r, 1, U)
                                at_least(dve, made1, ((i + 1) if live(i, NG) else NG) * K1)
                                second(i - 1, s1, r1)

                        steps(dve, NG, 3, step, warm=8, unroll=U)

        def softmax_pass():
            with ExitStack() as ctx:
                big = [sums_T[:, n * (CHUNK + 2):(n + 1) * (CHUNK + 2)] for n in range(6)]
                score, fwd, bwd = (big[n][:, 0:CHUNK] for n in (0, 2, 3))
                dst_i = big[4].bitcast(I32)
                dst_f = big[5]
                pen = big[1][:, 0:CHUNK + 1]
                ends_i = sbuf(ctx, "soft_ends_i", [HEADS, 2, CHUNKS], I32)
                ends_f = sbuf(ctx, "soft_ends_f", [HEADS, 2, CHUNKS])
                pen_c = sbuf(ctx, "soft_pen_c", [HEADS, 2, CHUNKS])
                state = sbuf(ctx, "soft_state", [HEADS, 2, CHUNKS])
                carry = sbuf(ctx, "soft_carry", [HEADS, 2, CHUNKS + 1])
                start = sbuf(ctx, "soft_start", [P, 2])
                loaded = sem(ctx, "soft_loaded")
                done = sem(ctx, "soft_done")
                moved = sem(ctx, "soft_moved")
                exped = sem(ctx, "soft_exped")
                stored = sem(ctx, "soft_stored")
                line = A["dst_line"]
                flat_in = scores_T.rearrange("h (k n) -> (h k) n", n=CHUNK)
                flat_out = exps_T.rearrange("h (k n) -> (h k) n", n=CHUNK)
                ENDS, CARRIES = [10, 13], [11, 14]

                with nc.Block() as block:

                    @block.sync
                    def _(sp):
                        with nc.allow_non_contiguous_dma(reason="the nodes at the chunks' ends, once"):
                            for h in range(HEADS):
                                src = bass.AP(line.tensor, line.offset, [[CHUNK, CHUNKS], [1, CHUNK + 2]])
                                sp.dma_start(dst_i[h * CHUNKS:(h + 1) * CHUNKS, :], src).then_inc(loaded, 16)
                                for n in range(2):
                                    ends = bass.AP(line.tensor, line.offset + (CHUNK if n else 1), [[1, 1], [CHUNK, CHUNKS]])
                                    sp.dma_start(ends_i[h:h + 1, n, :], ends).then_inc(loaded, 16)
                            sp.dma_start(score, flat_in).then_inc(loaded, 16)
                            for n, last in enumerate((fwd[:, CHUNK - 1:CHUNK], bwd[:, 0:1])):
                                sp.wait_ge(done, ENDS[n])
                                sp.dma_start(chunk_ends[n, :].unsqueeze(1), last).then_inc(moved, 16)
                                sp.wait_ge(moved, 64 * n + 16)
                                sp.dma_start(state[:, n, :], chunk_ends[n, :].rearrange("(h k) -> h k", h=HEADS)).then_inc(moved, 16)
                                sp.wait_ge(done, CARRIES[n])
                                sp.dma_start(chunk_carries[n, :].rearrange("(h k) -> h k", h=HEADS), carry[:, n, n:n + CHUNKS]).then_inc(moved, 16)
                                sp.wait_ge(moved, 64 * n + 48)
                                sp.dma_start(start[:, n:n + 1], chunk_carries[n, :].unsqueeze(1)).then_inc(moved, 16)
                        sp.wait_ge(exped, 1)
                        sp.dma_start(flat_out, score).then_inc(stored, 16)
                        sp.wait_ge(stored, 16)

                    @block.vector
                    def _(dve):
                        count = [0]

                        def then(ins):
                            count[0] += 1
                            ins.then_inc(done, 1)
                            dve.wait_ge(done, count[0])

                        def scan(out, p, v, initial):
                            return nc.vector.tensor_tensor_scan(out, p, v, initial, ALU.add, ALU.max)

                        dve.wait_ge(loaded, 16 * (3 * HEADS + 1))
                        then(nc.vector.tensor_copy(dst_f, dst_i))
                        then(nc.vector.tensor_copy(ends_f[:, :, :], ends_i[:, :, :]))
                        then(nc.vector.tensor_tensor(pen, dst_f[:, 1:CHUNK + 2], dst_f[:, 0:CHUNK + 1], ALU.not_equal))
                        then(nc.vector.tensor_scalar(pen, pen, LOWEST, None, ALU.mult))
                        then(nc.vector.memset(carry[:, :, :], LOWEST))
                        then(nc.vector.memset(pen_c[:, :, :], 0.0))
                        then(nc.vector.tensor_tensor(pen_c[:, 0, 1:CHUNKS], ends_f[:, 1, 0:CHUNKS - 1], ends_f[:, 1, 1:CHUNKS], ALU.not_equal))
                        then(nc.vector.tensor_tensor(pen_c[:, 1, 0:CHUNKS - 1], ends_f[:, 0, 0:CHUNKS - 1], ends_f[:, 0, 1:CHUNKS], ALU.not_equal))
                        then(nc.vector.tensor_scalar(pen_c[:, :, :], pen_c[:, :, :], LOWEST, None, ALU.mult))
                        then(scan(fwd, pen[:, 0:CHUNK], score, LOWEST))
                        dve.wait_ge(moved, 32)
                        then(scan(carry[:, 0, 1:CHUNKS + 1], pen_c[:, 0, :], state[:, 0, :], LOWEST))
                        dve.wait_ge(moved, 64)
                        then(scan(fwd, pen[:, 0:CHUNK], score, start[:, 0:1]))
                        back_pen, back_fwd, back_out = pen[:, 1:CHUNK + 1][:, ::-1], fwd[:, ::-1], bwd[:, ::-1]
                        then(scan(back_out, back_pen, back_fwd, LOWEST))
                        dve.wait_ge(moved, 96)
                        then(scan(carry[:, 1, 0:CHUNKS][:, ::-1], pen_c[:, 1, :][:, ::-1], state[:, 1, :][:, ::-1], LOWEST))
                        dve.wait_ge(moved, 128)
                        then(scan(back_out, back_pen, back_fwd, start[:, 1:2]))
                        then(nc.vector.tensor_tensor(score, score, bwd, ALU.subtract))

                    @block.scalar
                    def _(act):
                        act.wait_ge(done, 16)
                        nc.scalar.activation(score, score, ACT.Exp).then_inc(exped, 1)

        def spread_exps():
            J = P // HEADS
            BLOCKS, REST = divmod(NG * TG, J)
            with ExitStack() as ctx:
                rows = sbuf(ctx, "spread_rows", [P, (BLOCKS + 1) * P])
                ps = [psum(ctx, f"spread_ps{s}", [P, 512]) for s in range(2)]
                zeroed = sem(ctx, "spread_zeroed")
                loaded = sem(ctx, "spread_loaded")
                turned = sem(ctx, "spread_turned")
                copied = sem(ctx, "spread_copied")

                with nc.Block() as block:

                    @block.sync
                    def _(sp):
                        for h in range(HEADS):
                            sp.dma_start(rows[h * J:(h + 1) * J, 0:BLOCKS * P].rearrange("j (b e) -> j b e", e=P),
                                         exps_T[h, 0:BLOCKS * J * P].rearrange("(b j e) -> j b e", j=J, e=P)).then_inc(loaded, 16)
                        sp.wait_ge(zeroed, 1)
                        for h in range(HEADS):
                            sp.dma_start(rows[h * J:h * J + REST, BLOCKS * P:],
                                         exps_T[h, BLOCKS * J * P:].rearrange("(j e) -> j e", e=P)).then_inc(loaded, 16)

                    @block.vector
                    def _(dve):
                        nc.vector.memset(rows[:, BLOCKS * P:], 0.0).then_inc(zeroed, 1)

                    @block.tensor
                    def _(pe):
                        pe.wait_ge(loaded, 2 * HEADS * 16)

                        for b in range(BLOCKS + 1):
                            at_least(pe, copied, b - 1)
                            nc.tensor.transpose(ps[b % 2][:, 0:P], rows[:, b * P:(b + 1) * P], ident[:, :]).then_inc(turned, 1)

                    @block.scalar
                    def _(act):
                        def step(b, s, r, tiles=J):
                            at_least(act, turned, b + 1)
                            nc.scalar.activation(exps[:, ds(b * J * HEADS, tiles * HEADS)].rearrange("p (j h) -> p h j", h=HEADS),
                                                 ps[s][:, 0:P].rearrange("p (h j) -> p h j", h=HEADS)[:, :, 0:tiles], ACT.Copy).then_inc(copied, 1)

                        steps(act, BLOCKS, 0, step)
                        step(BLOCKS, BLOCKS % 2, 0, REST)

        def gather_messages(tag, first):
            BW = 2 * HF + HEADS
            K = 3
            U = 4
            with ExitStack() as ctx:
                msg = [sbuf(ctx, f"{tag}sum_msg{s}", [P, TG, FEAT]) for s in range(U)]
                prod = [sbuf(ctx, f"{tag}sum_prod{s}", [P, TG, 2, BW]) for s in range(2)]
                hot = [sbuf(ctx, f"{tag}sum_hot{s}", [P, TG, SUM_WIN]) for s in range(2)]
                spare_ps = psum(ctx, f"{tag}sum_spare_ps", [P, 512])
                spare = sbuf(ctx, f"{tag}sum_spare", [1, 2])
                win_ps = [psum(ctx, f"{tag}sum_win_ps{s}", [P, 512]) for s in range(2)]
                zeroed = sem(ctx, f"{tag}sum_zeroed")
                placed = sem(ctx, f"{tag}sum_placed")
                msg_loaded = [sem(ctx, f"{tag}sum_msg_loaded{s}") for s in range(U)]
                made = sem(ctx, f"{tag}sum_made")
                summed = sem(ctx, f"{tag}sum_summed")
                added = sem(ctx, f"{tag}sum_added")

                with nc.Block() as block:

                    @block.sync
                    def _(sp):
                        def step(i, s, r):
                            at_least(sp, made, (i - 3) * K)
                            sp.dma_start(msg[s][:, :, :], messages[ds(i * GE, GE), :].rearrange("(t p) f -> p t f", p=P)
                                         ).then_inc(msg_loaded[s], 16)

                        steps(sp, NG, 0, step, unroll=U)

                    @block.gpsimd
                    def _(pool):
                        for b in range(2):
                            if first:
                                nc.gpsimd.memset(sums_T[:, b * COLS:(b + 1) * COLS], 0.0).then_inc(zeroed, 1)
                            else:
                                nc.gpsimd.memset(spare[:, b:b + 1], 0.0).then_inc(zeroed, 1)

                    @block.tensor
                    def _(pe):
                        pe.wait_ge(zeroed, 1)

                        def step(i, s, r):
                            if isinstance(i, int) and i == 4:
                                warm_up(spare_ps)
                            if live(i - 1, NG):
                                s1 = (s - 1) % 2
                                at_least(pe, made, i * K)
                                at_least(pe, added, i - 2)
                                for b in range(2):
                                    for t in range(TG):
                                        ins = nc.tensor.matmul(win_ps[s1][0:BW, b * SUM_WIN:(b + 1) * SUM_WIN], prod[s1][:, t, b, :],
                                                               hot[s1][:, t, :], start=t == 0, stop=t == TG - 1)
                                ins.then_inc(summed, 1)

                        steps(pe, NG, 1, step, warm=8, unroll=U)

                    @block.scalar
                    def _(act):
                        act.wait_ge(zeroed, 2)

                    @block.vector
                    def _(dve):
                        place_windows(dve, SUM_WIN, first, placed)
                        dve.wait_ge(zeroed, 2)

                        def products(i, s, r):
                            at_least(dve, made, i * K)
                            at_least(dve, summed, i - 1)
                            nc.vector.tensor_tensor(hot[s % 2][:, :, :], iota_win[:, :].unsqueeze(1).to_broadcast([P, TG, SUM_WIN]),
                                                    dst_rel[:, ds(i * TG, TG)].unsqueeze(2).to_broadcast([P, TG, SUM_WIN]),
                                                    ALU.is_equal).then_inc(made, 1)
                            at_least(dve, msg_loaded[s], 16 * (r + 1))
                            e = exps[:, ds(i * TG * HEADS, TG * HEADS)].rearrange("p (k h) -> p k h", h=2)
                            nc.vector.tensor_tensor(prod[s % 2][:, :, :, 0:2 * HF].rearrange("p t b (h f) -> p (t b) h f", h=2),
                                                    msg[s][:, :, :].rearrange("p t (b h f) -> p (t b) h f", b=2, h=2),
                                                    e.unsqueeze(3).to_broadcast([P, 2 * TG, 2, HF]), ALU.mult).then_inc(made, 1)
                            e = exps[:, ds(i * TG * HEADS, TG * HEADS)].rearrange("p (t h) -> p t h", h=HEADS)
                            nc.vector.tensor_copy(prod[s % 2][:, :, :, 2 * HF:BW], e.unsqueeze(2).to_broadcast([P, TG, 2, HEADS])).then_inc(made, 1)

                        def step(i, s, r):
                            if live(i, NG):
                                products(i, s, r)
                            if live(i - 2, NG):
                                add_window(dve, i - 2, win_ps[s % 2], BW, 2, SUM_WIN, summed, added)

                        steps(dve, NG, 2, step, warm=8, unroll=U)

        def post_l2():
            BW, HB = 2 * HF + HEADS, 2 * HF
            N_LOAD = 2 * 2 * (1 + XYZ)
            U = 4
            with ExitStack() as ctx:
                w_all = sbuf(ctx, "l2_post_w_all", [BW, 2, FEAT])
                w = sbuf(ctx, "l2_post_w", [BW, 2, 2 * FEAT + 2])
                row_i = sbuf(ctx, "l2_post_row_i", [BW, 1], I32)
                in_head = sbuf(ctx, "l2_post_in_head", [BW, 2])
                inv = [sbuf(ctx, f"l2_post_inv{s}", [P, 2, 2]) for s in range(U)]
                sums = [sbuf(ctx, f"l2_post_sums{s}", [BW, 2, P]) for s in range(U)]
                ps = [psum(ctx, f"l2_post_ps{s}", [P, 2, 512]) for s in range(U)]
                zeroed = sem(ctx, "l2_post_zeroed")
                rows_ready = sem(ctx, "l2_post_rows_ready")
                masks = sem(ctx, "l2_post_masks")
                w_loaded = sem(ctx, "l2_post_w_loaded")
                w_made = sem(ctx, "l2_post_w_made")
                copied = sem(ctx, "l2_post_copied")
                mapped = sem(ctx, "l2_post_mapped")
                ready = sem(ctx, "l2_post_ready")
                fin = sem(ctx, "l2_post_fin")

                with nc.Block() as block:

                    @block.sync
                    def _(sp):
                        sp.wait_ge(zeroed, 1)
                        for b in range(2):
                            for k in range(2):
                                h, at = 2 * b + k, k * HF
                                sp.dma_start(w_all[at:at + HS, b, 0:SC], A["L2_gnn_Wps"][h * HS:(h + 1) * HS, :]).then_inc(w_loaded, 16)
                                for c in range(XYZ):
                                    lo = at + HS + c * HV
                                    sp.dma_start(w_all[lo:lo + HV, b, SC + c * VC:SC + (c + 1) * VC],
                                                 A["L2_gnn_Wpv"][h * HV:(h + 1) * HV, :]).then_inc(w_loaded, 16)

                    @block.gpsimd
                    def _(pool):
                        nc.gpsimd.iota(row_i[:, :], pattern=[[1, 1]], base=0, channel_multiplier=1).then_inc(rows_ready, 1)

                    @block.scalar
                    def _(act):
                        def step(i, s, r):
                            at_least(act, mapped, i - 3)
                            nc.scalar.activation(sums[s][:, :, :], sums4[0:BW, 0:2, ds(i * P, P)], ACT.Copy).then_inc(copied, 1)

                        steps(act, NT, 0, step, unroll=U)

                    @block.tensor
                    def _(pe):
                        pe.wait_ge(w_made, 12)

                        def step(i, s, r):
                            at_least(pe, copied, i + 1)
                            at_least(pe, fin, (i - 3) * 4)
                            for b in range(2):
                                ins = nc.tensor.matmul(ps[s][:, b, 0:2 * FEAT + 2], sums[s][:, b, :], w[:, b, :])
                            ins.then_inc(mapped, 1)

                        steps(pe, NT, 0, step, unroll=U)

                    @block.vector
                    def _(dve):
                        nc.vector.memset(w_all[:, :, :], 0.0).then_inc(zeroed, 1)
                        dve.wait_ge(rows_ready, 1)
                        for k in range(2):
                            nc.vector.tensor_scalar(in_head[:, k:k + 1], row_i[:, :], k * HF - 0.5, None, ALU.is_gt).then_inc(masks, 1)
                            dve.wait_ge(masks, 2 * k + 1)
                            nc.vector.scalar_tensor_tensor(in_head[:, k:k + 1], row_i[:, :], (k + 1) * HF - 0.5, in_head[:, k:k + 1],
                                                           ALU.is_lt, ALU.mult).then_inc(masks, 1)
                        dve.wait_ge(masks, 4)
                        dve.wait_ge(w_loaded, 16 * N_LOAD)
                        for b in range(2):
                            for k in range(2):
                                at, mask = k * FEAT, in_head[:, k:k + 1]
                                nc.vector.tensor_scalar(w[:, b, at:at + SC], w_all[:, b, 0:SC], mask, None, ALU.mult).then_inc(w_made, 1)
                                nc.vector.tensor_scalar(w[:, b, at + SC:at + FEAT].rearrange("p (u c) -> p c u", c=XYZ),
                                                        by_component(w_all[:, b, SC:FEAT]), mask, None, ALU.mult).then_inc(w_made, 1)
                                nc.vector.tensor_scalar(w[:, b, 2 * FEAT + k:2 * FEAT + k + 1], row_i[:, :], float(HB + 2 * b + k), None,
                                                        ALU.is_equal).then_inc(w_made, 1)

                        def step(i, s, r):
                            at_least(dve, mapped, i + 1)
                            nc.vector.tensor_scalar(inv[s][:, :, :], ps[s][:, :, 2 * FEAT:2 * FEAT + 2], 1e-16, None, ALU.add).then_inc(ready, 1)
                            at_least(dve, ready, i * 2 + 1)
                            nc.vector.reciprocal(inv[s][:, :, :], inv[s][:, :, :]).then_inc(ready, 1)
                            at_least(dve, ready, i * 2 + 2)
                            row = x[:, ds(i * FEAT, FEAT)]
                            for b in range(2):
                                for k in range(2):
                                    at_least(dve, fin, i * 4 + 2 * b + k)
                                    nc.vector.scalar_tensor_tensor(row, ps[s][:, b, k * FEAT:(k + 1) * FEAT], inv[s][:, b, k:k + 1], row,
                                                                   ALU.mult, ALU.add).then_inc(fin, 1)

                        steps(dve, NT, 0, step, unroll=U)

        def layer_2():
            node_pass("l2", ["L2_gnn_Ws_src", "L2_gnn_Ws_dst"], ["L2_gnn_Wv_src", "L2_gnn_Wv_dst"], [table[2], table[3]], finish_l2, 4,
                      gamma=("L2_gnn_gamma_s", "L2_gnn_beta_s", "L2_gnn_gamma_v"))
            attention_pass()
            softmax_pass()
            spread_exps()
            all_windows(SUM_WIN, gather_messages)
            post_l2()

        def store_x():
            with ExitStack() as ctx:
                stored = sem(ctx, "result_stored")
                full = NODES // P
                with nc.Block() as block:

                    @block.sync
                    def _(sp):
                        sp.dma_start(out[0:full * P, :].rearrange("(t p) f -> p t f", p=P), x3[:, 0:full, :]).then_inc(stored, 16)
                        sp.dma_start(out[full * P:NODES, :], x3[0:NODES - full * P, full, :]).then_inc(stored, 16)
                        sp.wait_ge(stored, 32)

        import math
        c_self = math.sin(math.pi / 8)
        setup()
        node_pass("l0", ["L0_gnn_Wl1_0", "L0_gnn_Wsc0"], ["L0_gnn_Wl1_1", "L0_gnn_Wsc1"], [table[0]], finish_l0, 4,
                  [(0, SC ** -0.5), (0, VC ** -0.5)])
        all_windows(EDGE_WIN, lambda tag, first: edge_pass(
            tag + "l0", first, table[0], "edge_attr_8_T", "L0_gnn_Wfc1", "L0_gnn_Wfc2", "L0_gnn_Wfc3",
            ACT.Gelu_apprx_tanh, [8.0 ** -0.5, SC ** -0.5]))
        post_l0()
        node_pass("l1", ["L1_gnn_W1_s", "L1_gnn_W_sc_s"], ["L1_gnn_W1_v", "L1_gnn_W_sc_v"], [table[1], self_rows], finish_l1, 4,
                  [(0, SC ** -0.5), (0, VC ** -0.5)])
        all_windows(EDGE_WIN, lambda tag, first: edge_pass(
            tag + "l1", first, table[1], "edge_attr_8_T", "L1_gnn_fcW1", None, "L1_gnn_fcW2", ACT.Silu, [8.0 ** -0.5]))
        post_l1()
        layer_2()
        node_pass("l3", ["L3_gnn_Ws_l1_a", "L3_gnn_Ws_l1_c", "L3_gnn_Ws_sc_a", "L3_gnn_Ws_sc_c"],
                  ["L3_gnn_Wv_l1_a", "L3_gnn_Wv_l1_c", "L3_gnn_Wv_sc_a", "L3_gnn_Wv_sc_c"], [table[4]], finish_l3, 8,
                  [(0, 1.0), (1, 1.0), (0, c_self), (1, c_self)])
        all_windows(EDGE_WIN, lambda tag, first: edge_pass(
            tag + "l3", first, table[4], "edge_attr_10_T", "L3_gnn_W_fc1", None, "L3_gnn_W_fc2", ACT.Silu, [1.0]))
        post_l3()
        store_x()


def kernel(**inputs):
    import numpy as np
    import concourse.bacc as bacc
    from concourse import mybir
    from concourse.bass_utils import run_bass_kernel_spmd

    given = {n: np.asarray(v) for n, v in inputs.items()}

    def padded(a, rows, fill=0):
        return np.concatenate([a, np.full((rows - a.shape[0],) + a.shape[1:], fill, a.dtype)])

    def grouped(a):
        a = a.reshape((NG, TG, P) + a.shape[1:])
        a = np.moveaxis(a, 1, 2)
        return np.ascontiguousarray(a.reshape(NG * P, -1))

    src = padded(given.pop("src"), EPAD)
    dst = padded(given.pop("dst"), EPAD, NODES)
    y = padded(given.pop("edge_attr_4"), EPAD)
    arrays = {
        "x": padded(given.pop("x"), NPAD),
        "src_groups": grouped(src),
        "dst_groups": grouped(dst),
        "dst_tiles": dst.reshape(NG * TG, P).T,
        "dst_first": dst[::GE][None, :],
        "dst_last": dst[GE - 1::GE][None, :],
        "dst_line": np.concatenate([np.full(1, -1, np.int32), dst, np.full(1, NODES + 1, np.int32)])[None, :],
        "y_all": grouped(y[:, [0, 1, 2, 3, 1, 2]]).reshape(NG, P, TG * YC).transpose(1, 0, 2).reshape(P, -1),
        "y4": y.reshape(NG * TG, P, 4).transpose(1, 0, 2).reshape(P, -1),
    }
    for n, name in enumerate(["node_vec1", "node_vec1_n2", "node_vec1_n3"]):
        arrays[f"attr_{n}"] = padded(given.pop(name), NPAD).reshape(NT, P).T
    arrays["edge_attr_10_T"] = padded(given.pop("edge_attr_10"), EPAD).T
    a = padded(given.pop("edge_attr_16"), EPAD).reshape(NG, 2, 2 * P, 16).transpose(1, 3, 0, 2)
    arrays["edge_attr_16_T"] = np.concatenate([a, np.zeros_like(a)], axis=1).reshape(2 * QUARTER, -1)
    a = padded(given.pop("edge_attr_8"), EPAD)
    arrays["edge_attr_8_T"] = a.reshape(NG, TG // 2, 2, P, -1).transpose(2, 4, 0, 1, 3).reshape(2 * a.shape[1], -1)
    for name, a in given.items():
        arrays[name] = a[:, None] if a.ndim == 1 else a.reshape(-1, 1) if a.ndim == 3 else a
    for name in ["L3_gnn_Ws_l2_a", "L3_gnn_Ws_l2_c", "L3_gnn_Wv_l2_a", "L3_gnn_Wv_l2_c", "L2_gnn_Ws_val"]:
        arrays[f"{name}_T"] = given[name].T
    arrays = {f"in_{n}": np.ascontiguousarray(a) for n, a in arrays.items()}

    nc = bacc.Bacc("TRN2", target_bir_lowering=False, num_devices=1)
    A = {n[3:]: nc.dram_tensor(n, a.shape, mybir.dt.from_np(a.dtype), kind="ExternalInput").ap() for n, a in arrays.items()}
    out = nc.dram_tensor("out", (NODES, FEAT), mybir.dt.float32, kind="ExternalOutput").ap()
    build(nc, A, out)
    return run_bass_kernel_spmd(nc, [arrays], core_ids=[0]).results[0]["out"]
```
